# Optimizing a Trainium2 kernel written in Bass

```python
import numpy as np
import jax
import jax.numpy as jnp

def _softmax(x, axis=-1):
    return jax.nn.softmax(x, axis=axis)

def _gelu(x):
    return jax.nn.gelu(x, approximate=True)

def _silu(x):
    return jax.nn.silu(x)

def _sigmoid(x):
    return jax.nn.sigmoid(x)

def _layernorm(x, axis=-1, eps=1e-05):
    m = jnp.mean(x, axis=axis, keepdims=True)
    v = jnp.var(x, axis=axis, keepdims=True)
    return (x - m) / jnp.sqrt(v + eps)

def _scatter_add(tgt, idx, src, axis=0):
    return tgt.at[idx].add(src)

def _segment_sum(src, seg, n):
    return jax.ops.segment_sum(src, seg, n)
kernel_name = 'mk_decoder_postln_d2_seqx_r4_7a1782'

def setup_inputs(seed: int=0):
    np.random.seed(seed)
    _w = jnp.asarray

    def _rec_inputs():
        import jax
        import jax.numpy as jnp
        _rk = jax.random.key(seed)
        x = -0.0003929 + 0.9999 * jax.random.normal(jax.random.fold_in(_rk, 1), (32, 100, 256), jnp.float32)
        _lenS = 100 - jax.random.randint(jax.random.fold_in(_rk, 7), (32,), 0, max(1, 100 // 4) + 1, jnp.int32)
        _lenS2 = 361 - jax.random.randint(jax.random.fold_in(_rk, 8), (32,), 0, max(1, 361 // 4) + 1, jnp.int32)
        _ctx_1024P = jax.random.normal(jax.random.fold_in(_rk, 11), (32, 16, 256), jnp.float32)
        _ctx_1024c = jax.random.dirichlet(jax.random.fold_in(_rk, 511), 0.3 * jnp.ones((16,), jnp.float32), (32, 361))
        _ctx_1024t = jnp.einsum('bsk,bkd->bsd', _ctx_1024c, _ctx_1024P)
        _ctx_1024t = _ctx_1024t * jax.lax.rsqrt(jnp.mean(jnp.square(_ctx_1024t)) + 1e-12) * 0.953939
        ctx_1024 = 4.13588e-05 + 0.999923 * (_ctx_1024t + 0.3 * jax.random.normal(jax.random.fold_in(_rk, 611), (32, 361, 256), jnp.float32))
        return (x, ctx_1024)
    x, ctx_1024 = _rec_inputs()

    def _L0_attn_setup():
        import jax, jax.numpy as jnp
        import numpy as np
        D_MODEL = 256
        D_INNER = 512
        EPS = 1e-06

        def _phi(x):
            return jax.nn.elu(x) + 1.0
        key = jax.random.key(seed)
        ks = jax.random.split(key, 9)
        s_in = 1.0 / np.sqrt(D_MODEL)
        s_out = 1.0 / np.sqrt(D_INNER)
        x = jax.random.normal(ks[0], (4, 512, D_MODEL), dtype=jnp.float32)
        Wq = jax.random.uniform(ks[1], (D_MODEL, D_INNER), jnp.float32, -s_in, s_in)
        bq = jax.random.uniform(ks[2], (D_INNER,), jnp.float32, -s_in, s_in)
        Wk = jax.random.uniform(ks[3], (D_MODEL, D_INNER), jnp.float32, -s_in, s_in)
        bk = jax.random.uniform(ks[4], (D_INNER,), jnp.float32, -s_in, s_in)
        Wv = jax.random.uniform(ks[5], (D_MODEL, D_INNER), jnp.float32, -s_in, s_in)
        bv = jax.random.uniform(ks[6], (D_INNER,), jnp.float32, -s_in, s_in)
        Wo = jax.random.uniform(ks[7], (D_INNER, D_MODEL), jnp.float32, -s_out, s_out)
        bo = jax.random.uniform(ks[8], (D_MODEL,), jnp.float32, -s_out, s_out)
        return {'x': x, 'Wq': Wq, 'bq': bq, 'Wk': Wk, 'bk': bk, 'Wv': Wv, 'bv': bv, 'Wo': Wo, 'bo': bo}
    _L0_attn_all = _L0_attn_setup()
    _L0_attn_in = {k: v for k, v in _L0_attn_all.items() if k in ('Wq', 'bq', 'Wk', 'bk', 'Wv', 'bv', 'Wo', 'bo')}
    del _L0_attn_all

    def _L0_xattn_setup():
        import jax, jax.numpy as jnp
        import numpy as np
        H = 256
        B = 8
        L_CHAR = 512
        L_SUB = 256

        def _linear(x, W, b):
            return jnp.einsum('blh,oh->blo', x, W) + b

        def _interp_linear(x, out_len):
            L_in = x.shape[1]
            pos = (jnp.arange(out_len, dtype=x.dtype) + 0.5) * (L_in / out_len) - 0.5
            pos = jnp.clip(pos, 0.0, L_in - 1)
            lo = jnp.floor(pos).astype(jnp.int32)
            hi = jnp.minimum(lo + 1, L_in - 1)
            w = (pos - lo.astype(x.dtype))[None, :, None]
            return x[:, lo] * (1 - w) + x[:, hi] * w
        key = jax.random.key(seed)
        ks = jax.random.split(key, 18)
        s = 0.02
        inp = {'char_emb': jax.random.normal(ks[0], (B, L_CHAR, H), jnp.float32), 'subword_emb': jax.random.normal(ks[1], (B, L_SUB, H), jnp.float32)}
        names = ['Wq_c', 'Wk_s', 'Wv_s', 'Wq_s', 'Wk_c', 'Wv_c']
        for i, n in enumerate(names):
            inp[n] = jax.random.normal(ks[2 + 2 * i], (H, H), jnp.float32) * s
            inp['b' + n[1:]] = jax.random.normal(ks[3 + 2 * i], (H,), jnp.float32) * s
        inp['Wg'] = jax.random.normal(ks[14], (H, 2 * H), jnp.float32) * s
        inp['bg'] = jax.random.normal(ks[15], (H,), jnp.float32) * s
        return inp
    _L0_xattn_all = _L0_xattn_setup()
    _L0_xattn_in = {k: v for k, v in _L0_xattn_all.items() if k in ('Wq_c', 'bq_c', 'Wk_s', 'bk_s', 'Wv_s', 'bv_s', 'Wq_s', 'bq_s', 'Wk_c', 'bk_c', 'Wv_c', 'bv_c', 'Wg', 'bg')}
    del _L0_xattn_all

    def _L0_ffn_setup():
        import jax, jax.numpy as jnp
        import numpy as np
        D = 256
        H = 1024
        E = 64
        K = 3
        B, S = (2, 512)
        C = 128
        key = jax.random.key(seed)
        ks = jax.random.split(key, 6)
        s = 0.02
        return {'x': jax.random.normal(ks[0], (B, S, D), jnp.float32), 'gate_w': jax.random.normal(ks[1], (D, E), jnp.float32) * s, 'gate_b': jnp.zeros((E,), jnp.float32), 'w1': jax.random.normal(ks[2], (E, D, H), jnp.float32) * s, 'b1': jnp.zeros((E, H), jnp.float32), 'w2': jax.random.normal(ks[3], (E, H, D), jnp.float32) * s, 'b2': jnp.zeros((E, D), jnp.float32)}
    _L0_ffn_all = _L0_ffn_setup()
    _L0_ffn_in = {k: v for k, v in _L0_ffn_all.items() if k in ('gate_w', 'gate_b', 'w1', 'b1', 'w2', 'b2')}
    del _L0_ffn_all

    def _L1_attn_setup():
        import jax, jax.numpy as jnp
        import numpy as np
        import math
        D_MODEL = 256
        NUM_HEADS = 16
        key = jax.random.key(seed)
        k1, k2, k3 = jax.random.split(key, 3)
        B, S = (2, 512)
        x = jax.random.normal(k1, (B, S, D_MODEL), dtype=jnp.float32)
        W_kqv = jax.random.normal(k2, (D_MODEL, 3 * D_MODEL), dtype=jnp.float32) * (1.0 / math.sqrt(D_MODEL))
        m = jax.random.normal(k3, (NUM_HEADS, 1, 1), dtype=jnp.float32)
        return {'x': x, 'W_kqv': W_kqv, 'm': m}
    _L1_attn_all = _L1_attn_setup()
    _L1_attn_in = {k: v for k, v in _L1_attn_all.items() if k in ('W_kqv', 'm')}
    del _L1_attn_all

    def _L1_xattn_setup():
        import jax, jax.numpy as jnp
        import numpy as np
        D_MODEL = 256
        N_HEADS = 16
        HEAD_DIM = D_MODEL // N_HEADS
        MAX_REL = 32
        B, T, S = (2, 512, 512)

        def _rel_idx(length_q, length_k):
            dist = jnp.arange(length_k)[None, :] - jnp.arange(length_q)[:, None]
            return jnp.clip(dist, -MAX_REL, MAX_REL) + MAX_REL
        key = jax.random.key(seed)
        ks = jax.random.split(key, 13)
        sd = 1.0 / np.sqrt(D_MODEL)
        inp = {'query': jax.random.normal(ks[0], (B, T, D_MODEL), jnp.float32), 'key': jax.random.normal(ks[1], (B, S, D_MODEL), jnp.float32), 'value': jax.random.normal(ks[2], (B, S, D_MODEL), jnp.float32), 'Wq': jax.random.normal(ks[3], (D_MODEL, D_MODEL), jnp.float32) * sd, 'bq': jnp.zeros((D_MODEL,), jnp.float32), 'Wk': jax.random.normal(ks[4], (D_MODEL, D_MODEL), jnp.float32) * sd, 'bk': jnp.zeros((D_MODEL,), jnp.float32), 'Wv': jax.random.normal(ks[5], (D_MODEL, D_MODEL), jnp.float32) * sd, 'bv': jnp.zeros((D_MODEL,), jnp.float32), 'Wo': jax.random.normal(ks[6], (D_MODEL, D_MODEL), jnp.float32) * sd, 'bo': jnp.zeros((D_MODEL,), jnp.float32), 'rel_k_table': jax.random.normal(ks[7], (2 * MAX_REL + 1, HEAD_DIM), jnp.float32) * 0.05, 'rel_v_table': jax.random.normal(ks[8], (2 * MAX_REL + 1, HEAD_DIM), jnp.float32) * 0.05}
        return inp
    _L1_xattn_all = _L1_xattn_setup()
    _L1_xattn_in = {k: v for k, v in _L1_xattn_all.items() if k in ('Wq', 'bq', 'Wk', 'bk', 'Wv', 'bv', 'Wo', 'bo', 'rel_k_table', 'rel_v_table')}
    del _L1_xattn_all

    def _L1_ffn_setup():
        import jax, jax.numpy as jnp
        import numpy as np
        BLOCK = 32
        W_BITS = 4
        ACT_BITS = 16

        def act_qdq(x):
            qmax = 2.0 ** (ACT_BITS - 1) - 1.0
            scale = jnp.maximum(jnp.max(jnp.abs(x)) / qmax, 1e-12)
            return jnp.clip(jnp.round(x / scale), -qmax - 1.0, qmax) * scale

        def fixed_qdq_u16(x):
            scale = 1.0 / 65536.0
            return jnp.clip(jnp.round(x / scale), 0.0, 65535.0) * scale

        def lpbq_dequant(w):
            O, I = w.shape
            qmax = 2.0 ** (W_BITS - 1) - 1.0
            wb = w.reshape(O, I // BLOCK, BLOCK)
            s = jnp.maximum(jnp.max(jnp.abs(wb), axis=-1, keepdims=True) / qmax, 1e-12)
            wq = jnp.clip(jnp.round(wb / s), -qmax - 1.0, qmax) * s
            return wq.reshape(O, I)
        key = jax.random.key(seed)
        k1, k2, k3, k4 = jax.random.split(key, 4)
        B, S, H, I = (2, 1024, 256, 768)
        x = jax.random.normal(k1, (B, S, H), jnp.float32)
        w_gate = jax.random.normal(k2, (I, H), jnp.float32) * 0.02
        w_up = jax.random.normal(k3, (I, H), jnp.float32) * 0.02
        w_down = jax.random.normal(k4, (H, I), jnp.float32) * 0.02
        return {'x': x, 'w_gate': w_gate, 'w_up': w_up, 'w_down': w_down}
    _L1_ffn_all = _L1_ffn_setup()
    _L1_ffn_in = {k: v for k, v in _L1_ffn_all.items() if k in ('w_gate', 'w_up', 'w_down')}
    del _L1_ffn_all
    return {'x': x, 'ctx_1024': ctx_1024, 'L0_attn_Wq': _L0_attn_in['Wq'], 'L0_attn_bq': _L0_attn_in['bq'], 'L0_attn_Wk': _L0_attn_in['Wk'], 'L0_attn_bk': _L0_attn_in['bk'], 'L0_attn_Wv': _L0_attn_in['Wv'], 'L0_attn_bv': _L0_attn_in['bv'], 'L0_attn_Wo': _L0_attn_in['Wo'], 'L0_attn_bo': _L0_attn_in['bo'], 'L0_xattn_Wq_c': _L0_xattn_in['Wq_c'], 'L0_xattn_bq_c': _L0_xattn_in['bq_c'], 'L0_xattn_Wk_s': _L0_xattn_in['Wk_s'], 'L0_xattn_bk_s': _L0_xattn_in['bk_s'], 'L0_xattn_Wv_s': _L0_xattn_in['Wv_s'], 'L0_xattn_bv_s': _L0_xattn_in['bv_s'], 'L0_xattn_Wq_s': _L0_xattn_in['Wq_s'], 'L0_xattn_bq_s': _L0_xattn_in['bq_s'], 'L0_xattn_Wk_c': _L0_xattn_in['Wk_c'], 'L0_xattn_bk_c': _L0_xattn_in['bk_c'], 'L0_xattn_Wv_c': _L0_xattn_in['Wv_c'], 'L0_xattn_bv_c': _L0_xattn_in['bv_c'], 'L0_xattn_Wg': _L0_xattn_in['Wg'], 'L0_xattn_bg': _L0_xattn_in['bg'], 'L0_ffn_gate_w': _L0_ffn_in['gate_w'], 'L0_ffn_gate_b': _L0_ffn_in['gate_b'], 'L0_ffn_w1': _L0_ffn_in['w1'], 'L0_ffn_b1': _L0_ffn_in['b1'], 'L0_ffn_w2': _L0_ffn_in['w2'], 'L0_ffn_b2': _L0_ffn_in['b2'], 'L1_attn_W_kqv': _L1_attn_in['W_kqv'], 'L1_attn_m': _L1_attn_in['m'], 'L1_xattn_Wq': _L1_xattn_in['Wq'], 'L1_xattn_bq': _L1_xattn_in['bq'], 'L1_xattn_Wk': _L1_xattn_in['Wk'], 'L1_xattn_bk': _L1_xattn_in['bk'], 'L1_xattn_Wv': _L1_xattn_in['Wv'], 'L1_xattn_bv': _L1_xattn_in['bv'], 'L1_xattn_Wo': _L1_xattn_in['Wo'], 'L1_xattn_bo': _L1_xattn_in['bo'], 'L1_xattn_rel_k_table': _L1_xattn_in['rel_k_table'], 'L1_xattn_rel_v_table': _L1_xattn_in['rel_v_table'], 'L1_ffn_w_gate': _L1_ffn_in['w_gate'], 'L1_ffn_w_up': _L1_ffn_in['w_up'], 'L1_ffn_w_down': _L1_ffn_in['w_down']}

def reference(x, ctx_1024, L0_attn_Wq, L0_attn_bq, L0_attn_Wk, L0_attn_bk, L0_attn_Wv, L0_attn_bv, L0_attn_Wo, L0_attn_bo, L0_xattn_Wq_c, L0_xattn_bq_c, L0_xattn_Wk_s, L0_xattn_bk_s, L0_xattn_Wv_s, L0_xattn_bv_s, L0_xattn_Wq_s, L0_xattn_bq_s, L0_xattn_Wk_c, L0_xattn_bk_c, L0_xattn_Wv_c, L0_xattn_bv_c, L0_xattn_Wg, L0_xattn_bg, L0_ffn_gate_w, L0_ffn_gate_b, L0_ffn_w1, L0_ffn_b1, L0_ffn_w2, L0_ffn_b2, L1_attn_W_kqv, L1_attn_m, L1_xattn_Wq, L1_xattn_bq, L1_xattn_Wk, L1_xattn_bk, L1_xattn_Wv, L1_xattn_bv, L1_xattn_Wo, L1_xattn_bo, L1_xattn_rel_k_table, L1_xattn_rel_v_table, L1_ffn_w_gate, L1_ffn_w_up, L1_ffn_w_down):
    import jax
    import jax.numpy as jnp

    def _L0_attn_ref(x, Wq, bq, Wk, bk, Wv, bv, Wo, bo):
        import jax, jax.numpy as jnp
        import numpy as np
        D_MODEL = 256
        D_INNER = 512
        EPS = 1e-06

        def _phi(x):
            return jax.nn.elu(x) + 1.0
        Q = _phi(x @ Wq + bq)
        K = _phi(x @ Wk + bk)
        V = x @ Wv + bv
        n = x.shape[1]
        scores = jnp.einsum('bnd,bmd->bnm', Q, K)
        mask = jnp.tril(jnp.ones((n, n), dtype=scores.dtype))
        scores = scores * mask
        numerator = jnp.einsum('bnm,bme->bne', scores, V)
        denominator = scores.sum(axis=-1, keepdims=True) + EPS
        out = numerator / denominator
        return out @ Wo + bo

    def _L0_xattn_ref(char_emb, subword_emb, Wq_c, bq_c, Wk_s, bk_s, Wv_s, bv_s, Wq_s, bq_s, Wk_c, bk_c, Wv_c, bv_c, Wg, bg):
        import jax, jax.numpy as jnp
        import numpy as np
        H = 256
        B = 8
        L_CHAR = 512
        L_SUB = 256

        def _linear(x, W, b):
            return jnp.einsum('blh,oh->blo', x, W) + b

        def _interp_linear(x, out_len):
            L_in = x.shape[1]
            pos = (jnp.arange(out_len, dtype=x.dtype) + 0.5) * (L_in / out_len) - 0.5
            pos = jnp.clip(pos, 0.0, L_in - 1)
            lo = jnp.floor(pos).astype(jnp.int32)
            hi = jnp.minimum(lo + 1, L_in - 1)
            w = (pos - lo.astype(x.dtype))[None, :, None]
            return x[:, lo] * (1 - w) + x[:, hi] * w
        h = char_emb.shape[-1]
        scale = 1.0 / jnp.sqrt(jnp.asarray(h, char_emb.dtype))
        Q_char = _linear(char_emb, Wq_c, bq_c)
        K_sub = _linear(subword_emb, Wk_s, bk_s)
        V_sub = _linear(subword_emb, Wv_s, bv_s)
        scores = jnp.einsum('bqh,bkh->bqk', Q_char, K_sub) * scale
        char2sub = jnp.einsum('bqk,bkh->bqh', jax.nn.softmax(scores, axis=-1), V_sub)
        Q_sub = _linear(subword_emb, Wq_s, bq_s)
        K_char = _linear(char_emb, Wk_c, bk_c)
        V_char = _linear(char_emb, Wv_c, bv_c)
        scores2 = jnp.einsum('bqh,bkh->bqk', Q_sub, K_char) * scale
        sub2char = jnp.einsum('bqk,bkh->bqh', jax.nn.softmax(scores2, axis=-1), V_char)
        L_char = char_emb.shape[1]
        if sub2char.shape[1] != L_char:
            sub2char = _interp_linear(sub2char, L_char)
        gate_in = jnp.concatenate([char2sub, sub2char], axis=-1)
        gate = jax.nn.sigmoid(jnp.einsum('blh,oh->blo', gate_in, Wg) + bg)
        return gate * char2sub + (1 - gate) * sub2char

    def _L0_ffn_ref(x, gate_w, gate_b, w1, b1, w2, b2):
        import jax, jax.numpy as jnp
        import numpy as np
        D = 256
        H = 1024
        E = 64
        K = 3
        B, S = (2, 512)
        C = 128
        xf = x.reshape(-1, D)
        T = xf.shape[0]
        logits = xf @ gate_w + gate_b
        top_l, top_i = jax.lax.top_k(logits, K)
        gates = jax.nn.softmax(top_l, axis=-1)
        fe = top_i.reshape(-1)
        fg = gates.reshape(-1)
        tok = jnp.repeat(jnp.arange(T), K)
        oh = jax.nn.one_hot(fe, E, dtype=jnp.int32)
        pos = (jnp.cumsum(oh, axis=0) * oh).sum(-1) - 1
        valid = pos < C
        buf = jnp.zeros((E, C, D), x.dtype).at[fe, pos].set(xf[tok], mode='drop')
        h = jax.nn.gelu(jnp.einsum('ecd,edh->ech', buf, w1) + b1[:, None, :], approximate=False)
        y = jnp.einsum('ech,ehd->ecd', h, w2) + b2[:, None, :]
        rows = y[fe, jnp.minimum(pos, C - 1)] * (fg * valid.astype(x.dtype))[:, None]
        out = jnp.zeros_like(xf).at[tok].add(rows)
        return out.reshape(x.shape)

    def _L1_attn_ref(x, W_kqv, m):
        import jax, jax.numpy as jnp
        import numpy as np
        import math
        D_MODEL = 256
        NUM_HEADS = 16
        B, S, D = x.shape
        H = NUM_HEADS
        hd = D // H
        scale = math.sqrt(D)
        kqv = x @ W_kqv
        k, q, v = jnp.split(kqv, 3, axis=-1)
        q = q.reshape(B, S, H, hd)
        k = k.reshape(B, S, H, hd)
        v = v.reshape(B, S, H, hd)
        rel = (jnp.arange(S)[None, :] - jnp.arange(S)[:, None]).astype(x.dtype)
        bias = m[None, :, :, :] * rel[None, None, :, :]
        score = jnp.einsum('bqhd,bkhd->bhqk', q, k) / scale + bias
        causal = jnp.tril(jnp.ones((S, S), dtype=bool))
        score = jnp.where(causal[None, None, :, :], score, -jnp.inf)
        attn = jax.nn.softmax(score, axis=-1)
        out = jnp.einsum('bhqk,bkhd->bqhd', attn, v).reshape(B, S, D)
        return out

    def _L1_xattn_ref(query, key, value, Wq, bq, Wk, bk, Wv, bv, Wo, bo, rel_k_table, rel_v_table):
        import jax, jax.numpy as jnp
        import numpy as np
        D_MODEL = 256
        N_HEADS = 16
        HEAD_DIM = D_MODEL // N_HEADS
        MAX_REL = 32
        B, T, S = (2, 512, 512)

        def _rel_idx(length_q, length_k):
            dist = jnp.arange(length_k)[None, :] - jnp.arange(length_q)[:, None]
            return jnp.clip(dist, -MAX_REL, MAX_REL) + MAX_REL
        b, t, _ = query.shape
        s = key.shape[1]
        q = query @ Wq + bq
        k = key @ Wk + bk
        v = value @ Wv + bv
        rq = q.reshape(b, t, N_HEADS, HEAD_DIM).transpose(0, 2, 1, 3)
        rk = k.reshape(b, s, N_HEADS, HEAD_DIM).transpose(0, 2, 1, 3)
        rv = v.reshape(b, s, N_HEADS, HEAD_DIM).transpose(0, 2, 1, 3)
        attn1 = jnp.einsum('bhqd,bhkd->bhqk', rq, rk)
        rel_k = rel_k_table[_rel_idx(t, s)]
        attn2 = jnp.einsum('bhqd,qkd->bhqk', rq, rel_k)
        scale = jnp.sqrt(jnp.asarray(HEAD_DIM, q.dtype))
        attn = jax.nn.softmax((attn1 + attn2) / scale, axis=-1)
        w1 = jnp.einsum('bhqk,bhkd->bhqd', attn, rv)
        rel_v = rel_v_table[_rel_idx(t, s)]
        w2 = jnp.einsum('bhqk,qkd->bhqd', attn, rel_v)
        x = (w1 + w2).transpose(0, 2, 1, 3).reshape(b, t, D_MODEL)
        return x @ Wo + bo

    def _L1_ffn_ref(x, w_gate, w_up, w_down):
        import jax, jax.numpy as jnp
        import numpy as np
        BLOCK = 32
        W_BITS = 4
        ACT_BITS = 16

        def act_qdq(x):
            qmax = 2.0 ** (ACT_BITS - 1) - 1.0
            scale = jnp.maximum(jnp.max(jnp.abs(x)) / qmax, 1e-12)
            return jnp.clip(jnp.round(x / scale), -qmax - 1.0, qmax) * scale

        def fixed_qdq_u16(x):
            scale = 1.0 / 65536.0
            return jnp.clip(jnp.round(x / scale), 0.0, 65535.0) * scale

        def lpbq_dequant(w):
            O, I = w.shape
            qmax = 2.0 ** (W_BITS - 1) - 1.0
            wb = w.reshape(O, I // BLOCK, BLOCK)
            s = jnp.maximum(jnp.max(jnp.abs(wb), axis=-1, keepdims=True) / qmax, 1e-12)
            wq = jnp.clip(jnp.round(wb / s), -qmax - 1.0, qmax) * s
            return wq.reshape(O, I)
        x = act_qdq(x)
        up = act_qdq(x @ lpbq_dequant(w_up).T)
        gate = act_qdq(x @ lpbq_dequant(w_gate).T)
        sig = fixed_qdq_u16(jax.nn.sigmoid(gate))
        gate = act_qdq(gate * sig)
        o = act_qdq(gate * up)
        return o @ lpbq_dequant(w_down).T
    x = _layernorm(x + _L0_attn_ref(x, L0_attn_Wq, L0_attn_bq, L0_attn_Wk, L0_attn_bk, L0_attn_Wv, L0_attn_bv, L0_attn_Wo, L0_attn_bo), axis=-1)
    x = _layernorm(x + _L0_xattn_ref(x, ctx_1024, L0_xattn_Wq_c, L0_xattn_bq_c, L0_xattn_Wk_s, L0_xattn_bk_s, L0_xattn_Wv_s, L0_xattn_bv_s, L0_xattn_Wq_s, L0_xattn_bq_s, L0_xattn_Wk_c, L0_xattn_bk_c, L0_xattn_Wv_c, L0_xattn_bv_c, L0_xattn_Wg, L0_xattn_bg), axis=-1)
    x = _layernorm(x + _L0_ffn_ref(x, L0_ffn_gate_w, L0_ffn_gate_b, L0_ffn_w1, L0_ffn_b1, L0_ffn_w2, L0_ffn_b2), axis=-1)
    x = _layernorm(x + _L1_attn_ref(x, L1_attn_W_kqv, L1_attn_m), axis=-1)
    x = _layernorm(x + _L1_xattn_ref(x, ctx_1024, ctx_1024, L1_xattn_Wq, L1_xattn_bq, L1_xattn_Wk, L1_xattn_bk, L1_xattn_Wv, L1_xattn_bv, L1_xattn_Wo, L1_xattn_bo, L1_xattn_rel_k_table, L1_xattn_rel_v_table), axis=-1)
    x = _layernorm(x + _L1_ffn_ref(x, L1_ffn_w_gate, L1_ffn_w_up, L1_ffn_w_down), axis=-1)
    return x

_drawn_inputs = setup_inputs


def setup_inputs(seed=0):
    import zlib

    import numpy as np

    out = dict(_drawn_inputs(seed))
    spreads = {'L0_ffn_gate_b': (0.0, 0.1),
     'L0_ffn_b1': (0.0, 0.518),
     'L0_ffn_b2': (0.0, 0.1),
     'L1_xattn_bq': (0.0, 0.418),
     'L1_xattn_bk': (0.0, 2.0),
     'L1_xattn_bv': (0.0, 0.1),
     'L1_xattn_bo': (0.0, 0.1)}
    factors = {'L0_attn_Wq': 47.223,
     'L0_attn_bq': 64.0,
     'L0_attn_Wk': 39.746,
     'L0_attn_bk': 64.0,
     'L0_xattn_Wq_c': 8.0,
     'L0_xattn_bq_c': 8.0,
     'L0_xattn_Wk_s': 8.0,
     'L0_xattn_bk_s': 64.0,
     'L0_xattn_bv_s': 4.136,
     'L0_xattn_Wq_s': 8.0,
     'L0_xattn_bq_s': 8.0,
     'L0_xattn_Wk_c': 8.0,
     'L0_xattn_bk_c': 64.0,
     'L0_xattn_bv_c': 4.059,
     'L0_xattn_Wg': 8.0,
     'L0_xattn_bg': 22.831,
     'L1_xattn_rel_k_table': 8.0,
     'L1_xattn_rel_v_table': 2.715}
    for name, (base, spread) in spreads.items():
        noise = np.random.default_rng([zlib.crc32(name.encode()), seed]).standard_normal(out[name].shape)
        drawn = base * np.exp(spread * noise) if base else spread * noise
        out[name] = jnp.asarray(drawn.astype(out[name].dtype))
    for name, factor in factors.items():
        out[name] = (out[name] * factor).astype(out[name].dtype)
    return out
```

```python
from contextlib import ExitStack

import concourse.bass as bass
from concourse import mybir

F32 = mybir.dt.float32
U32 = mybir.dt.uint32
ALU = mybir.AluOpType
ACT = mybir.ActivationFunctionType
AX = mybir.AxisListType

P = 128
LN_EPS = 1e-5
ROUND = 12582912.0
TINY = 1e-12


class Names:

    def __init__(self, nc, ctx, stage):
        self.nc, self.ctx, self.stage, self.sems = nc, ctx, stage, []
        ctx.callback(self.clear)

    def clear(self):
        if self.sems:
            self.nc.clear_and_free_semaphores(self.sems)
            self.nc.all_engine_barrier()

    def sb(self, name, shape, dt=F32):
        return self.ctx.enter_context(self.nc.sbuf_tensor(f"{self.stage}_{name}", shape, dt))

    def ps(self, name, shape, dt=F32):
        return self.ctx.enter_context(self.nc.psum_tensor(f"{self.stage}_{name}", shape, dt))

    def sem(self, name):
        self.sems.append(self.nc.alloc_semaphore(name=f"{self.stage}_{name}"))
        return self.sems[-1]


class Chain:

    def __init__(self, eng, sem, per):
        self.eng, self.sem, self.per, self.n, self.turn = eng, sem, per, 0, 0

    def start(self, turn):
        self.turn, self.n = turn, 0

    def end(self):
        assert self.n == self.per, (self.n, self.per)

    def __call__(self, instruction):
        self.n += 1
        instruction.then_inc(self.sem, 1)
        self.eng.wait_ge(self.sem, self.turn * self.per + self.n)


def at(x, i):
    v = x[:, bass.ds(i, 1)]
    return v.rearrange("p a b -> p (a b)") if len(v.shape) == 3 else v.rearrange("p a b c -> p (a b) c")


class Turn:

    def __init__(self, i, parity, half):
        self.i, self.parity, self.half = i, parity, half

    def __add__(self, k):
        p = self.parity + k
        return Turn(self.i + k, p % 2, self.half + p // 2)

    def within(self, n):
        return not isinstance(self.i, int) or 0 <= self.i < n


def turns(eng, body, first, loop_from, loop_to, last):
    for i in range(first, loop_from):
        body(Turn(i, i % 2, i // 2))
    with eng.Fori(0, (loop_to - loop_from) // 2) as j:
        for k in range(2):
            i = loop_from + k
            body(Turn(2 * j + i, i % 2, j + i // 2))
    for i in range(loop_to, last):
        body(Turn(i, i % 2, i // 2))


def finish_norm(nc, m, block, keep, s_stats):
    stats, mean, rstd = keep["stats"], keep["mean"], keep["rstd"]
    S, B, _ = stats.shape
    half_sum = m.sb("norm_sum", [S, B])
    diff = m.sb("norm_diff", [S, B])
    spread = m.sb("norm_spread", [S, B])
    var = m.sb("norm_var", [S, B])
    eps = m.sb("norm_eps", [S, 1])
    s_step = m.sem("norm_steps")
    s_log = m.sem("norm_logs")

    @block.vector
    def _(dve):
        step = Chain(dve, s_step, 6)
        step.start(0)
        dve.wait_ge(s_stats, B)
        nc.vector.memset(eps[:], LN_EPS)
        nc.vector.tensor_tensor(half_sum[:], stats[:, :, 1], stats[:, :, 4], ALU.add)
        nc.vector.tensor_tensor(diff[:], stats[:, :, 1], stats[:, :, 4], ALU.subtract)
        step(nc.vector.tensor_tensor(spread[:], stats[:, :, 2], stats[:, :, 5], ALU.add))
        step(nc.vector.tensor_tensor(diff[:], diff[:], diff[:], ALU.mult))
        step(nc.vector.tensor_scalar(mean[:], half_sum[:], 0.5, None, ALU.mult))
        step(nc.vector.tensor_scalar(diff[:], diff[:], 0.25, None, ALU.mult))
        step(nc.vector.scalar_tensor_tensor(out=var[:], in0=spread[:], scalar=1.0 / keep["y"].shape[2],
                                            in1=diff[:], op0=ALU.mult, op1=ALU.add))
        dve.wait_ge(s_log, 1)
        step(nc.vector.tensor_scalar(var[:], rstd[:], -0.5, None, ALU.mult))

    @block.scalar
    def _(act):
        act.wait_ge(s_step, 5)
        nc.scalar.activation(rstd[:], var[:], ACT.Ln, bias=eps[:]).then_inc(s_log, 1)
        act.wait_ge(s_step, 6)
        nc.scalar.activation(rstd[:], var[:], ACT.Exp).then_inc(s_log, 1)


def linear_attention(nc, io, keep):
    B, S, D = io["x"].shape
    E = io["L0_attn_Wq"].shape[1]
    KC, EC = D // P, E // P
    G = 4
    TURNS = B // G
    N = G * S
    y_nat = keep["y"]
    with ExitStack() as ctx:
        m = Names(nc, ctx, "lin")
        w_q = m.sb("w_q", [P, KC, E])
        w_k = m.sb("w_k", [P, KC, E])
        w_vT = m.sb("w_vT", [P, EC, D])
        w_o = m.sb("w_o", [P, EC, D])
        w_vo = m.sb("w_vo", [P, KC, D])
        bias_cols = m.sb("bias_cols", [P, 3, EC])
        bias_up = m.sb("bias_up", [P, 2, EC])
        bv_wide = m.sb("bv_wide", [P, EC, S])
        b_vo = m.sb("b_vo", [S, D])
        b_o = m.sb("b_o", [S, D])
        causal = m.sb("causal", [S, G, S])
        xT = m.sb("xT", [P, 2, KC, N])
        phi = m.sb("phi", [P, 2, 2, EC, N])
        low = m.sb("low", [P, 2, N])
        expd = m.sb("expd", [P, 2, N])
        values = m.sb("values", [S, G, D + 1])
        scores = m.sb("scores", [S, G, S])
        resid = m.sb("resid", [S, 2, G, D])
        den = m.sb("den", [S, G])
        rden = m.sb("rden", [S, G])
        ps_qk = m.ps("ps_qk", [P, 4, 512])
        ps_v = m.ps("ps_v", [P, 1, 512])
        ps_s = m.ps("ps_s", [P, 512])
        ps_o = m.ps("ps_o", [P, 2, 512])

        s_w = m.sem("weights")
        s_x = m.sem("x_whole")
        s_const = m.sem("constants")
        s_wide = m.sem("bv_widened")
        s_wvo = m.sem("wvo_product")
        s_wvo_sb = m.sem("wvo_stored")
        s_xT = [m.sem(f"xT{u}_loaded") for u in range(2)]
        s_proj = m.sem("qk_projected")
        s_low = m.sem("qk_low")
        s_exp = m.sem("qk_exp")
        s_phi = m.sem("qk_phi")
        s_val = m.sem("values_projected")
        s_val_sb = m.sem("values_stored")
        s_sc = m.sem("scores_ready")
        s_sc_sb = m.sem("scores_masked")
        s_out = m.sem("rows_summed")
        s_y = m.sem("rows_divided")
        s_res = m.sem("residual_ready")
        s_res_free = m.sem("residual_free")
        s_chain = m.sem("dve_chain")
        s_stats = m.sem("stats_ready")
        block = ctx.enter_context(nc.Block())

        @block.sync
        def _(sp):
            sp.dma_start(w_q[:], io["L0_attn_Wq"].rearrange("(c p) e -> p c e", p=P)).then_inc(s_w, 16)
            sp.dma_start(w_k[:], io["L0_attn_Wk"].rearrange("(c p) e -> p c e", p=P)).then_inc(s_w, 16)
            sp.dma_start(w_vT[:], io["L0_attn_WvT"].rearrange("(c p) d -> p c d", p=P)).then_inc(s_w, 16)
            sp.dma_start(w_o[:], io["L0_attn_Wo"].rearrange("(c p) d -> p c d", p=P)).then_inc(s_w, 16)
            sp.dma_start(b_o[:], io["L0_attn_bo"].partition_broadcast(S)).then_inc(s_w, 16)
            for n, name in enumerate(("L0_attn_bq", "L0_attn_bk", "L0_attn_bv")):
                sp.dma_start(bias_cols[:, n, :], io[name + "_cols"]).then_inc(s_w, 16)
            sp.dma_start(y_nat[:], io["x"].rearrange("b s d -> s b d")).then_inc(s_x, 16)
            with sp.Fori(0, TURNS // 2) as j:
                for u in range(2):
                    sp.wait_ge(s_val, 2 * (2 * j + u) + 2)
                    sp.dma_start(xT[:, u], io["xT"].rearrange("(c p) n -> p c n", p=P)[
                        :, :, bass.ds((2 * j + u) * N, N)]).then_inc(s_xT[u], 16)

        @block.gpsimd
        def _(pool):
            nc.gpsimd.memset(causal[:], 1.0).then_inc(s_const, 1)
            nc.gpsimd.memset(values[:, :, D:D + 1], 1.0).then_inc(s_const, 1)
            pool.wait_ge(s_const, 2)
            nc.gpsimd.affine_select(out=causal[:], in_=causal[:], pattern=[[0, G], [1, S]], compare_op=ALU.is_ge,
                                    fill=0.0, base=0, channel_multiplier=-1).then_inc(s_const, 1)
            pool.wait_ge(s_w, 8 * 16)
            pool.wait_ge(s_x, 16)
            with pool.Fori(0, TURNS // 2) as j:
                for u in range(2):
                    pool.wait_ge(s_res_free, 2 * j + u + 1)
                    rows = y_nat[:, bass.ds((2 * j + u) * G, G), :]
                    nc.gpsimd.tensor_tensor(resid[:, u], rows, b_o[:].unsqueeze(1).to_broadcast([S, G, D]),
                                            ALU.add).then_inc(s_res, 1)

        @block.scalar
        def _(act):
            act.wait_ge(s_const, 3)
            with act.Fori(0, TURNS // 2) as j:
                for u in range(2):
                    t = 2 * j + u
                    for n in range(2 * EC):
                        act.wait_ge(s_low, t * 2 * EC + (n + 1))
                        nc.scalar.activation(expd[:, n % 2, :], low[:, n % 2, :], ACT.Exp).then_inc(s_exp, 1)

        @block.tensor
        def _(pe):
            pe.wait_ge(s_w, 8 * 16)
            pe.wait_ge(s_wide, 1)
            for c in range(KC):
                for e in range(EC):
                    nc.tensor.matmul(ps_v[:, 0, c * D:(c + 1) * D], w_vT[:, e, c * P:(c + 1) * P], w_o[:, e, :],
                                     start=(e == 0), stop=(e == EC - 1))
            for e in range(EC):
                last = nc.tensor.matmul(ps_o[0:S, 0, 0:D], bv_wide[:, e, :], w_o[:, e, :],
                                        start=(e == 0), stop=(e == EC - 1))
            last.then_inc(s_wvo, 1)
            pe.wait_ge(s_wvo_sb, 1)
            pe.sem_inc(s_val, 4)
            with pe.Fori(0, TURNS // 2) as j:
                for u in range(2):
                    t = 2 * j + u
                    pe.wait_ge(s_xT[u], j * 16 + 16)
                    for n in range(2 * EC):
                        w, e = (w_q, w_k)[n // EC], n % EC
                        pe.wait_ge(s_phi, t * 2 * EC + (n + 1))
                        for c in range(KC):
                            last = nc.tensor.matmul(ps_qk[:, n % 4, 0:N],
                                                    w[:, c, e * P:(e + 1) * P], xT[:, u, c, :],
                                                    start=(c == 0), stop=(c == KC - 1))
                        last.then_inc(s_proj, 1)
                    for h in range(2):
                        if h:
                            pe.wait_ge(s_val_sb, 2 * t + 1)
                        for i in range(2):
                            q = 2 * h + i
                            for c in range(KC):
                                last = nc.tensor.matmul(ps_v[0:S, 0, i * D:(i + 1) * D],
                                                        xT[:, u, c, q * S:(q + 1) * S], w_vo[:, c, :],
                                                        start=(c == 0), stop=(c == KC - 1))
                        last.then_inc(s_val, 1)
                    pe.wait_ge(s_phi, t * 2 * EC + (2 * EC + 4))
                    for q in range(G):
                        for e in range(EC):
                            last = nc.tensor.matmul(ps_s[0:S, q * S:(q + 1) * S],
                                                    phi[:, u, 1, e, q * S:(q + 1) * S],
                                                    phi[:, u, 0, e, q * S:(q + 1) * S],
                                                    start=(e == 0), stop=(e == EC - 1))
                    last.then_inc(s_sc, 1)
                    pe.wait_ge(s_sc_sb, t + 1)
                    pe.wait_ge(s_val_sb, 2 * t + 2)
                    for q in range(G):
                        pe.wait_ge(s_y, t * G + (q + 1))
                        nc.tensor.matmul(ps_o[0:S, q % 2, 0:D + 1], scores[:, q, :], values[:, q, :],
                                         start=True, stop=True).then_inc(s_out, 1)

        @block.vector
        def _(dve):
            chain = Chain(dve, s_chain, 2 * G)
            dve.wait_ge(s_w, 8 * 16)
            nc.vector.tensor_scalar(bias_up[:], bias_cols[:, 0:2, :], 1.0, None, ALU.add)
            nc.vector.tensor_copy(bv_wide[:], bias_cols[:, 2, :].unsqueeze(2).to_broadcast([P, EC, S])).then_inc(s_wide, 1)
            dve.wait_ge(s_wvo, 1)
            nc.vector.tensor_copy(w_vo[:], ps_v[:, 0, :].rearrange("p (c d) -> p c d", c=KC))
            nc.vector.tensor_copy(b_vo[:], ps_o[0:S, 0, 0:D]).then_inc(s_wvo_sb, 1)
            dve.wait_ge(s_wvo_sb, 1)
            dve.wait_ge(s_const, 3)
            dve.sem_inc(s_phi, 4)
            dve.sem_inc(s_y, 2)
            dve.sem_inc(s_res_free, 2)
            with dve.Fori(0, TURNS // 2) as j:
                for u in range(2):
                    t = 2 * j + u
                    chain.start(t)

                    def lower(n):
                        dve.wait_ge(s_proj, t * 2 * EC + (n + 1))
                        nc.vector.tensor_scalar(low[:, n % 2, :], ps_qk[:, n % 4, 0:N],
                                                bias_cols[:, n // EC, n % EC:n % EC + 1], 0.0,
                                                ALU.add, ALU.min).then_inc(s_low, 1)

                    def upper(n):
                        dve.wait_ge(s_exp, t * 2 * EC + (n + 1))
                        nc.vector.scalar_tensor_tensor(
                            out=phi[:, u, n // EC, n % EC, :], in0=ps_qk[:, n % 4, 0:N],
                            scalar=bias_up[:, n // EC, n % EC:n % EC + 1], in1=expd[:, n % 2, :],
                            op0=ALU.add, op1=ALU.max).then_inc(s_phi, 1)

                    lower(0)
                    for n in range(1, 2 * EC):
                        lower(n)
                        upper(n - 1)
                    upper(2 * EC - 1)
                    for h in range(2):
                        dve.wait_ge(s_val, 2 * t + (h + 5))
                        nc.vector.tensor_tensor(
                            values[:, 2 * h:2 * h + 2, 0:D], ps_v[0:S, 0, :].rearrange("p (q d) -> p q d", q=2),
                            b_vo[:].unsqueeze(1).to_broadcast([S, 2, D]), ALU.add).then_inc(s_val_sb, 1)
                    dve.wait_ge(s_sc, t + 1)
                    nc.vector.tensor_tensor(scores[:], ps_s[0:S, 0:N].rearrange("p (q s) -> p q s", q=G),
                                            causal[:], ALU.mult).then_inc(s_sc_sb, 1)
                    dve.wait_ge(s_res, t + 1)
                    for q in range(G):
                        b = t * G + q
                        dve.wait_ge(s_out, b + 1)
                        chain(nc.vector.tensor_scalar(den[:, q:q + 1], ps_o[0:S, q % 2, D:D + 1], 1e-6, None, ALU.add))
                        chain(nc.vector.reciprocal(rden[:, q:q + 1], den[:, q:q + 1]))
                        nc.vector.scalar_tensor_tensor(out=at(y_nat, b), in0=ps_o[0:S, q % 2, 0:D],
                                                       scalar=rden[:, q:q + 1], in1=resid[:, u, q, :],
                                                       op0=ALU.mult, op1=ALU.add).then_inc(s_y, 1)
                    for q in range(G):
                        dve.wait_ge(s_y, t * G + (q + 3))
                        nc.vector.bn_stats(at(keep["stats"], t * G + q), at(y_nat, t * G + q)).then_inc(s_stats, 1)
                    dve.wait_ge(s_y, t * G + (G + 2))
                    dve.sem_inc(s_res_free, 1)
                    chain.end()
        finish_norm(nc, m, block, keep, s_stats)


def mutual_attention(nc, io, keep):
    B, S, D = io["x"].shape
    L = io["ctx_1024"].shape[1]
    KC = D // P
    CH = 3
    STEP = L // CH
    R = L - (CH - 1) * STEP
    SCALE = float(D) ** -0.5
    y_nat, mean, rstd = keep["y"], keep["mean"], keep["rstd"]
    with ExitStack() as ctx:
        m = Names(nc, ctx, "mut")
        w = {n: m.sb(n, [P, KC, D]) for n in ("Wq_c", "Wk_s", "Wk_c", "Wq_s", "WvT_s", "WvT_c")}
        w_gT = m.sb("WgT", [P, 2 * KC, D])
        cols = {n: m.sb(n + "_col", [P, KC]) for n in ("bq_c", "bk_s", "bk_c", "bq_s", "bv_s", "bv_c", "bg")}
        interp = m.sb("interp", [R, CH, S])
        ident = m.sb("ident", [P, P])
        sel_c = m.sb("sel_c", [2, L])
        sel_r = m.sb("sel_r", [2, R])
        a_w = m.sb("a_w", [P, 2, KC, D])
        a_b = m.sb("a_b", [P, 2, KC])
        row_w = m.sb("row_w", [P, KC, 2])
        prod = m.sb("prod", [P, KC, 2])
        ones = m.sb("ones", [P, 2])
        row_b = m.sb("row_b", [2, 1])
        bv = m.sb("bv", [P, 2 * KC])
        neg_bg = m.sb("neg_bg", [P, KC])
        ctx_nat = m.sb("ctx_nat", [R, 2, CH, D])
        ctx_T = m.sb("ctx_T", [P, 2, KC, L])
        xn = m.sb("xn", [S, 2, D])
        xT = m.sb("xT", [P, KC, S])
        u = m.sb("u", [P, 2, KC, S])
        rows = m.sb("rows", [2, S])
        mx1 = m.sb("mx1", [S, 1])
        nmx1 = m.sb("nmx1", [S, 1])
        sum1 = m.sb("sum1", [S, 1])
        rec1 = m.sb("rec1", [S, 1])
        p1 = m.sb("p1", [S, L])
        p1n = m.sb("p1n", [S, L])
        p1T = m.sb("p1T", [R, CH, S])
        mx2 = m.sb("mx2", [R, CH])
        nmx2 = m.sb("nmx2", [R, CH])
        sum2 = m.sb("sum2", [R, CH])
        rec2 = m.sb("rec2", [R, CH])
        p2 = m.sb("p2", [R, CH, S])
        p2n = m.sb("p2n", [R, CH, S])
        tT = m.sb("tT", [S, S])
        yT = m.sb("yT", [P, KC, S])
        zT = m.sb("zT", [P, KC, S])
        cs = m.sb("cs", [P, 2 * KC, S])
        gate_e = m.sb("gate_e", [P, KC, S])
        gate = m.sb("gate", [P, KC, S])
        diff = m.sb("diff", [P, KC, S])
        mix = m.sb("mix", [P, KC, S])
        mixed = m.sb("mixed", [P, KC, S])
        ps_yy = m.ps("ps_yy", [P, 512])
        ps_p = m.ps("ps_p", [P, 512])
        ps_tz = m.ps("ps_tz", [P, 512])
        ps_u = m.ps("ps_u", [P, 512])
        ps_s1 = m.ps("ps_s1", [P, 512])
        ps_s2 = m.ps("ps_s2", [P, 512])
        ps_cs = m.ps("ps_cs", [P, 512])
        ps_g = m.ps("ps_g", [P, 512])
        ps_xT = ps_yy[:, 0:KC * S].rearrange("p (c s) -> p c s", c=KC)
        ps_y = ps_yy[:, 0:KC * S].rearrange("p (c s) -> p c s", c=KC)
        ps_p1T = ps_p[0:R, 0:CH * S].rearrange("p (c s) -> p c s", c=CH)
        ps_rows = ps_s2[0:2, 384:384 + S]
        ps_t = ps_tz[0:S, 0:S]
        ps_z = ps_tz[:, 256:256 + KC * S].rearrange("p (c s) -> p c s", c=KC)
        ps_uv = ps_u[:, 0:2 * KC * S].rearrange("p (n c s) -> p n c s", n=2, c=KC)
        ps_sub = ps_s2[0:R, 0:CH * S].rearrange("p (c s) -> p c s", c=CH)
        ps_csv = ps_cs[:, 0:2 * KC * S].rearrange("p (c s) -> p c s", c=2 * KC)
        ps_gate = ps_g[:, 0:KC * S].rearrange("p (c s) -> p c s", c=KC)
        ps_out = ps_yy[0:S, 0:D]

        s_w = m.sem("weights")
        s_const = m.sem("constants")
        s_mul = m.sem("weights_multiplied")
        s_mul_sb = m.sem("products_stored")
        s_prod = m.sem("bias_products")
        s_ctx = [m.sem(f"context{v}_loaded") for v in range(2)]
        s_xn = m.sem("rows_normalised")
        s_xn_kept = m.sem("rows_normalised_in_place")
        s_xT = m.sem("xT_transposed")
        s_xT_sb = m.sem("xT_stored")
        s_u = m.sem("u_projected")
        s_u_sb = m.sem("u_stored")
        s_rows = m.sem("row_terms")
        s_rows_sb = m.sem("row_terms_stored")
        s_s1 = m.sem("scores1")
        s_mx1 = m.sem("max1")
        s_e1 = m.sem("exp1")
        s_r1 = m.sem("sum1_inverted")
        s_p1n = m.sem("weights1")
        s_p1T = m.sem("weights1_transposed")
        s_p1T_sb = m.sem("weights1T_stored")
        s_s2 = m.sem("scores2")
        s_mx2 = m.sem("max2")
        s_e2 = m.sem("exp2")
        s_r2 = m.sem("sum2_inverted")
        s_p2n = m.sem("weights2")
        s_t = m.sem("t_ready")
        s_t_sb = m.sem("t_stored")
        s_y = m.sem("y_ready")
        s_y_sb = m.sem("y_stored")
        s_z = m.sem("z_ready")
        s_z_sb = m.sem("z_stored")
        s_cs = m.sem("cs_ready")
        s_cs_sb = m.sem("cs_stored")
        s_g = m.sem("gate_logits")
        s_ge = m.sem("gate_exp")
        s_gd = m.sem("gate_denominator")
        s_gate = m.sem("gate_ready")
        s_diff = m.sem("difference")
        s_mix = m.sem("mix_scaled")
        s_mixed = m.sem("mixed")
        s_out = m.sem("out_transposed")
        s_sum = m.sem("rows_added")
        s_stats = m.sem("stats_ready")
        s_took = m.sem("waits_taken")
        block = ctx.enter_context(nc.Block())
        NW = len(w) + 1 + len(cols) + 1

        @block.sync
        def _(sp):
            for n, tile in w.items():
                sp.dma_start(tile[:], io["L0_xattn_" + n].rearrange("(c p) d -> p c d", p=P)).then_inc(s_w, 16)
            sp.dma_start(w_gT[:], io["L0_xattn_WgT"].rearrange("(c p) d -> p c d", p=P)).then_inc(s_w, 16)
            for n, tile in cols.items():
                sp.dma_start(tile[:], io[f"L0_xattn_{n}_cols"]).then_inc(s_w, 16)
            sp.dma_start(interp[:], io["interp"]).then_inc(s_w, 16)

            def load(t):
                v = t.parity
                nat = io["ctx_1024"]
                sp.wait_ge(s_y, t.i + 1)
                sp.wait_ge(s_s2, t.i + 1)
                sp.dma_start(ctx_nat[:, v], bass.AP(nat.tensor, nat[bass.ds(t.i, 1)].offset,
                                                    [[D, R], [STEP * D, CH], [1, D]])).then_inc(s_ctx[v], 16)
                sp.dma_start(ctx_T[:, v], io["ctxT"].rearrange("b (c p) l -> p b c l", p=P)[
                    :, bass.ds(t.i, 1)].rearrange("p b c l -> p (b c) l")).then_inc(s_ctx[v], 16)

            turns(sp, load, 0, 0, B, B)

        @block.gpsimd
        def _(pool):
            nc.gpsimd.memset(ident[:], 1.0).then_inc(s_const, 1)
            nc.gpsimd.memset(sel_c[:], 1.0).then_inc(s_const, 1)
            nc.gpsimd.memset(sel_r[:], 1.0).then_inc(s_const, 1)
            nc.gpsimd.memset(ones[:], 1.0).then_inc(s_const, 1)
            pool.wait_ge(s_const, 4)
            nc.gpsimd.affine_select(out=ident[:], in_=ident[:], pattern=[[1, P]], compare_op=ALU.is_equal,
                                    fill=0.0, base=0, channel_multiplier=-1).then_inc(s_const, 1)
            nc.gpsimd.affine_select(out=sel_c[:], in_=sel_c[:], pattern=[[0, L]], compare_op=ALU.is_equal,
                                    fill=0.0, base=0, channel_multiplier=1).then_inc(s_const, 1)
            nc.gpsimd.affine_select(out=sel_r[:], in_=sel_r[:], pattern=[[0, R]], compare_op=ALU.is_equal,
                                    fill=0.0, base=-1, channel_multiplier=1).then_inc(s_const, 1)

            pool.sem_inc(s_mixed, 1)

            def turn(b):
                pool.wait_ge(s_cs_sb, b.i + 1)
                nc.gpsimd.tensor_tensor(diff[:], cs[:, 0:KC, :], cs[:, KC:2 * KC, :], ALU.subtract).then_inc(s_diff, 1)
                pool.wait_ge(s_gate, b.i + 1)
                pool.wait_ge(s_diff, b.i + 1)
                nc.gpsimd.tensor_tensor(mix[:], gate[:], diff[:], ALU.mult).then_inc(s_mix, 1)
                pool.wait_ge(s_mix, b.i + 1)
                pool.wait_ge(s_out, b.i + 1)
                nc.gpsimd.tensor_tensor(mixed[:], mix[:], cs[:, KC:2 * KC, :], ALU.add).then_inc(s_mixed, 1)

            turns(pool, turn, 0, 0, B, B)

        @block.scalar
        def _(act):
            def copied(sem, ready, n, out, in_):
                act.wait_ge(ready, n)
                nc.scalar.copy(out, in_).then_inc(sem, 1)

            def turn(t):
                b, nxt = t, t + 1
                if nxt.within(B):
                    copied(s_xT_sb, s_xT, nxt.i + 1, xT[:], ps_xT)
                if b.within(B):
                    copied(s_p1T_sb, s_p1T, b.i + 2, p1T[:], ps_p1T)
                    copied(s_t_sb, s_t, b.i + 2, tT[:], ps_t)
                    copied(s_y_sb, s_y, b.i + 3, yT[:], ps_y)
                    copied(s_z_sb, s_z, b.i + 1, zT[:], ps_z)
                if nxt.within(B):
                    act.wait_ge(s_mx1, 2 * nxt.i + 2)
                    act.wait_ge(s_p1n, nxt.i + 1)
                    nc.scalar.activation(p1[:], ps_s1[0:S, 0:L], ACT.Exp, bias=nmx1[:], scale=SCALE,
                                         accum_out=sum1[:]).then_inc(s_e1, 1)
                    act.wait_ge(s_mx2, 2 * nxt.i + 2)
                    act.wait_ge(s_p2n, nxt.i + 1)
                    for c in range(CH):
                        last = nc.scalar.activation(p2[:, c, :], ps_sub[:, c, :], ACT.Exp, bias=nmx2[:, c:c + 1],
                                                    scale=SCALE, accum_out=sum2[:, c:c + 1])
                    last.then_inc(s_e2, 1)
                if b.within(B):
                    act.wait_ge(s_g, b.i + 1)
                    for c in range(KC):
                        last = nc.scalar.activation(gate_e[:, c, :], ps_gate[:, c, :], ACT.Exp,
                                                    bias=neg_bg[:, c:c + 1], scale=-1.0)
                    last.then_inc(s_ge, 1)

            act.wait_ge(s_mul_sb, 1)
            turns(act, turn, -1, 1, B - 1, B)

        @block.vector
        def _(dve):
            dve.wait_ge(s_w, 16 * NW)
            for c, (x, y) in enumerate((("bq_c", "bk_s"), ("bk_c", "bq_s"))):
                nc.vector.tensor_tensor(prod[:, :, c], cols[x][:], cols[y][:], ALU.mult)
            nc.vector.tensor_copy(bv[:, 0:KC], cols["bv_s"][:])
            nc.vector.tensor_copy(bv[:, KC:2 * KC], cols["bv_c"][:])
            nc.vector.tensor_scalar(neg_bg[:], cols["bg"][:], -1.0, None, ALU.mult).then_inc(s_prod, 1)
            dve.wait_ge(s_mul, 1)
            for n, bank in ((0, ps_s1), (1, ps_s2)):
                nc.vector.tensor_copy(a_w[:, n], bank[:, 0:KC * D].rearrange("p (c d) -> p c d", c=KC))
            nc.vector.tensor_copy(a_b[:], ps_u[:, 0:2 * KC].rearrange("p (n c) -> p n c", n=2))
            nc.vector.tensor_copy(row_w[:], ps_u[:, 64:64 + 2 * KC].rearrange("p (c n) -> p c n", n=2))
            nc.vector.tensor_copy(row_b[:], ps_u[0:2, 128:129]).then_inc(s_mul_sb, 1)
            dve.wait_ge(s_mul_sb, 1)

            dve.sem_inc(s_p1n, 1)
            dve.sem_inc(s_p2n, 1)

            def turn(t):
                prev, b, nxt = t + -1, t, t + 1
                if nxt.within(B):
                    for n, out in enumerate((xn[:, nxt.parity, :], at(y_nat, nxt.i))):
                        last = nc.vector.tensor_scalar(out, at(y_nat, nxt.i), mean[:, bass.ds(nxt.i, 1)],
                                                       rstd[:, bass.ds(nxt.i, 1)], ALU.subtract, ALU.mult)
                        last.then_inc((s_xn, s_xn_kept)[n], 1)
                if prev.within(B):
                    dve.wait_ge(s_ge, prev.i + 1)
                    nc.vector.tensor_scalar(gate_e[:], gate_e[:], 1.0, None, ALU.add).then_inc(s_gd, 1)
                    dve.wait_ge(s_gd, prev.i + 1)
                    nc.vector.reciprocal(gate[:], gate_e[:]).then_inc(s_gate, 1)
                if nxt.within(B):
                    dve.wait_ge(s_u, nxt.i + 1)
                    nc.vector.tensor_tensor(u[:], ps_uv, a_b[:].unsqueeze(3).to_broadcast([P, 2, KC, S]),
                                            ALU.add).then_inc(s_u_sb, 1)
                    dve.wait_ge(s_rows, nxt.i + 1)
                    nc.vector.tensor_scalar(rows[:], ps_rows, row_b[:], None, ALU.add).then_inc(s_rows_sb, 1)
                    dve.wait_ge(s_s1, nxt.i + 1)
                    nc.vector.reduce_max(mx1[:], ps_s1[0:S, 0:L], AX.X).then_inc(s_mx1, 1)
                    dve.wait_ge(s_mx1, 2 * nxt.i + 1)
                    nc.vector.tensor_scalar(nmx1[:], mx1[:], -SCALE, None, ALU.mult).then_inc(s_mx1, 1)
                    dve.wait_ge(s_s2, nxt.i + 3)
                    nc.vector.reduce_max(mx2[:], ps_sub, AX.X).then_inc(s_mx2, 1)
                    dve.wait_ge(s_mx2, 2 * nxt.i + 1)
                    nc.vector.tensor_scalar(nmx2[:], mx2[:], -SCALE, None, ALU.mult).then_inc(s_mx2, 1)
                    dve.wait_ge(s_e1, nxt.i + 1)
                    nc.vector.reciprocal(rec1[:], sum1[:]).then_inc(s_r1, 1)
                    dve.wait_ge(s_r1, nxt.i + 1)
                    dve.wait_ge(s_p1T, nxt.i + 1)
                    nc.vector.tensor_scalar(p1n[:], p1[:], rec1[:], None, ALU.mult).then_inc(s_p1n, 1)
                if b.within(B):
                    dve.wait_ge(s_cs, b.i + 1)
                    dve.wait_ge(s_mixed, b.i + 1)
                    nc.vector.tensor_tensor(cs[:], ps_csv, bv[:].unsqueeze(2).to_broadcast([P, 2 * KC, S]),
                                            ALU.add).then_inc(s_cs_sb, 1)
                if nxt.within(B):
                    dve.wait_ge(s_e2, nxt.i + 1)
                    nc.vector.reciprocal(rec2[:], sum2[:]).then_inc(s_r2, 1)
                    dve.wait_ge(s_r2, nxt.i + 1)
                    dve.wait_ge(s_t, nxt.i + 1)
                    nc.vector.tensor_tensor(p2n[:], p2[:], rec2[:].unsqueeze(2).to_broadcast([R, CH, S]),
                                            ALU.mult).then_inc(s_p2n, 1)
                if prev.within(B):
                    dve.wait_ge(s_out, prev.i + 2)
                    dve.wait_ge(s_xn_kept, prev.i + 1)
                    nc.vector.tensor_tensor(at(y_nat, prev.i), ps_out, at(y_nat, prev.i), ALU.add).then_inc(s_sum, 1)
                    dve.wait_ge(s_sum, prev.i + 1)
                    nc.vector.bn_stats(at(keep["stats"], prev.i), at(y_nat, prev.i)).then_inc(s_stats, 1)

            turns(dve, turn, -1, 1, B - 1, B + 1)

        @block.tensor
        def _(pe):
            def mm(out, lhsT, rhs, k, n, start=None, stop=None):
                return nc.tensor.matmul(out, lhsT, rhs, start=(k == 0) if start is None else start,
                                        stop=(k == n - 1) if stop is None else stop)

            pe.wait_ge(s_w, 16 * NW)
            pe.wait_ge(s_const, 7)
            pe.wait_ge(s_prod, 1)
            for n, (x, y, bank, bx) in enumerate((("Wq_c", "Wk_s", ps_s1, "bq_c"), ("Wk_c", "Wq_s", ps_s2, "bk_c"))):
                for c in range(KC):
                    for o in range(KC):
                        mm(bank[:, c * D:(c + 1) * D], w[x][:, o, c * P:(c + 1) * P], w[y][:, o, :], o, KC)
                for c in range(KC):
                    for o in range(KC):
                        mm(ps_u[:, n * KC + c:n * KC + c + 1], w[y][:, o, c * P:(c + 1) * P], cols[bx][:, o:o + 1], o, KC)
            for n, (x, bx) in enumerate((("Wq_c", "bk_s"), ("Wk_c", "bq_s"))):
                for c in range(KC):
                    for o in range(KC):
                        mm(ps_u[:, 64 + 2 * c + n:65 + 2 * c + n], w[x][:, o, c * P:(c + 1) * P], cols[bx][:, o:o + 1], o, KC)
            for o in range(KC):
                last = mm(ps_u[0:2, 128:129], prod[:, o, :], ones[:, 0:1], o, KC)
            last.then_inc(s_mul, 1)
            pe.wait_ge(s_mul_sb, 1)
            pe.sem_inc(s_y, 2)
            pe.sem_inc(s_s2, 2)
            pe.sem_inc(s_p1T, 1)
            pe.sem_inc(s_t, 1)
            pe.sem_inc(s_out, 1)

            def turn(t):
                prev, b, nxt = t + -1, t, t + 1
                v, vn = b.parity, nxt.parity
                if nxt.within(B):
                    pe.wait_ge(s_xn, nxt.i + 1)
                    if not isinstance(nxt.i, int) or nxt.i > 2:
                        pe.wait_ge(s_sum, nxt.i - 2)
                    for c in range(KC):
                        last = nc.tensor.transpose(ps_xT[:, c, :], xn[:, vn, c * P:(c + 1) * P], ident[0:S, 0:S])
                    last.then_inc(s_xT, 1)
                if b.within(B):
                    pe.wait_ge(s_p1n, b.i + 2)
                    for c in range(CH):
                        last = nc.tensor.transpose(ps_p1T[:, c, :], p1n[:, c * STEP:c * STEP + R], ident[0:S, 0:S])
                    last.then_inc(s_p1T, 1)
                    pe.wait_ge(s_p2n, b.i + 2)
                    for c in range(CH):
                        last = mm(ps_t, p2n[:, c, :], interp[:, c, :], c, CH)
                    last.then_inc(s_t, 1)
                if nxt.within(B):
                    pe.wait_ge(s_xT_sb, nxt.i + 1)
                    for n in range(2):
                        for c in range(KC):
                            for k in range(KC):
                                last = mm(ps_uv[:, n, c, :], a_w[:, n, k, c * P:(c + 1) * P], xT[:, k, :], k, KC)
                    last.then_inc(s_u, 1)
                if b.within(B):
                    if not isinstance(b.i, int) or b.i > 1:
                        pe.wait_ge(s_sum, b.i - 1)
                    pe.wait_ge(s_p1T_sb, b.i + 1)
                    for c in range(KC):
                        for k in range(CH):
                            r = R if k == CH - 1 else STEP
                            last = mm(ps_y[:, c, :], ctx_nat[0:r, v, k, c * P:(c + 1) * P], p1T[0:r, k, :], k, CH)
                    last.then_inc(s_y, 1)
                    pe.wait_ge(s_t_sb, b.i + 1)
                    for c in range(KC):
                        last = mm(ps_z[:, c, :], xn[:, v, c * P:(c + 1) * P], tT[:], 0, 1)
                    last.then_inc(s_z, 1)
                if nxt.within(B):
                    for k in range(KC):
                        last = mm(ps_rows, row_w[:, k, :], xT[:, k, :], k, KC)
                    last.then_inc(s_rows, 1)
                    pe.wait_ge(s_u_sb, nxt.i + 1)
                    pe.wait_ge(s_ctx[vn], 32 * nxt.half + 32)
                    for k in range(KC):
                        mm(ps_s1[0:S, 0:L], u[:, 0, k, :], ctx_T[:, vn, k, :], k, KC, stop=False)
                    pe.wait_ge(s_rows_sb, nxt.i + 1)
                    mm(ps_s1[0:S, 0:L], rows[:], sel_c[:], 1, 2).then_inc(s_s1, 1)
                    for c in range(CH):
                        for k in range(KC):
                            mm(ps_sub[:, c, :], ctx_T[:, vn, k, c * STEP:c * STEP + R], u[:, 1, k, :], k, KC, stop=False)
                        last = mm(ps_sub[:, c, :], sel_r[:], rows[:], 1, 2)
                    last.then_inc(s_s2, 1)
                if b.within(B):
                    pe.wait_ge(s_y_sb, b.i + 1)
                    pe.wait_ge(s_z_sb, b.i + 1)
                    for n, (wn, src) in enumerate((("WvT_s", yT), ("WvT_c", zT))):
                        for c in range(KC):
                            for k in range(KC):
                                last = mm(ps_csv[:, n * KC + c, :], w[wn][:, k, c * P:(c + 1) * P], src[:, k, :], k, KC)
                    last.then_inc(s_cs, 1)
                if prev.within(B):
                    pe.wait_ge(s_mixed, prev.i + 2)
                    for c in range(KC):
                        last = nc.tensor.transpose(ps_out[:, c * P:(c + 1) * P], mixed[:, c, :], ident[:])
                    last.then_inc(s_out, 1)
                if b.within(B):
                    pe.wait_ge(s_cs_sb, b.i + 1)
                    for c in range(KC):
                        for k in range(2 * KC):
                            last = mm(ps_gate[:, c, :], w_gT[:, k, c * P:(c + 1) * P], cs[:, k, :], k, 2 * KC)
                    last.then_inc(s_g, 1)

            turns(pe, turn, -1, 1, B - 1, B + 1)

        finish_norm(nc, m, block, keep, s_stats)


def routed_ffn(nc, io, keep):
    B, S, D = io["x"].shape
    E, _, H = io["L0_ffn_w1"].shape
    KC, HC = D // P, H // P
    TOP, CAP = 3, P
    G = 4
    GROUPS = B // G
    FAR = 1 << 17
    y_nat, mean, rstd = keep["y"], keep["mean"], keep["rstd"]
    x_rows = nc.dram_tensor("moe_x_rows", (B * S, D), F32, kind="Internal").ap()
    table = nc.dram_tensor("moe_table", (CAP * E, 1), U32, kind="Internal").ap()
    y_rows = nc.dram_tensor("moe_y_rows", (E * CAP, D), F32, kind="Internal").ap()
    with ExitStack() as ctx:
        m = Names(nc, ctx, "moe")
        ident = m.sb("ident", [P, P])
        before = m.sb("before", [S, S])
        ones = m.sb("ones", [P, P])
        iota_i = m.sb("iota_i", [S, E], mybir.dt.int32)
        iota_e = m.sb("iota_e", [S, E])
        row_i = m.sb("row_i", [S, G], mybir.dt.int32)
        row_f = m.sb("row_f", [S, G])
        zero_u = m.sb("zero_u", [P, CAP * E // P], U32)
        gate_w = m.sb("gate_w", [P, KC, E])
        gate_b = m.sb("gate_b", [S, E])
        xg = m.sb("xg", [S, G, D])
        xgT = m.sb("xgT", [P, G, KC, S])
        lg = m.sb("lg", [S, G, E])
        top_v = m.sb("top_v", [S, 2, G, 8])
        top_i = m.sb("top_i", [S, G, 8], U32)
        top_f = m.sb("top_f", [S, 2, G, TOP])
        hot = m.sb("hot", [S, 2, G, TOP, E])
        hot01 = m.sb("hot01", [S, G, E])
        mask = m.sb("mask", [S, 2, G, E])
        mask_sum = m.sb("mask_sum", [S, E])
        earlier = m.sb("earlier", [S, E])
        hot_pos = m.sb("hot_pos", [S, G, TOP, E])
        pos = m.sb("pos", [S, G, TOP])
        capped = m.sb("capped", [S, G, TOP])
        full = m.sb("full", [S, G, TOP])
        taken = m.sb("taken", [S, G, TOP])
        slot = m.sb("slot", [S, G, TOP])
        slot_u = m.sb("slot_u", [S, 2, G, TOP], U32)
        row_u = m.sb("row_u", [S, 2, G], U32)
        logit = m.sb("logit", [S, G, TOP])
        expd = m.sb("expd", [S, G, TOP])
        sums = m.sb("sums", [S, G])
        recs = m.sb("recs", [S, G])
        share = m.sb("share", [S, G, TOP])
        gates = m.sb("gates", [S, B, TOP])
        y_row = m.sb("y_row", [S, B, TOP], U32)
        places = m.sb("places", [P, E], U32)
        place = m.sb("place", [P, 2], U32)
        b1 = m.sb("b1", [P, E, HC])
        b2 = m.sb("b2", [1, 2, D])
        w1 = m.sb("w1", [P, 2, KC, H])
        w2 = m.sb("w2", [P, 2, HC, D])
        xe = m.sb("xe", [P, 2, D])
        xeT = m.sb("xeT", [P, 2, KC, CAP])
        hT = m.sb("hT", [P, HC, CAP])
        ye = m.sb("ye", [P, 2, D])
        near = m.sb("near", [S, 2, TOP], U32)
        got = m.sb("got", [S, 2, TOP, D])
        acc = m.sb("acc", [S, 2, D])
        ps_T = m.ps("ps_T", [P, 2, 512])
        ps_lg = m.ps("ps_lg", [P, 512])
        ps_pos = m.ps("ps_pos", [P, 512])
        ps_h = m.ps("ps_h", [P, 2, 512])
        ps_y = m.ps("ps_y", [P, 2, 512])
        ps_xT = [ps_T[:, v, 0:2 * KC * S].rearrange("p (g c s) -> p g c s", g=2, c=KC) for v in range(2)]
        ps_logit = ps_lg[0:S, 0:G * E].rearrange("p (g e) -> p g e", g=G)
        ps_place = ps_pos[0:S, 0:G * E].rearrange("p (g e) -> p g e", g=G)

        sem = m.sem
        s_w, s_const, s_zero, s_zero_out = sem("weights"), sem("constants"), sem("zeros"), sem("table_zeroed")
        s_xg, s_xg_out, s_xg_kept = sem("rows_normalised"), sem("rows_stored"), sem("rows_kept")
        s_T, s_T_sb, s_lgp, s_lg = sem("rows_transposed"), sem("rowsT_stored"), sem("logits_summed"), sem("logits")
        s_topv, s_top, s_topf, s_hot = sem("top_values"), sem("top_numbers"), sem("top_floats"), sem("one_hot")
        s_hot01, s_mask, s_msum = sem("one_hot_pair"), sem("mask"), sem("mask_summed")
        s_earlier, s_place, s_back = sem("earlier_counts"), sem("places_counted"), sem("back_chain")
        s_logit, s_exp, s_slots = sem("top_logits"), sem("top_exp"), sem("slots")
        s_scat = [sem(f"numbers_scattered{v}") for v in range(2)]
        s_places, s_col = sem("places_loaded"), sem("place_column")
        s_w1 = [sem(f"w1_{v}_loaded") for v in range(2)]
        s_w2 = [sem(f"w2_{v}_loaded") for v in range(2)]
        s_xe = [sem(f"expert_rows{v}") for v in range(2)]
        s_xeT, s_xeT_sb, s_h, s_gelu = sem("expert_rowsT"), sem("expert_rowsT_stored"), sem("hidden"), sem("gelu")
        s_ye, s_ye_sb = sem("expert_out"), sem("expert_out_stored")
        s_yout = [sem(f"expert_out{v}_in_dram") for v in range(2)]
        s_hot_pos = sem("places_by_rank")
        s_near = sem("near_column")
        s_got = [sem(f"results_gathered{v}") for v in range(2)]
        s_acc, s_sum, s_stats, s_took = sem("acc_chain"), sem("rows_added"), sem("stats_ready"), sem("waits_taken")
        block = ctx.enter_context(nc.Block())

        @block.sync
        def _(sp):
            sp.dma_start(gate_w[:], io["L0_ffn_gate_w"].rearrange("(c p) e -> p c e", p=P)).then_inc(s_w, 16)
            sp.dma_start(gate_b[:], io["L0_ffn_gate_b"].partition_broadcast(S)).then_inc(s_w, 16)
            sp.dma_start(b1[:], io["L0_ffn_b1_cols"]).then_inc(s_w, 16)
            sp.wait_ge(s_zero, 1)
            sp.dma_start(table.rearrange("(p c) o -> p (c o)", p=P), zero_u[:]).then_inc(s_zero_out, 16)

            def weights(t):
                v = t.parity
                sp.wait_ge(s_h, 2 * t.i + 2)
                sp.dma_start(w1[:, v], io["L0_ffn_w1"][bass.ds(t.i, 1)].rearrange(
                    "o (c p) h -> p (o c) h", p=P)).then_inc(s_w1[v], 16)
                sp.wait_ge(s_ye, t.i + 1)
                sp.dma_start(w2[:, v], io["L0_ffn_w2"][bass.ds(t.i, 1)].rearrange(
                    "o (c p) d -> p (o c) d", p=P)).then_inc(s_w2[v], 16)
                sp.dma_start(b2[:, v], io["L0_ffn_b2"][bass.ds(t.i, 1)]).then_inc(s_w2[v], 16)

            for e in range(2):
                weights(Turn(e, e, 0))
            for g in range(GROUPS):
                sp.wait_ge(s_xg, g + 1)
                sp.dma_start(x_rows[g * G * S:(g + 1) * G * S].rearrange("(g s) d -> s g d", g=G),
                             xg[:]).then_inc(s_xg_out, 16)
                sp.wait_ge(s_xg_out, 16 * (g + 1))
            for v in range(2):
                sp.wait_ge(s_scat[v], 16 * G * TOP * GROUPS // 2)
            sp.dma_start(places[:], table.rearrange("(p e) o -> p (e o)", p=P)).then_inc(s_places, 16)
            def store(t):
                v = t.parity
                sp.wait_ge(s_ye_sb, t.i + 3)
                sp.dma_start(y_rows[bass.ds(t.i * CAP, CAP)], ye[:, v, :]).then_inc(s_yout[v], 16)

            def turn(t):
                weights(t)
                store(t + -2)

            turns(sp, turn, 2, 2, E, E)
            for e in range(E - 2, E):
                store(Turn(e, e % 2, e // 2))

        @block.gpsimd
        def _(pool):
            nc.gpsimd.memset(zero_u[:], 0).then_inc(s_zero, 1)
            nc.gpsimd.memset(ident[:], 1.0).then_inc(s_const, 1)
            nc.gpsimd.memset(before[:], 1.0).then_inc(s_const, 1)
            nc.gpsimd.memset(ones[:], 1.0).then_inc(s_const, 1)
            nc.gpsimd.memset(earlier[:], 0.0).then_inc(s_const, 1)
            nc.gpsimd.iota(iota_i[:], pattern=[[1, E]], base=0, channel_multiplier=0).then_inc(s_const, 1)
            nc.gpsimd.iota(row_i[:], pattern=[[S, G]], base=0, channel_multiplier=1).then_inc(s_const, 1)
            pool.wait_ge(s_const, 6)
            nc.gpsimd.tensor_copy(iota_e[:], iota_i[:]).then_inc(s_const, 1)
            nc.gpsimd.tensor_copy(row_f[:], row_i[:]).then_inc(s_const, 1)
            nc.gpsimd.affine_select(out=ident[:], in_=ident[:], pattern=[[1, P]], compare_op=ALU.is_equal,
                                    fill=0.0, base=0, channel_multiplier=-1).then_inc(s_const, 1)
            nc.gpsimd.affine_select(out=before[:], in_=before[:], pattern=[[1, S]], compare_op=ALU.is_gt,
                                    fill=0.0, base=0, channel_multiplier=-1).then_inc(s_const, 1)
            pool.wait_ge(s_zero_out, 16)
            pool.sem_inc(s_xg_kept, 1)
            pool.sem_inc(s_earlier, 1)

            def route(t):
                g, nxt = t, t + 1
                if g.within(GROUPS):
                    v = g.parity
                    pool.wait_ge(s_msum, g.i + 1)
                    pool.wait_ge(s_place, g.i + 1)
                    nc.gpsimd.tensor_tensor(earlier[:], earlier[:], mask_sum[:], ALU.add).then_inc(s_earlier, 1)
                if nxt.within(GROUPS):
                    pool.wait_ge(s_xg, nxt.i + 1)
                    pool.sem_inc(s_took, 1)
                    nc.gpsimd.tensor_copy(y_nat[:, bass.ds(nxt.i * G, G), :], xg[:]).then_inc(s_xg_kept, 1)
                if g.within(GROUPS):
                    pool.wait_ge(s_slots, g.i + 1)
                    pool.sem_inc(s_took, 1)
                    for q in range(G):
                        for k in range(TOP):
                            nc.gpsimd.indirect_dma_start(
                                out=table[:], out_offset=bass.IndirectOffsetOnAxis(ap=slot_u[:, v, q, k:k + 1], axis=0),
                                in_=row_u[:, v, q:q + 1], in_offset=None, bounds_check=CAP * E - 1,
                                oob_is_err=False).then_inc(s_scat[v], 16)

            turns(pool, route, -1, 1, GROUPS - 1, GROUPS)

            pool.wait_ge(s_places, 16)
            pool.wait_ge(s_xg_out, 16 * GROUPS)

            def gather(t):
                v = t.parity
                pool.wait_ge(s_xeT, t.i + 1)
                pool.sem_inc(s_took, 1)
                nc.gpsimd.tensor_copy(place[:, v:v + 1], places[:, bass.ds(t.i, 1)]).then_inc(s_col, 1)
                pool.wait_ge(s_col, t.i + 1)
                pool.sem_inc(s_took, 1)
                nc.gpsimd.indirect_dma_start(
                    out=xe[:, v, :], out_offset=None, in_=x_rows[:],
                    in_offset=bass.IndirectOffsetOnAxis(ap=place[:, v:v + 1], axis=0)).then_inc(s_xe[v], 16)

            turns(pool, gather, 0, 0, E, E)
            for v in range(2):
                pool.wait_ge(s_yout[v], 16 * (E // 2))

            def collect(t):
                v = t.parity
                pool.wait_ge(s_sum, t.i + 1)
                pool.sem_inc(s_took, 1)
                nc.gpsimd.tensor_copy(near[:, v, :], at(y_row, t.i)).then_inc(s_near, 1)
                pool.wait_ge(s_near, t.i + 1)
                pool.sem_inc(s_took, 1)
                for k in range(TOP):
                    nc.gpsimd.indirect_dma_start(
                        out=got[:, v, k, :], out_offset=None, in_=y_rows[:],
                        in_offset=bass.IndirectOffsetOnAxis(ap=near[:, v, k:k + 1], axis=0)).then_inc(s_got[v], 16)

            turns(pool, collect, 0, 0, B, B)

        @block.scalar
        def _(act):
            def route(t):
                g, nxt = t, t + 1
                if nxt.within(GROUPS):
                    for h in range(2):
                        act.wait_ge(s_T, 2 * nxt.i + (h + 1))
                        nc.scalar.copy(xgT[:, 2 * h:2 * h + 2], ps_xT[h]).then_inc(s_T_sb, 1)
                if g.within(GROUPS):
                    act.wait_ge(s_logit, g.i + 1)
                    nc.scalar.activation(expd[:], logit[:], ACT.Exp).then_inc(s_exp, 1)

            turns(act, route, -1, 1, GROUPS - 1, GROUPS)

            def expert(t):
                v = t.parity
                act.wait_ge(s_xeT, t.i + 3)
                nc.scalar.copy(xeT[:, v], ps_T[:, v, 0:KC * CAP].rearrange("p (c n) -> p c n", c=KC)).then_inc(s_xeT_sb, 1)
                for h in range(2):
                    act.wait_ge(s_h, 2 * t.i + (h + 5))
                    act.wait_ge(s_ye, t.i + 2)
                    for c in range(HC // 2):
                        k = h * HC // 2 + c
                        last = nc.scalar.activation(hT[:, k, :], ps_h[:, h, c * CAP:(c + 1) * CAP], ACT.Gelu,
                                                    bias=at(b1, t.i)[:, k:k + 1])
                    last.then_inc(s_gelu, 1)

            turns(act, expert, 0, 0, E, E)

        @block.tensor
        def _(pe):
            def mm(out, lhsT, rhs, k, n):
                return nc.tensor.matmul(out, lhsT, rhs, start=(k == 0), stop=(k == n - 1))

            pe.wait_ge(s_w, 16 * 3)
            pe.wait_ge(s_const, 10)
            pe.sem_inc(s_h, 4)
            pe.sem_inc(s_ye, 2)
            pe.sem_inc(s_xeT, 2)

            def route(t):
                g, nxt = t, t + 1
                if g.within(GROUPS):
                    v = g.parity
                    pe.wait_ge(s_mask, g.i + 1)
                    pe.wait_ge(s_earlier, g.i + 1)
                    pe.wait_ge(s_hot_pos, g.i + 1)
                    for q in range(G):
                        mm(ps_place[:, q, :], before[:], mask[:, v, q, :], 0, 2)
                        for q2 in range(q):
                            mm(ps_place[:, q, :], ones[0:S, 0:S], mask[:, v, q2, :], 1, 3)
                        last = mm(ps_place[:, q, :], ones[0:S, 0:S], earlier[:], 1, 2)
                    last.then_inc(s_place, 1)
                if nxt.within(GROUPS):
                    pe.wait_ge(s_xg, nxt.i + 1)
                    for h in range(2):
                        for q in range(2):
                            for c in range(KC):
                                last = nc.tensor.transpose(ps_xT[h][:, q, c, :], xg[:, 2 * h + q, c * P:(c + 1) * P],
                                                           ident[0:S, 0:S])
                        last.then_inc(s_T, 1)
                    pe.wait_ge(s_T_sb, 2 * nxt.i + 2)
                    for q in range(G):
                        for c in range(KC):
                            last = mm(ps_logit[:, q, :], xgT[:, q, c, :], gate_w[:, c, :], c, KC)
                    last.then_inc(s_lgp, 1)

            turns(pe, route, -1, 1, GROUPS - 1, GROUPS)

            def expert(t):
                e, nxt = t, t + 1
                v, vn = e.parity, nxt.parity
                if e.within(E):
                    pe.wait_ge(s_w1[v], 16 * e.half + 16)
                    pe.wait_ge(s_xeT_sb, e.i + 1)
                    for h in range(2):
                        for c in range(HC // 2):
                            n = h * HC // 2 + c
                            for k in range(KC):
                                last = mm(ps_h[:, h, c * CAP:(c + 1) * CAP], w1[:, v, k, n * P:(n + 1) * P],
                                          xeT[:, v, k, :], k, KC)
                        last.then_inc(s_h, 1)
                if nxt.within(E):
                    pe.wait_ge(s_xe[vn], 16 * nxt.half + 16)
                    for c in range(KC):
                        last = nc.tensor.transpose(ps_T[:, vn, c * P:(c + 1) * P], xe[:, vn, c * P:(c + 1) * P], ident[:])
                    last.then_inc(s_xeT, 1)
                if e.within(E):
                    pe.wait_ge(s_w2[v], 32 * e.half + 32)
                    pe.wait_ge(s_ye_sb, e.i + 1)
                    mm(ps_y[:, v, 0:D], ones[0:1, :], b2[:, v, :], 0, 2)
                    for h in range(2):
                        pe.wait_ge(s_gelu, 2 * e.i + (h + 1))
                        for c in range(HC // 2):
                            n = h * HC // 2 + c
                            last = mm(ps_y[:, v, 0:D], hT[:, n, :], w2[:, v, n, :], 1 if n < HC - 1 else 2, 3)
                    last.then_inc(s_ye, 1)

            turns(pe, expert, -1, 1, E - 1, E)

        @block.vector
        def _(dve):
            back = Chain(dve, s_back, 13)
            accs = Chain(dve, s_acc, TOP - 1)
            dve.wait_ge(s_w, 16 * 3)
            dve.wait_ge(s_const, 10)
            dve.sem_inc(s_ye_sb, 2)
            dve.sem_inc(s_hot_pos, 1)
            dve.sem_inc(s_sum, 2)

            def route(t):
                g, nxt = t, t + 1
                if nxt.within(GROUPS):
                    v = nxt.parity
                    if not isinstance(nxt.i, int) or nxt.i > 0:
                        dve.wait_ge(s_T, 2 * nxt.i)
                        dve.wait_ge(s_xg_out, 16 * nxt.i)
                    dve.wait_ge(s_xg_kept, nxt.i + 1)
                    for q in range(G):
                        b = nxt.i * G + q
                        last = nc.vector.tensor_scalar(xg[:, q, :], at(y_nat, b), mean[:, bass.ds(b, 1)],
                                                       rstd[:, bass.ds(b, 1)], ALU.subtract, ALU.mult)
                    last.then_inc(s_xg, 1)
                    dve.wait_ge(s_lgp, nxt.i + 1)
                    nc.vector.tensor_tensor(lg[:], ps_logit, gate_b[:].unsqueeze(1).to_broadcast([S, G, E]),
                                            ALU.add).then_inc(s_lg, 1)
                    dve.wait_ge(s_lg, nxt.i + 1)
                    dve.sem_inc(s_took, 1)
                    for q in range(G):
                        last = nc.vector.max(top_v[:, v, q, :], lg[:, q, :])
                    last.then_inc(s_topv, 1)
                    dve.wait_ge(s_topv, nxt.i + 1)
                    dve.sem_inc(s_took, 1)
                    for q in range(G):
                        last = nc.vector.max_index(top_i[:, q, :], top_v[:, v, q, :], lg[:, q, :])
                    last.then_inc(s_top, 1)
                    dve.wait_ge(s_top, nxt.i + 1)
                    nc.vector.tensor_copy(top_f[:, v], top_i[:, :, 0:TOP]).then_inc(s_topf, 1)
                    dve.wait_ge(s_topf, nxt.i + 1)
                    for q in range(G):
                        last = nc.vector.tensor_tensor(
                            hot[:, v, q], iota_e[:].unsqueeze(1).to_broadcast([S, TOP, E]),
                            top_f[:, v, q, :].unsqueeze(2).to_broadcast([S, TOP, E]), ALU.is_equal)
                    last.then_inc(s_hot, 1)
                    dve.wait_ge(s_hot, nxt.i + 1)
                    nc.vector.tensor_tensor(hot01[:], hot[:, v, :, 0, :], hot[:, v, :, 1, :], ALU.add).then_inc(s_hot01, 1)
                    dve.wait_ge(s_hot01, nxt.i + 1)
                    nc.vector.tensor_tensor(mask[:, v], hot01[:], hot[:, v, :, 2, :], ALU.add).then_inc(s_mask, 1)
                    dve.wait_ge(s_mask, nxt.i + 1)
                    dve.wait_ge(s_earlier, nxt.i + 1)
                    nc.vector.reduce_sum(mask_sum[:], mask[:, v].rearrange("p g e -> p e g"), AX.X).then_inc(s_msum, 1)
                if g.within(GROUPS):
                    v = g.parity
                    back.start(g.i)
                    dve.wait_ge(s_place, g.i + 1)
                    for q in range(G):
                        last = nc.vector.tensor_tensor(hot_pos[:, q], hot[:, v, q],
                                                       ps_place[:, q, :].unsqueeze(1).to_broadcast([S, TOP, E]), ALU.mult)
                    last.then_inc(s_hot_pos, 1)
                    dve.wait_ge(s_hot_pos, g.i + 2)
                    back(nc.vector.reduce_sum(pos[:], hot_pos[:], AX.X))
                    back(nc.vector.tensor_scalar(capped[:], pos[:], float(CAP - 1), None, ALU.min))
                    back(nc.vector.scalar_tensor_tensor(out=slot[:], in0=top_f[:, v], scalar=float(CAP),
                                                        in1=capped[:], op0=ALU.mult, op1=ALU.add))
                    back(nc.vector.tensor_copy(y_row[:, bass.ds(g.i * G, G), :], slot[:]))
                    back(nc.vector.tensor_scalar(full[:], pos[:], float(CAP), float(FAR), ALU.is_ge, ALU.mult))
                    back(nc.vector.tensor_tensor(full[:], full[:], top_f[:, v], ALU.add))
                    back(nc.vector.scalar_tensor_tensor(out=slot[:], in0=pos[:], scalar=float(E), in1=full[:],
                                                        op0=ALU.mult, op1=ALU.add))
                    if not isinstance(g.i, int) or g.i > 1:
                        dve.wait_ge(s_scat[v], g.half * (16 * G * TOP))
                    nc.vector.tensor_copy(slot_u[:, v], slot[:])
                    nc.vector.tensor_scalar(row_u[:, v], row_f[:], 0.0, None, ALU.add).then_inc(s_slots, 1)
                    nc.vector.tensor_tensor(logit[:], top_v[:, v, :, 0:TOP],
                                            top_v[:, v, :, 0:1].to_broadcast([S, G, TOP]), ALU.subtract).then_inc(s_logit, 1)
                    dve.wait_ge(s_slots, g.i + 1)
                    back(nc.vector.tensor_scalar(row_f[:], row_f[:], float(G * S), None, ALU.add))
                    back(nc.vector.tensor_scalar(taken[:], pos[:], float(CAP), None, ALU.is_lt))
                    dve.wait_ge(s_exp, g.i + 1)
                    back(nc.vector.reduce_sum(sums[:], expd[:], AX.X))
                    back(nc.vector.reciprocal(recs[:], sums[:]))
                    back(nc.vector.tensor_tensor(share[:], expd[:], recs[:].unsqueeze(2).to_broadcast([S, G, TOP]), ALU.mult))
                    back(nc.vector.tensor_tensor(gates[:, bass.ds(g.i * G, G), :], share[:], taken[:], ALU.mult))
                    back.end()

            turns(dve, route, -1, 1, GROUPS - 1, GROUPS)

            def expert(t):
                v = t.parity
                dve.wait_ge(s_ye, t.i + 3)
                if not isinstance(t.i, int) or t.i > 1:
                    dve.wait_ge(s_yout[v], t.half * 16)
                nc.vector.tensor_copy(ye[:, v, :], ps_y[:, v, 0:D]).then_inc(s_ye_sb, 1)

            turns(dve, expert, 0, 2, E, E)
            dve.wait_ge(s_xg_kept, GROUPS + 1)

            def combine(t):
                v = t.parity
                accs.start(t.i)
                dve.wait_ge(s_got[v], t.half * (16 * TOP) + 16 * TOP)
                src = at(y_nat, t.i)
                for k in range(TOP):
                    last_k = k == TOP - 1
                    ins = nc.vector.scalar_tensor_tensor(
                        out=at(y_nat, t.i) if last_k else acc[:, k % 2, :], in0=got[:, v, k, :],
                        scalar=at(gates, t.i)[:, k:k + 1], in1=src, op0=ALU.mult, op1=ALU.add)
                    if last_k:
                        ins.then_inc(s_sum, 1)
                    else:
                        accs(ins)
                    src = acc[:, k % 2, :]
                accs.end()
                dve.wait_ge(s_sum, t.i + 3)
                nc.vector.bn_stats(at(keep["stats"], t.i), at(y_nat, t.i)).then_inc(s_stats, 1)

            turns(dve, combine, 0, 0, B, B)

        finish_norm(nc, m, block, keep, s_stats)


def head_masks(nc, eng, tile, s_const):
    heads = tile.shape[1]
    d = P // heads
    nc.gpsimd.memset(tile[:], 1.0).then_inc(s_const, 1)
    eng.wait_ge(s_const, 1)
    nc.gpsimd.affine_select(out=tile[:], in_=tile[:], pattern=[[-d, heads]], compare_op=ALU.is_ge, fill=0.0,
                            base=0, channel_multiplier=1).then_inc(s_const, 1)
    eng.wait_ge(s_const, 2)
    nc.gpsimd.affine_select(out=tile[:], in_=tile[:], pattern=[[d, heads]], compare_op=ALU.is_ge, fill=0.0,
                            base=d - 1, channel_multiplier=-1).then_inc(s_const, 1)


def causal_heads(nc, io, keep):
    B, S, D = io["x"].shape
    NH = io["L1_attn_m"].shape[0]
    HD = D // NH
    KC = D // P
    HC = NH // KC
    BH = HC // 2
    SCALE = float(D) ** -0.5
    LOW = -1e30
    y_nat, mean, rstd = keep["y"], keep["mean"], keep["rstd"]
    with ExitStack() as ctx:
        m = Names(nc, ctx, "cau")
        w = m.sb("w", [P, KC, 3 * D])
        slope = m.sb("slope", [S, NH])
        rel_i = m.sb("rel_i", [S, S], mybir.dt.int32)
        rel = m.sb("rel", [S, S])
        bias = m.sb("bias", [S, NH, S])
        in_head = m.sb("in_head", [P, HC])
        ident = m.sb("ident", [P, P])
        xn = m.sb("xn", [S, 2, D])
        xT = m.sb("xT", [P, KC, S])
        qT = m.sb("qT", [P, KC, S])
        k_heads = m.sb("k_heads", [P, KC, HC, S])
        vals = m.sb("vals", [S, 2, NH, HD + 1])
        sc = m.sb("sc", [S, KC, HC, S])
        mx = m.sb("mx", [S, KC, HC])
        low = m.sb("low", [S, KC, HC, S])
        prob = m.sb("prob", [S, KC, HC, S])
        probT = m.sb("probT", [S, KC, HC, S])
        rec = m.sb("rec", [S, NH])
        att = m.sb("att", [S, NH, HD])
        ps_x = m.ps("ps_x", [P, 512])
        ps_kk = m.ps("ps_kk", [P, 512])
        ps_v = m.ps("ps_v", [P, 512])
        ps_s = m.ps("ps_s", [P, 2, 512])
        ps_t = m.ps("ps_t", [P, 2, 512])
        ps_o = m.ps("ps_o", [P, 512])
        ps_xT = ps_x[:, 0:KC * S].rearrange("p (c s) -> p c s", c=KC)
        ps_q = ps_x[:, KC * S:2 * KC * S].rearrange("p (c s) -> p c s", c=KC)
        ps_k = ps_kk[:, 0:KC * S].rearrange("p (c s) -> p c s", c=KC)
        ps_sum = ps_o[0:S, 0:NH * (HD + 1)].rearrange("p (h d) -> p h d", h=NH)
        ps_sc = ps_s[0:S, :, 0:BH * S]
        ps_pT = ps_t[0:S, :, 0:BH * S]

        sem = m.sem
        s_w, s_const, s_head = sem("weights"), sem("constants"), sem("head_masks")
        s_rel, s_bias = sem("distances"), sem("bias_table")
        s_xn, s_xT, s_xT_sb = sem("rows_normalised"), sem("xT_transposed"), sem("xT_stored")
        s_xn_kept = sem("rows_normalised_in_place")
        s_k, s_q, s_q_sb, s_k_sb = sem("k_projected"), sem("q_projected"), sem("q_stored"), sem("k_spread")
        s_v, s_v_sb = sem("values"), sem("values_stored")
        s_s, s_sc, s_mx = sem("scores"), sem("scores_biased"), sem("maxima")
        s_low, s_p = sem("maxima_subtracted"), sem("weights_ready")
        s_t, s_t_sb = sem("weights_transposed"), sem("weightsT_stored")
        s_o, s_rec, s_att = sem("values_summed"), sem("sums_inverted"), sem("attended")
        s_sum, s_stats, s_took = sem("rows_added"), sem("stats_ready"), sem("waits_taken")
        block = ctx.enter_context(nc.Block())

        @block.sync
        def _(sp):
            sp.dma_start(w[:], io["L1_attn_W_kqv"].rearrange("(c p) n -> p c n", p=P)).then_inc(s_w, 16)
            sp.dma_start(slope[:], io["L1_attn_m"].rearrange("h a b -> (h a b)").partition_broadcast(S)).then_inc(s_w, 16)

        @block.gpsimd
        def _(pool):
            head_masks(nc, pool, in_head, s_head)
            nc.gpsimd.memset(ident[:], 1.0).then_inc(s_const, 1)
            nc.gpsimd.memset(vals[:, :, :, HD:HD + 1], 1.0).then_inc(s_const, 1)
            nc.gpsimd.iota(rel_i[:], pattern=[[1, S]], base=0, channel_multiplier=-1).then_inc(s_const, 1)
            pool.wait_ge(s_const, 3)
            nc.gpsimd.affine_select(out=ident[:], in_=ident[:], pattern=[[1, P]], compare_op=ALU.is_equal,
                                    fill=0.0, base=0, channel_multiplier=-1).then_inc(s_const, 1)
            nc.gpsimd.tensor_copy(rel[:], rel_i[:]).then_inc(s_rel, 1)
            pool.wait_ge(s_rel, 1)
            pool.wait_ge(s_w, 32)
            nc.gpsimd.tensor_tensor(bias[:], rel[:].unsqueeze(1).to_broadcast([S, NH, S]),
                                    slope[:].unsqueeze(2).to_broadcast([S, NH, S]), ALU.mult).then_inc(s_rel, 1)
            pool.wait_ge(s_rel, 2)
            nc.gpsimd.affine_select(out=bias[:], in_=bias[:], pattern=[[0, NH], [-1, S]], compare_op=ALU.is_ge,
                                    fill=LOW, base=0, channel_multiplier=1).then_inc(s_bias, 1)

            def turn(t):
                for h in range(KC):
                    pool.wait_ge(s_mx, 2 * t.i + (h + 1))
                    pool.wait_ge(s_p, 2 * t.i + (h + 1))
                    nc.gpsimd.tensor_tensor(low[:, h], sc[:, h], mx[:, h].unsqueeze(2).to_broadcast([S, HC, S]),
                                            ALU.subtract).then_inc(s_low, 1)

            turns(pool, turn, 0, 0, B, B)

        @block.scalar
        def _(act):
            act.sem_inc(s_p, 2)

            def weightsT(b, h):
                act.wait_ge(s_t, 2 * b.i + (h + 3))
                nc.scalar.copy(probT[:, h].rearrange("p (a h) s -> p a (h s)", a=2), ps_pT).then_inc(s_t_sb, 1)

            def weights(b, h):
                act.wait_ge(s_low, 2 * b.i + (h + 1))
                act.wait_ge(s_t, 2 * b.i + (h + 1))
                nc.scalar.activation(prob[:, h], low[:, h], ACT.Exp).then_inc(s_p, 1)

            def turn(t):
                b, nxt, far = t, t + 1, t + 2
                if b.within(B):
                    weightsT(b, 0)
                if far.within(B):
                    act.wait_ge(s_xT, far.i + 1)
                    nc.scalar.copy(xT[:], ps_xT).then_inc(s_xT_sb, 1)
                if b.within(B):
                    weightsT(b, 1)
                if far.within(B):
                    act.wait_ge(s_k, far.i + 1)
                    for h in range(HC):
                        last = nc.scalar.activation(k_heads[:, :, h, :], ps_k, ACT.Copy, scale=in_head[:, h:h + 1])
                    last.then_inc(s_k_sb, 1)
                    act.wait_ge(s_q, far.i + 1)
                    nc.scalar.copy(qT[:], ps_q).then_inc(s_q_sb, 1)
                if nxt.within(B):
                    weights(nxt, 0)
                if far.within(B):
                    act.wait_ge(s_v, far.i + 1)
                    nc.scalar.copy(vals[:, far.parity, :, 0:HD],
                                   ps_v[0:S, 0:D].rearrange("p (h d) -> p h d", h=NH)).then_inc(s_v_sb, 1)
                if nxt.within(B):
                    weights(nxt, 1)

            act.wait_ge(s_head, 3)
            act.wait_ge(s_const, 4)
            turns(act, turn, -2, 0, B - 2, B)

        @block.vector
        def _(dve):
            dve.wait_ge(s_w, 32)
            dve.wait_ge(s_bias, 1)
            dve.wait_ge(s_head, 3)
            dve.sem_inc(s_att, 1)

            def turn(t):
                b, nxt, far = t, t + 1, t + 2
                if far.within(B):
                    nc.vector.tensor_scalar(xn[:, far.parity, :], at(y_nat, far.i), mean[:, bass.ds(far.i, 1)],
                                            rstd[:, bass.ds(far.i, 1)], ALU.subtract, ALU.mult).then_inc(s_xn, 1)
                    nc.vector.tensor_scalar(at(y_nat, far.i), at(y_nat, far.i), mean[:, bass.ds(far.i, 1)],
                                            rstd[:, bass.ds(far.i, 1)], ALU.subtract, ALU.mult).then_inc(s_xn_kept, 1)
                if nxt.within(B):
                    for h in range(KC):
                        dve.wait_ge(s_s, 2 * nxt.i + (h + 1))
                        if not isinstance(nxt.i, int) or nxt.i > 0:
                            dve.wait_ge(s_low, 2 * nxt.i + (h - 1))
                        nc.vector.scalar_tensor_tensor(
                            out=sc[:, h].rearrange("p (a h) s -> p a (h s)", a=2), in0=ps_sc, scalar=SCALE,
                            in1=bias[:, h * HC:(h + 1) * HC].rearrange("p (a h) s -> p a (h s)", a=2),
                            op0=ALU.mult, op1=ALU.add).then_inc(s_sc, 1)
                        dve.wait_ge(s_sc, 2 * nxt.i + (h + 1))
                        nc.vector.reduce_max(mx[:, h], sc[:, h], AX.X).then_inc(s_mx, 1)
                if b.within(B):
                    dve.wait_ge(s_o, b.i + 1)
                    nc.vector.reciprocal(rec[:], ps_sum[:, :, HD]).then_inc(s_rec, 1)
                    dve.wait_ge(s_rec, b.i + 1)
                    nc.vector.tensor_tensor(att[:], ps_sum[:, :, 0:HD], rec[:].unsqueeze(2).to_broadcast([S, NH, HD]),
                                            ALU.mult).then_inc(s_att, 1)
                    dve.wait_ge(s_att, b.i + 2)
                    nc.vector.tensor_tensor(at(y_nat, b.i), att[:].rearrange("p h d -> p (h d)"),
                                            at(y_nat, b.i), ALU.add).then_inc(s_sum, 1)
                    dve.wait_ge(s_sum, b.i + 1)
                    nc.vector.bn_stats(at(keep["stats"], b.i), at(y_nat, b.i)).then_inc(s_stats, 1)

            turns(dve, turn, -2, 0, B - 2, B)

        @block.tensor
        def _(pe):
            def mm(out, lhsT, rhs, k, n):
                return nc.tensor.matmul(out, lhsT, rhs, start=(k == 0), stop=(k == n - 1))

            pe.wait_ge(s_w, 32)
            pe.wait_ge(s_const, 4)
            pe.sem_inc(s_t, 2)

            def weightsT(b, h):
                pe.wait_ge(s_p, 2 * b.i + (h + 3))
                if h:
                    pe.wait_ge(s_t_sb, 2 * b.i + h)
                for n in range(HC):
                    last = nc.tensor.transpose(ps_pT[:, n // BH, (n % BH) * S:(n % BH + 1) * S], prob[:, h, n, :],
                                               ident[0:S, 0:S])
                last.then_inc(s_t, 1)

            def sums(b, h):
                pe.wait_ge(s_t_sb, 2 * b.i + (h + 1))
                for n in range(HC):
                    last = mm(ps_sum[:, h * HC + n, :], probT[:, h, n, :], vals[:, b.parity, h * HC + n, :], 0, 1)
                if h == KC - 1:
                    last.then_inc(s_o, 1)

            def scores(b, h):
                if h == 0:
                    pe.wait_ge(s_q_sb, b.i + 1)
                    pe.wait_ge(s_k_sb, b.i + 1)
                if h or not isinstance(b.i, int) or b.i > 0:
                    pe.wait_ge(s_sc, 2 * b.i + h)
                for a in range(2):
                    last = mm(ps_sc[:, a, :], qT[:, h, :],
                              k_heads[:, h, a * BH:(a + 1) * BH, :].rearrange("p h s -> p (h s)"), 0, 1)
                last.then_inc(s_s, 1)

            def project(n, out, sem):
                for c in range(KC):
                    for k in range(KC):
                        last = mm(out[:, c, :], w[:, k, n * D + c * P:n * D + (c + 1) * P], xT[:, k, :], k, KC)
                last.then_inc(sem, 1)

            def turn(t):
                b, nxt, far = t, t + 1, t + 2
                if nxt.within(B):
                    scores(nxt, 0)
                if b.within(B):
                    weightsT(b, 0)
                if far.within(B):
                    pe.wait_ge(s_xn, far.i + 1)
                    for c in range(KC):
                        last = nc.tensor.transpose(ps_xT[:, c, :], xn[:, far.parity, c * P:(c + 1) * P], ident[0:S, 0:S])
                    last.then_inc(s_xT, 1)
                if nxt.within(B):
                    scores(nxt, 1)
                if far.within(B):
                    pe.wait_ge(s_xT_sb, far.i + 1)
                    project(0, ps_k, s_k)
                if b.within(B):
                    weightsT(b, 1)
                if far.within(B):
                    project(1, ps_q, s_q)
                if b.within(B):
                    pe.wait_ge(s_v_sb, b.i + 1)
                    pe.wait_ge(s_att, b.i + 1)
                    sums(b, 0)
                    sums(b, 1)
                if far.within(B):
                    if not isinstance(far.i, int) or far.i > 0:
                        pe.wait_ge(s_v_sb, far.i)
                    for k in range(KC):
                        last = mm(ps_v[0:S, 0:D], xT[:, k, :], w[:, k, 2 * D:3 * D], k, KC)
                    last.then_inc(s_v, 1)

            turns(pe, turn, -2, 0, B - 2, B)

        finish_norm(nc, m, block, keep, s_stats)


def relative_cross(nc, io, keep):
    B, S, D = io["x"].shape
    L = io["ctx_1024"].shape[1]
    N_REL, HD = io["L1_xattn_rel_k_table"].shape
    REACH = N_REL // 2
    ND = 2 * REACH
    NH = D // HD
    KC = D // P
    HC = NH // KC
    CH = 3
    STEP = L // CH
    R = L - (CH - 1) * STEP
    NEAR = S + REACH - 1
    LEFT = S - 1 - REACH
    RW = NEAR + S - 1
    PW = REACH + NEAR
    FAR = LEFT + 1
    PAIRS = NH // 2
    SCALE = float(HD) ** -0.5
    y_nat, mean, rstd = keep["y"], keep["mean"], keep["rstd"]
    r_rows = nc.dram_tensor("rel_scores", (2, S, NH, RW), F32, kind="Internal").ap()
    p_rows = nc.dram_tensor("rel_weights", (2, S, NH, PW), F32, kind="Internal").ap()
    with ExitStack() as ctx:
        m = Names(nc, ctx, "rel")
        w = {n: m.sb(n, [P, KC, D]) for n in ("Wq", "Wk", "Wv", "Wo")}
        cols = {n: m.sb(n + "_col", [P, KC]) for n in ("bq", "bk")}
        bv = m.sb("bv", [R, D])
        bo = m.sb("bo", [S, D])
        last_v = m.sb("last_v", [R, 1, HD])
        tabT = m.sb("tabT", [P, N_REL])
        tab_diff = m.sb("tab_diff", [P, ND])
        tabT_heads = m.sb("tabT_heads", [P, HC, ND])
        tab_v = m.sb("tab_v", [P, HD])
        tab_v_last = m.sb("tab_v_last", [P, HD])
        tab_v_pair = m.sb("tab_v_pair", [P, 2, HD])
        k_bias = m.sb("k_bias", [P, KC])
        v_bias = m.sb("v_bias", [R, NH, HD])
        in_head = m.sb("in_head", [P, HC])
        beyond = m.sb("beyond", [S, FAR])
        ident = m.sb("ident", [P, P])
        zeros = m.sb("zeros", [S, NH, RW - NEAR])
        ctx_T = m.sb("ctx_T", [P, 2, KC, L])
        xn = m.sb("xn", [S, D])
        xT = m.sb("xT", [P, KC, S])
        qT = m.sb("qT", [P, KC, S])
        q_heads = m.sb("q_heads", [P, 2, KC, HC, S])
        kT = m.sb("kT", [P, 2, KC, L])
        vals = m.sb("vals", [R, 2, CH, NH, HD + 1])
        r_ext = m.sb("r_ext", [S, NH, NEAR])
        r_key = m.sb("r_key", [S, NH, NEAR])
        mx = m.sb("mx", [S, NH])
        nmx = m.sb("nmx", [S, NH])
        prob = m.sb("prob", [S, 2, NH, L])
        probT = m.sb("probT", [R, 2, CH, S])
        far = m.sb("far", [S, NH, FAR])
        by_dist = m.sb("by_dist", [S, NH, ND])
        distT = m.sb("distT", [P, PAIRS, S])
        att = m.sb("att", [S, NH, HD + 1])
        summed = m.sb("summed", [S, NH, HD])
        rec = m.sb("rec", [S, NH])
        att_n = m.sb("att_n", [S, D])
        attT = m.sb("attT", [P, KC, S])
        xb = m.sb("xb", [S, 2, D])
        ps_m = m.ps("ps_m", [P, 2, 512])
        ps_s = m.ps("ps_s", [P, 2, 2, 512])
        ps_t = m.ps("ps_t", [P, 512])
        ps_o = m.ps("ps_o", [P, 512])
        ps_two, ps_k, ps_v, ps_r, ps_dT, ps_w2 = [], [], [], [], [], []
        for v in range(2):
            ps_two.append(ps_m[:, v, 0:KC * S].rearrange("p (c s) -> p c s", c=KC))
            ps_k.append(ps_m[:, v, 0:L])
            ps_v.append(ps_m[0:R, v, 0:D])
            ps_r.append(ps_m[0:S, v, 0:HC * ND])
            ps_dT.append(ps_m[:, v, 0:PAIRS // 2 * S].rearrange("p (n s) -> p n s", n=PAIRS // 2))
            ps_w2.append(ps_m[0:S, v, 0:D])
        ps_out = ps_w2
        ps_pT = ps_t[0:R, 0:CH * S].rearrange("p (c s) -> p c s", c=CH)
        ps_sum = ps_o[0:S, 0:NH * (HD + 1)].rearrange("p (h d) -> p h d", h=NH)

        sem = m.sem
        s_w, s_const, s_head, s_zero = sem("weights"), sem("constants"), sem("head_masks"), sem("zeros_in_dram")
        s_tab, s_ready = sem("table_steps"), sem("tables_ready")
        s_ctx = [sem(f"context{v}_loaded") for v in range(2)]
        s_xn = sem("rows_normalised")
        s_job = [sem(f"bank{v}_filled") for v in range(2)]
        s_job_sb = [sem(f"bank{v}_emptied") for v in range(2)]
        s_xb = sem("residual_ready")
        s_qh = sem("queries_spread")
        s_rpad = sem("distances_padded")
        s_rout, s_rkey = sem("distances_in_dram"), sem("distances_by_key")
        s_s, s_add, s_max, s_neg, s_p = (sem("scores"), sem("scores_added"), sem("maxima"), sem("maxima_scaled"),
                                         sem("weights_ready"))
        s_t, s_t_sb, s_pv, s_att = sem("weights_transposed"), sem("weightsT_stored"), sem("values_summed"), sem("sums_stored")
        s_pout, s_pdist, s_far, s_far_sum = (sem("weights_in_dram"), sem("weights_by_distance"), sem("far_masked"),
                                             sem("far_summed"))
        s_tail = sem("tail_chain")
        s_stats, s_took = sem("stats_ready"), sem("waits_taken")
        block = ctx.enter_context(nc.Block())

        JOBS = [("next", "xT"), ("next", "q"), ("next", "r0"), ("next", "r1"), ("next", "k0"), ("next", "k1"),
                ("next", "v0"), ("next", "v1"), ("next", "v2"), ("last", "d0"), ("last", "d1"), ("last", "w2"),
                ("last", "aT"), ("last", "out")]
        SLOTS = [(0,), (1,), (2, 3), (4, 5), (6, 7), (8, 9), (10, 11), (12, 13)]
        NUMBER = {what: n for n, (_, what) in enumerate(JOBS)}

        def share(v, n, *kinds):
            return sum(k % 2 == v and who in kinds for k, (who, _) in enumerate(JOBS[:n]))

        def before(t, n):
            v, nj = n % 2, len(JOBS)
            nexts = share(v, nj, "next")
            if isinstance(t.i, int) and t.i <= 0:
                return (t.i + 1) * nexts + share(v, n, "next")
            if isinstance(t.i, int) and t.i >= B - 1:
                return (2 * nexts + (B - 2) * share(v, nj, "next", "last")
                        + (t.i - (B - 1)) * share(v, nj, "last") + share(v, n, "last"))
            return 2 * nexts + (t.i - 1) * share(v, nj, "next", "last") + share(v, n, "next", "last")

        def wait_filled(eng, t, what):
            n = NUMBER[what]
            eng.wait_ge(s_job[n % 2], before(t, n) + 1)

        def wait_emptied(eng, t, what):
            n = NUMBER[what]
            eng.wait_ge(s_job_sb[n % 2], before(t, n) + 1)

        def jobs(t, slot):
            for n in SLOTS[slot]:
                who, what = JOBS[n]
                b = t + 1 if who == "next" else t + -1
                if b.within(B):
                    yield n, what, b

        @block.sync
        def _(sp):
            for n, tile in w.items():
                sp.dma_start(tile[:], io["L1_xattn_" + n].rearrange("(c p) d -> p c d", p=P)).then_inc(s_w, 16)
            for n, tile in cols.items():
                sp.dma_start(tile[:], io[f"L1_xattn_{n}_cols"]).then_inc(s_w, 16)
            sp.dma_start(bv[:], io["L1_xattn_bv"].partition_broadcast(R)).then_inc(s_w, 16)
            sp.dma_start(bo[:], io["L1_xattn_bo"].partition_broadcast(S)).then_inc(s_w, 16)
            sp.dma_start(last_v[:, 0, :], io["L1_xattn_rel_v_table"][N_REL - 1].partition_broadcast(R)).then_inc(s_w, 16)
            sp.dma_start(tab_v_last[:], io["L1_xattn_rel_v_table"][N_REL - 1].partition_broadcast(P)).then_inc(s_w, 16)
            for h in range(HC):
                sp.dma_start(tabT[h * HD:(h + 1) * HD, :], io["L1_xattn_rel_k_tableT"]).then_inc(s_w, 16)
            for h in range(2):
                sp.dma_start(tab_v[h * ND:(h + 1) * ND, :], io["L1_xattn_rel_v_table"][0:ND]).then_inc(s_w, 16)
            sp.wait_ge(s_const, 4)
            for v in range(2):
                sp.dma_start(r_rows[v, :, :, NEAR:RW], zeros[:]).then_inc(s_zero, 16)
                sp.dma_start(p_rows[v, :, :, 0:REACH], zeros[:, :, 0:REACH]).then_inc(s_zero, 16)
            sp.wait_ge(s_zero, 64)

            def turn(t):
                b, nxt, prev = t, t + 1, t + -1
                if nxt.within(B):
                    if not isinstance(nxt.i, int) or nxt.i > 1:
                        wait_filled(sp, t + -2, "v2")
                    sp.sem_inc(s_took, 1)
                    sp.dma_start(ctx_T[:, nxt.parity], io["ctxT"].rearrange("b (c p) l -> p b c l", p=P)[
                        :, bass.ds(nxt.i, 1)].rearrange("p b c l -> p (b c) l")).then_inc(s_ctx[nxt.parity], 16)
                if prev.within(B):
                    v = prev.parity
                    sp.wait_ge(s_p, PAIRS * prev.i + (PAIRS + 2))
                    sp.dma_start(p_rows[v, :, :, REACH:PW], prob[:, v, :, 0:NEAR]).then_inc(s_pout, 16)
                    sp.wait_ge(s_pout, 16 * prev.i + 16)
                    sp.sem_inc(s_took, 1)
                    if not isinstance(prev.i, int) or prev.i > 0:
                        wait_filled(sp, t + -1, "d1")
                    sp.dma_start(by_dist[:], bass.AP(p_rows.tensor, p_rows[v].offset,
                                                     [[NH * PW + 1, S], [PW, NH], [1, ND]])).then_inc(s_pdist, 16)
                if nxt.within(B):
                    v = nxt.parity
                    sp.wait_ge(s_rpad, nxt.i + 1)
                    sp.dma_start(r_rows[v, :, :, 0:NEAR], r_ext[:]).then_inc(s_rout, 16)
                    sp.wait_ge(s_rout, 16 * nxt.i + 16)
                    sp.sem_inc(s_took, 1)
                    if not isinstance(nxt.i, int) or nxt.i > 0:
                        sp.wait_ge(s_add, PAIRS * nxt.i)
                    sp.dma_start(r_key[:], bass.AP(r_rows.tensor, r_rows[v].offset + (S - 1),
                                                   [[NH * RW - 1, S], [RW, NH], [1, NEAR]])).then_inc(s_rkey, 16)

            turns(sp, turn, -1, 3, B - 1, B + 1)

        @block.gpsimd
        def _(pool):
            head_masks(nc, pool, in_head, s_head)
            nc.gpsimd.memset(ident[:], 1.0).then_inc(s_const, 1)
            nc.gpsimd.memset(beyond[:], 1.0).then_inc(s_const, 1)
            nc.gpsimd.memset(zeros[:], 0.0).then_inc(s_const, 1)
            nc.gpsimd.memset(vals[:, :, :, :, HD:HD + 1], 1.0).then_inc(s_const, 1)
            nc.gpsimd.memset(tab_v_pair[:], 0.0).then_inc(s_const, 1)
            pool.wait_ge(s_const, 5)
            nc.gpsimd.affine_select(out=ident[:], in_=ident[:], pattern=[[1, P]], compare_op=ALU.is_equal,
                                    fill=0.0, base=0, channel_multiplier=-1).then_inc(s_const, 1)
            nc.gpsimd.affine_select(out=beyond[:], in_=beyond[:], pattern=[[-1, FAR]], compare_op=ALU.is_ge,
                                    fill=0.0, base=-REACH, channel_multiplier=1).then_inc(s_const, 1)
            pool.wait_ge(s_ready, 1)

            def turn(t):
                nxt, prev = t + 1, t + -1
                if prev.within(B):
                    pool.wait_ge(s_p, PAIRS * prev.i + (PAIRS + 2))
                    if not isinstance(prev.i, int) or prev.i > 0:
                        pool.wait_ge(s_far_sum, prev.i)
                    nc.gpsimd.tensor_tensor(far[:], prob[:, prev.parity, :, 0:FAR],
                                            beyond[:].unsqueeze(1).to_broadcast([S, NH, FAR]), ALU.mult).then_inc(s_far, 1)
                if nxt.within(B):
                    wait_emptied(pool, t, "r1")
                    nc.gpsimd.tensor_tensor(q_heads[:, nxt.parity], qT[:].unsqueeze(2).to_broadcast([P, KC, HC, S]),
                                            in_head[:].unsqueeze(1).unsqueeze(3).to_broadcast([P, KC, HC, S]),
                                            ALU.mult).then_inc(s_qh, 1)
                    nc.gpsimd.tensor_copy(r_ext[:, :, 0:LEFT], r_ext[:, :, LEFT:LEFT + 1].to_broadcast([S, NH, LEFT])
                                          ).then_inc(s_rpad, 1)
                    pool.wait_ge(s_xn, nxt.i + 1)
                    if not isinstance(prev.i, int) or prev.i >= 0:
                        pool.wait_ge(s_stats, prev.i + 1)
                    nc.gpsimd.tensor_tensor(xb[:, nxt.parity], xn[:], bo[:], ALU.add).then_inc(s_xb, 1)

            turns(pool, turn, -1, 3, B - 1, B + 1)

        ON_ACT = ("xT", "r0", "r1", "k0", "k1", "aT")

        @block.scalar
        def _(act):
            act.wait_ge(s_ready, 1)
            act.sem_inc(s_p, 2)

            def empty(t, n, what, b):
                bank = n % 2
                wait_filled(act, t, what)
                if what == "xT":
                    nc.scalar.copy(xT[:], ps_two[bank]).then_inc(s_job_sb[bank], 1)
                elif what in ("r0", "r1"):
                    h = int(what[1])
                    if h == 0 and (not isinstance(b.i, int) or b.i > 0):
                        act.wait_ge(s_rout, 16 * b.i)
                    nc.scalar.copy(r_ext[:, h * HC:(h + 1) * HC, LEFT:NEAR],
                                   ps_r[bank].rearrange("p (h r) -> p h r", h=HC)).then_inc(s_job_sb[bank], 1)
                elif what in ("k0", "k1"):
                    c = int(what[1])
                    nc.scalar.activation(kT[:, b.parity, c, :], ps_k[bank], ACT.Identity,
                                         bias=k_bias[:, c:c + 1]).then_inc(s_job_sb[bank], 1)
                else:
                    nc.scalar.copy(attT[:], ps_two[bank]).then_inc(s_job_sb[bank], 1)

            def turn(t):
                for n in range(PAIRS):
                    pt = (t, n - 2) if n >= 2 else (t + -1, n + PAIRS - 2)
                    if pt[0].within(B):
                        g = PAIRS * pt[0].i + pt[1]
                        for h in range(2):
                            act.wait_ge(s_t, 2 * g + (h + 1))
                            if h == 0 and (not isinstance(g, int) or g > 0):
                                act.wait_ge(s_pv, g)
                            nc.scalar.copy(probT[:, h], ps_pT).then_inc(s_t_sb, 1)
                    if t.within(B):
                        act.wait_ge(s_neg, PAIRS * t.i + (n + 1))
                        if n == 0 and (not isinstance(t.i, int) or t.i > 1):
                            act.wait_ge(s_pout, 16 * (t.i - 1))
                            act.wait_ge(s_far, t.i - 1)
                        for h in range(2):
                            last = nc.scalar.activation(prob[:, t.parity, 2 * n + h, :], ps_s[0:S, n % 2, h, 0:L], ACT.Exp,
                                                        bias=nmx[:, 2 * n + h:2 * n + h + 1], scale=SCALE)
                        last.then_inc(s_p, 1)
                    for k, what, b in jobs(t, n):
                        if what in ON_ACT:
                            empty(t, k, what, b)

            turns(act, turn, -1, 3, B - 1, B + 1)

        @block.vector
        def _(dve):
            tab = Chain(dve, s_tab, 6)
            tab.start(0)
            dve.wait_ge(s_w, 16 * (4 + 2 + 4 + HC + 2))
            dve.wait_ge(s_head, 3)
            dve.wait_ge(s_const, 7)
            nc.vector.tensor_scalar(k_bias[:], cols["bk"][:], tabT[:, ND:ND + 1], None, ALU.add)
            tab(nc.vector.tensor_scalar(tab_diff[:], tabT[:, 0:ND], tabT[:, ND:ND + 1], None, ALU.subtract))
            tab(nc.vector.tensor_tensor(tabT_heads[:], tab_diff[:].unsqueeze(1).to_broadcast([P, HC, ND]),
                                        in_head[:].unsqueeze(2).to_broadcast([P, HC, ND]), ALU.mult))
            tab(nc.vector.tensor_tensor(v_bias[:], bv[:].rearrange("p (h d) -> p h d", h=NH),
                                        last_v[:, 0:1, :].to_broadcast([R, NH, HD]), ALU.add))
            tab(nc.vector.tensor_tensor(tab_v[:], tab_v[:], tab_v_last[:], ALU.subtract))
            tab(nc.vector.tensor_copy(tab_v_pair[0:ND, 0, :], tab_v[0:ND, :]))
            tab(nc.vector.tensor_copy(tab_v_pair[ND:2 * ND, 1, :], tab_v[ND:2 * ND, :]))
            dve.sem_inc(s_ready, 1)
            tail = Chain(dve, s_tail, 2)

            def empty(t, n, what, b):
                bank = n % 2
                wait_filled(dve, t, what)
                if what == "q":
                    nc.vector.tensor_tensor(qT[:], ps_two[bank], cols["bq"][:].unsqueeze(2).to_broadcast([P, KC, S]),
                                            ALU.add).then_inc(s_job_sb[bank], 1)
                elif what in ("v0", "v1", "v2"):
                    c = int(what[1])
                    nc.vector.tensor_tensor(vals[:, b.parity, c, :, 0:HD], ps_v[bank].rearrange("p (h d) -> p h d", h=NH),
                                            v_bias[:], ALU.add).then_inc(s_job_sb[bank], 1)
                elif what in ("d0", "d1"):
                    h = int(what[1])
                    nc.vector.tensor_copy(distT[:, h * PAIRS // 2:(h + 1) * PAIRS // 2, :], ps_dT[bank]).then_inc(s_job_sb[bank], 1)
                elif what == "w2":
                    tail.start(b.i)
                    tail(nc.vector.reciprocal(rec[:], att[:, :, HD]))
                    nc.vector.tensor_tensor(summed[:], ps_w2[bank].rearrange("p (h d) -> p h d", h=NH), att[:, :, 0:HD],
                                            ALU.add).then_inc(s_job_sb[bank], 1)
                    wait_emptied(dve, t, what)
                    tail(nc.vector.tensor_tensor(att_n[:].rearrange("p (h d) -> p h d", h=NH), summed[:],
                                                 rec[:].unsqueeze(2).to_broadcast([S, NH, HD]), ALU.mult))
                elif what == "out":
                    dve.wait_ge(s_xb, b.i + 1)
                    nc.vector.tensor_tensor(at(y_nat, b.i), ps_out[bank], xb[:, b.parity], ALU.add).then_inc(s_job_sb[bank], 1)
                    wait_emptied(dve, t, what)
                    nc.vector.bn_stats(at(keep["stats"], b.i), at(y_nat, b.i)).then_inc(s_stats, 1)
                    tail.end()

            def turn(t):
                nxt, prev = t + 1, t + -1
                for n in range(PAIRS):
                    if n == 0 and nxt.within(B):
                        if not isinstance(nxt.i, int) or nxt.i > 0:
                            dve.wait_ge(s_xb, nxt.i)
                        nc.vector.tensor_scalar(xn[:], at(y_nat, nxt.i), mean[:, bass.ds(nxt.i, 1)],
                                                rstd[:, bass.ds(nxt.i, 1)], ALU.subtract, ALU.mult).then_inc(s_xn, 1)
                    if t.within(B):
                        g = PAIRS * t.i + n
                        bank = ps_s[0:S, n % 2]
                        two = slice(2 * n, 2 * n + 2)
                        if n == 0:
                            dve.wait_ge(s_rkey, 16 * t.i + 16)
                        dve.wait_ge(s_s, g + 1)
                        nc.vector.tensor_tensor(bank[:, :, 0:NEAR], bank[:, :, 0:NEAR], r_key[:, two, :],
                                                ALU.add).then_inc(s_add, 1)
                        dve.wait_ge(s_add, g + 1)
                        nc.vector.reduce_max(mx[:, two], bank[:, :, 0:L], AX.X).then_inc(s_max, 1)
                        dve.wait_ge(s_max, g + 1)
                        nc.vector.tensor_scalar(nmx[:, two], mx[:, two], -SCALE, None, ALU.mult).then_inc(s_neg, 1)
                    if n == 1 and prev.within(B):
                        dve.wait_ge(s_pv, PAIRS * prev.i + PAIRS)
                        nc.vector.tensor_copy(att[:], ps_sum).then_inc(s_att, 1)
                    if n == 4 and prev.within(B):
                        dve.wait_ge(s_far, prev.i + 1)
                        dve.wait_ge(s_pdist, 16 * prev.i + 16)
                        nc.vector.reduce_sum(by_dist[:, :, 0], far[:], AX.X).then_inc(s_far_sum, 1)
                    for k, what, b in jobs(t, n):
                        if what not in ON_ACT:
                            empty(t, k, what, b)

            turns(dve, turn, -1, 3, B - 1, B + 1)

        @block.tensor
        def _(pe):
            def mm(out, lhsT, rhs, k, n):
                return nc.tensor.matmul(out, lhsT, rhs, start=(k == 0), stop=(k == n - 1))

            pe.wait_ge(s_ready, 1)

            def fill(t, n, what, b):
                bank = n % 2
                o = before(t, n)
                if not isinstance(o, int) or o > 0:
                    pe.wait_ge(s_job_sb[bank], o)
                if what == "xT":
                    pe.wait_ge(s_xn, b.i + 1)
                    for c in range(KC):
                        last = nc.tensor.transpose(ps_two[bank][:, c, :], xn[:, c * P:(c + 1) * P], ident[0:S, 0:S])
                elif what == "q":
                    wait_emptied(pe, t, "xT")
                    for c in range(KC):
                        for k in range(KC):
                            last = mm(ps_two[bank][:, c, :], w["Wq"][:, k, c * P:(c + 1) * P], xT[:, k, :], k, KC)
                elif what in ("r0", "r1"):
                    if what == "r0":
                        wait_emptied(pe, t, "q")
                    last = mm(ps_r[bank], qT[:, int(what[1]), :], tabT_heads[:].rearrange("p h r -> p (h r)"), 0, 1)
                elif what in ("k0", "k1"):
                    c = int(what[1])
                    if c == 0:
                        pe.wait_ge(s_ctx[b.parity], 16 * b.half + 16)
                    for k in range(KC):
                        last = mm(ps_k[bank], w["Wk"][:, k, c * P:(c + 1) * P], ctx_T[:, b.parity, k, :], k, KC)
                elif what in ("v0", "v1", "v2"):
                    c = int(what[1])
                    for k in range(KC):
                        last = mm(ps_v[bank], ctx_T[:, b.parity, k, c * STEP:c * STEP + R], w["Wv"][:, k, :], k, KC)
                elif what in ("d0", "d1"):
                    h = int(what[1])
                    pe.wait_ge(s_far_sum, b.i + 1)
                    for k in range(PAIRS // 2):
                        p = h * (PAIRS // 2) + k
                        last = nc.tensor.transpose(ps_dT[bank][:, k, :], by_dist[:, 2 * p:2 * p + 2, :].rearrange("p h r -> p (h r)"),
                                                   ident[0:S, 0:S])
                elif what == "w2":
                    wait_emptied(pe, t, "d0")
                    wait_emptied(pe, t, "d1")
                    for p in range(PAIRS):
                        last = mm(ps_w2[bank][:, p * 2 * HD:(p + 1) * 2 * HD], distT[:, p, :],
                                  tab_v_pair[:].rearrange("p h d -> p (h d)"), 0, 1)
                elif what == "aT":
                    pe.wait_ge(s_tail, 2 * b.i + 2)
                    for c in range(KC):
                        last = nc.tensor.transpose(ps_two[bank][:, c, :], att_n[:, c * P:(c + 1) * P], ident[0:S, 0:S])
                else:
                    wait_emptied(pe, t, "aT")
                    for k in range(KC):
                        last = mm(ps_out[bank], attT[:, k, :], w["Wo"][:, k, :], k, KC)
                last.then_inc(s_job[bank], 1)

            def turn(t):
                if t.within(B):
                    for what in ("k0", "k1", "v1", "v2"):
                        wait_emptied(pe, t + -1, what)
                for n in range(PAIRS):
                    todo = list(jobs(t, n))
                    pt, pn = (t, n - 2) if n >= 2 else (t + -1, n + PAIRS - 2)
                    g = PAIRS * pt.i + pn
                    for h in range(2):
                        if pt.within(B):
                            if h == 0:
                                pe.wait_ge(s_p, g + 3)
                            if not isinstance(g, int) or g + h > 0:
                                pe.wait_ge(s_t_sb, 2 * g + h)
                            for c in range(CH):
                                last = nc.tensor.transpose(ps_pT[:, c, :], prob[:, pt.parity, 2 * pn + h, c * STEP:c * STEP + R],
                                                           ident[0:S, 0:S])
                            last.then_inc(s_t, 1)
                        if t.within(B):
                            if h == 0:
                                pe.wait_ge(s_p, PAIRS * t.i + (n + 1))
                                if n == 0:
                                    pe.wait_ge(s_qh, t.i + 1)
                            head = 2 * n + h
                            last = mm(ps_s[0:S, n % 2, h, 0:L], q_heads[:, t.parity, head // HC, head % HC, :],
                                      kT[:, t.parity, head // HC, :], 0, 1)
                            if h == 1:
                                last.then_inc(s_s, 1)
                    for k, what, b in todo[:1]:
                        fill(t, k, what, b)
                    if pt.within(B):
                        pe.wait_ge(s_t_sb, 2 * g + 2)
                        if pn == 0 and (not isinstance(pt.i, int) or pt.i > 0):
                            pe.wait_ge(s_att, pt.i)
                        for h in range(2):
                            for c in range(CH):
                                r = R if c == CH - 1 else STEP
                                last = mm(ps_sum[:, 2 * pn + h, :], probT[0:r, h, c, :],
                                          vals[0:r, pt.parity, c, 2 * pn + h, :], c, CH)
                        last.then_inc(s_pv, 1)
                    for k, what, b in todo[1:]:
                        fill(t, k, what, b)

            turns(pe, turn, -1, 3, B - 1, B + 1)

        finish_norm(nc, m, block, keep, s_stats)


QMAX = 2.0 ** 15 - 1.0


def global_scale(nc, m, block, maxima, n_sem, sem_done, parts, scale, inverse, tag):
    top = m.sb(f"{tag}_top", [parts, 1])
    all_top = m.sb(f"{tag}_all_top", [parts, 1])
    s_top, s_all, s_scale, s_inv = (m.sem(f"{tag}_{n}") for n in ("top", "all_top", "scaled", "inverted"))

    @block.vector
    def _(dve):
        dve.wait_ge(sem_done, n_sem)
        nc.vector.reduce_max(top[:], maxima, AX.X).then_inc(s_top, 1)
        dve.wait_ge(s_all, 1)
        nc.vector.tensor_scalar(scale, all_top[:], 1.0 / QMAX, TINY, ALU.mult, ALU.max).then_inc(s_scale, 1)
        dve.wait_ge(s_scale, 1)
        nc.vector.reciprocal(inverse, scale).then_inc(s_inv, 1)
        dve.wait_ge(s_inv, 1)

    @block.gpsimd
    def _(pool):
        pool.wait_ge(s_top, 1)
        nc.gpsimd.partition_all_reduce(all_top[:], top[:], parts, bass.bass_isa.ReduceOp.max).then_inc(s_all, 1)


def quantised_ffn(nc, io, keep):
    B, S, D = io["x"].shape
    I = io["L1_ffn_w_up"].shape[0]
    BLOCK = 32
    KC, IC = D // P, I // P
    G = 4
    GROUPS = B // G
    N = G * S
    y_nat, mean, rstd = keep["y"], keep["mean"], keep["rstd"]
    up_rows = nc.dram_tensor("ffn_up", (GROUPS, P, IC, N), F32, kind="Internal").ap()
    with ExitStack() as outer:
        o = Names(nc, outer, "ffn")
        ident = o.sb("ident", [P, P])
        w_inT = o.sb("w_inT", [P, 2, KC, I])
        w_dT = o.sb("w_dT", [P, IC, D])
        scales = o.sb("scales", [P, 10])
        gate = o.sb("gate", [P, GROUPS, IC, N])
        x_scale, x_inv = scales[0:S, 0:1], scales[0:S, 1:2]
        (u_scale, u_inv), (g_scale, g_inv), (a_scale, a_inv), (o_scale, o_inv) = (
            (scales[:, 2 * n:2 * n + 1], scales[:, 2 * n + 1:2 * n + 2]) for n in range(1, 5))

        with ExitStack() as ctx:
            m = Names(nc, ctx, "ffw")
            w_in = m.sb("w_in", [P, 2, IC, D])
            w_d = m.sb("w_d", [P, KC, I])
            flat = [w_in[:, 0].rearrange("p c d -> p (c d)"), w_in[:, 1].rearrange("p c d -> p (c d)"),
                    w_d[:].rearrange("p c d -> p (c d)")]
            NB = I * D // P // BLOCK
            top = m.sb("top", [P, 3, NB])
            step_ = m.sb("step", [P, 3, NB])
            inv = m.sb("inv", [P, 3, NB])
            row_top = m.sb("row_top", [S, B])
            ps = m.ps("ps", [P, 4, 512])
            s_w, s_const, s_q, s_t, s_t_sb = m.sem("weights"), m.sem("constants"), m.sem("quantised"), m.sem("transposed"), m.sem("stored")
            s_wq = m.sem("weights_ready")
            s_x, s_top = m.sem("rows_normalised"), m.sem("row_maxima")
            block = ctx.enter_context(nc.Block())

            @block.sync
            def _(sp):
                sp.dma_start(w_in[:, 0], io["L1_ffn_w_up"].rearrange("(c p) d -> p c d", p=P)).then_inc(s_w, 16)
                sp.dma_start(w_in[:, 1], io["L1_ffn_w_gate"].rearrange("(c p) d -> p c d", p=P)).then_inc(s_w, 16)
                sp.dma_start(w_d[:], io["L1_ffn_w_down"].rearrange("(c p) d -> p c d", p=P)).then_inc(s_w, 16)

            @block.gpsimd
            def _(pool):
                nc.gpsimd.memset(ident[:], 1.0).then_inc(s_const, 1)
                pool.wait_ge(s_const, 1)
                nc.gpsimd.affine_select(out=ident[:], in_=ident[:], pattern=[[1, P]], compare_op=ALU.is_equal,
                                        fill=0.0, base=0, channel_multiplier=-1).then_inc(s_const, 1)

            @block.vector
            def _(dve):
                def norm(t):
                    nc.vector.tensor_scalar(at(y_nat, t.i), at(y_nat, t.i), mean[:, bass.ds(t.i, 1)],
                                            rstd[:, bass.ds(t.i, 1)], ALU.subtract, ALU.mult).then_inc(s_x, 1)

                def largest(t):
                    dve.wait_ge(s_x, t.i + 1)
                    nc.vector.tensor_reduce(row_top[:, bass.ds(t.i, 1)], at(y_nat, t.i), AX.X, ALU.max,
                                            apply_absolute_value=True).then_inc(s_top, 1)

                def turn(t):
                    if t.within(B):
                        norm(t)
                    if (t + -1).within(B):
                        largest(t + -1)

                turns(dve, turn, 0, 2, B, B + 1)
                dve.wait_ge(s_w, 48)
                q = Chain(dve, s_q, 15)
                q.start(0)
                for n in range(3):
                    blocks = flat[n].rearrange("p (b k) -> p b k", k=BLOCK)
                    wide = lambda x: x[:, n].unsqueeze(2).to_broadcast([P, NB, BLOCK])
                    q(nc.vector.tensor_reduce(top[:, n], blocks, AX.X, ALU.max, apply_absolute_value=True))
                    q(nc.vector.tensor_scalar(step_[:, n], top[:, n], 1.0 / 7.0, TINY, ALU.mult, ALU.max))
                    q(nc.vector.reciprocal(inv[:, n], step_[:, n]))
                    q(nc.vector.tensor_tensor(blocks, blocks, wide(inv), ALU.mult))
                    q(nc.vector.tensor_scalar(blocks, blocks, ROUND, ROUND, ALU.add, ALU.subtract))
                    nc.vector.tensor_tensor(blocks, blocks, wide(step_), ALU.mult).then_inc(s_wq, 1)

            def transposes():
                for n in range(2):
                    for k in range(KC):
                        for c0 in range(0, IC, 4):
                            cs = range(c0, min(c0 + 4, IC))
                            yield n, [w_in[:, n, c, k * P:(k + 1) * P] for c in cs], w_inT[:, n, k, c0 * P:(cs[-1] + 1) * P]
                for c in range(0, IC, 2):
                    yield 2, [w_d[:, k, (c + e) * P:(c + e + 1) * P] for e in range(2) for k in range(KC)], \
                        w_dT[:, c:c + 2, :].rearrange("p e d -> p (e d)")

            @block.tensor
            def _(pe):
                pe.wait_ge(s_const, 2)
                for i, (n, tiles, _) in enumerate(transposes()):
                    pe.wait_ge(s_wq, n + 1)
                    if i >= 4:
                        pe.wait_ge(s_t_sb, i - 3)
                    for e, tile in enumerate(tiles):
                        last = nc.tensor.transpose(ps[:, i % 4, e * P:(e + 1) * P], tile, ident[:])
                    last.then_inc(s_t, 1)

            @block.scalar
            def _(act):
                for i, (n, tiles, out) in enumerate(transposes()):
                    act.wait_ge(s_t, i + 1)
                    nc.scalar.copy(out, ps[:, i % 4, 0:len(tiles) * P]).then_inc(s_t_sb, 1)

            global_scale(nc, m, block, row_top[:], B, s_top, S, x_scale, x_inv, "x")

        with ExitStack() as ctx:
            m = Names(nc, ctx, "ffp")
            xr = m.sb("xr", [S, G, D])
            xq = m.sb("xq", [S, 2, G, D])
            xqT = m.sb("xqT", [P, 2, KC, N])
            up = m.sb("up", [P, 2, IC, N])
            tops = m.sb("tops", [P, 2, GROUPS, IC])
            ps_x = m.ps("ps_x", [P, 2, 512])
            ps_h = m.ps("ps_h", [P, 4, 512])
            s_r, s_q, s_t, s_t_sb = m.sem("rounded"), m.sem("quantised"), m.sem("transposed"), m.sem("xT_stored")
            s_h, s_top, s_h_sb = m.sem("hidden"), m.sem("maxima"), m.sem("hidden_stored")
            s_up = [m.sem(f"up{v}_in_dram") for v in range(2)]
            block = ctx.enter_context(nc.Block())
            NH = 2 * IC

            @block.vector
            def _(dve):
                def quantise(t):
                    rows = y_nat[:, bass.ds(t.i * G, G), :]
                    if not isinstance(t.i, int) or t.i > 0:
                        dve.wait_ge(s_q, t.i)
                    nc.vector.tensor_scalar(xr[:], rows, x_inv, ROUND, ALU.mult, ALU.add).then_inc(s_r, 1)
                    dve.wait_ge(s_r, t.i + 1)
                    if not isinstance(t.i, int) or t.i > 1:
                        dve.wait_ge(s_t, KC * (t.i - 1))
                    nc.vector.tensor_scalar(xq[:, t.parity], xr[:], ROUND, x_scale, ALU.subtract, ALU.mult).then_inc(s_q, 1)

                def turn(t):
                    if (t + 1).within(GROUPS):
                        quantise(t + 1)
                    if t.within(GROUPS):
                        for n in range(NH):
                            k, c = n // IC, n % IC
                            dve.wait_ge(s_h_sb, NH * t.i + (n + 1))
                            nc.vector.tensor_reduce(at(tops[:, k], t.i)[:, c:c + 1], ps_h[:, n % 4, 0:N], AX.X, ALU.max,
                                                    apply_absolute_value=True).then_inc(s_top, 1)

                turns(dve, turn, -1, 1, GROUPS - 1, GROUPS)

            @block.scalar
            def _(act):
                def turn(t):
                    if (t + 1).within(GROUPS):
                        for c in range(KC):
                            act.wait_ge(s_t, KC * (t.i + 1) + (c + 1))
                            nc.scalar.copy(xqT[:, (t + 1).parity, c, :], ps_x[:, c, 0:N]).then_inc(s_t_sb, 1)
                    if t.within(GROUPS):
                        for n in range(NH):
                            k, c = n // IC, n % IC
                            act.wait_ge(s_h, NH * t.i + (n + 1))
                            if n == 0 and (not isinstance(t.i, int) or t.i > 1):
                                act.wait_ge(s_up[t.parity], 16 * t.half)
                            out = up[:, t.parity, c, :] if k == 0 else gate[:, bass.ds(t.i, 1), c, :].rearrange("p a n -> p (a n)")
                            nc.scalar.copy(out, ps_h[:, n % 4, 0:N]).then_inc(s_h_sb, 1)

                turns(act, turn, -1, 1, GROUPS - 1, GROUPS)

            @block.sync
            def _(sp):
                def turn(t):
                    sp.wait_ge(s_h_sb, NH * t.i + IC)
                    sp.dma_start(up_rows[bass.ds(t.i, 1)].rearrange("g p c n -> p (g c) n"), up[:, t.parity]).then_inc(s_up[t.parity], 16)

                turns(sp, turn, 0, 0, GROUPS, GROUPS)
                for v in range(2):
                    sp.wait_ge(s_up[v], 16 * GROUPS // 2)

            @block.tensor
            def _(pe):
                def turn(t):
                    nxt = t + 1
                    if nxt.within(GROUPS):
                        pe.wait_ge(s_q, nxt.i + 1)
                        if not isinstance(nxt.i, int) or nxt.i > 0:
                            pe.wait_ge(s_t_sb, KC * nxt.i)
                        for c in range(KC):
                            for q in range(G):
                                last = nc.tensor.transpose(ps_x[:, c, q * S:(q + 1) * S], xq[:, nxt.parity, q, c * P:(c + 1) * P],
                                                           ident[0:S, 0:S])
                            last.then_inc(s_t, 1)
                    if t.within(GROUPS):
                        pe.wait_ge(s_t_sb, KC * t.i + KC)
                        for n in range(NH):
                            k, c = n // IC, n % IC
                            if not isinstance(t.i, int) or NH * t.i + n >= 4:
                                pe.wait_ge(s_top, (t.i - 1) * NH + (n + NH - 3))
                            for j in range(KC):
                                last = nc.tensor.matmul(ps_h[:, n % 4, 0:N], w_inT[:, k, j, c * P:(c + 1) * P],
                                                        xqT[:, t.parity, j, :], start=(j == 0), stop=(j == KC - 1))
                            last.then_inc(s_h, 1)

                turns(pe, turn, -1, 1, GROUPS - 1, GROUPS)

            global_scale(nc, m, block, tops[:, 0].rearrange("p g c -> p (g c)"), NH * GROUPS, s_top, P, u_scale, u_inv, "u")
            global_scale(nc, m, block, tops[:, 1].rearrange("p g c -> p (g c)"), NH * GROUPS, s_top, P, g_scale, g_inv, "g")

        with ExitStack() as ctx:
            m = Names(nc, ctx, "ffs")
            rounded = m.sb("rounded", [P, 2, IC, N])
            gate_q = m.sb("gate_q", [P, 2, IC, N])
            sig = m.sb("sig", [P, 2, IC, N])
            tops = m.sb("tops", [P, GROUPS])
            round_c = m.sb("round_c", [P, 1])
            s_const = m.sem("constants")
            s_r, s_q, s_s, s_sr, s_sq = (m.sem(n) for n in ("rounded", "quantised", "sigmoids", "sigmoids_rounded", "sigmoids_clipped"))
            s_g, s_top = m.sem("gated"), m.sem("maxima")
            block = ctx.enter_context(nc.Block())

            @block.scalar
            def _(act):
                act.wait_ge(s_const, 1)

                def turn(t):
                    nxt, v = t + 1, t.parity
                    if nxt.within(GROUPS):
                        if not isinstance(nxt.i, int) or nxt.i > 1:
                            act.wait_ge(s_q, nxt.i - 1)
                        nc.scalar.activation(rounded[:, nxt.parity], gate[:, bass.ds(nxt.i, 1)].rearrange("p a c n -> p (a c) n"),
                                             ACT.Identity, bias=round_c[:], scale=g_inv).then_inc(s_r, 1)
                    if t.within(GROUPS):
                        act.wait_ge(s_q, t.i + 1)
                        if not isinstance(t.i, int) or t.i > 1:
                            act.wait_ge(s_g, t.i - 1)
                        nc.scalar.activation(sig[:, v], gate_q[:, v], ACT.Sigmoid).then_inc(s_s, 1)

                turns(act, turn, -1, 1, GROUPS - 1, GROUPS)

            @block.vector
            def _(dve):
                nc.vector.memset(round_c[:], ROUND).then_inc(s_const, 1)

                def quantise(t):
                    dve.wait_ge(s_r, t.i + 1)
                    nc.vector.tensor_scalar(gate_q[:, t.parity], rounded[:, t.parity], ROUND, g_scale,
                                            ALU.subtract, ALU.mult).then_inc(s_q, 1)

                def turn(t):
                    v = t.parity
                    if (t + 1).within(GROUPS):
                        quantise(t + 1)
                    if t.within(GROUPS):
                        here = gate[:, bass.ds(t.i, 1)].rearrange("p a c n -> p (a c) n")
                        dve.wait_ge(s_s, t.i + 1)
                        nc.vector.tensor_scalar(sig[:, v], sig[:, v], 65536.0, ROUND, ALU.mult, ALU.add).then_inc(s_sr, 1)
                        dve.wait_ge(s_sr, t.i + 1)
                        nc.vector.tensor_scalar(sig[:, v], sig[:, v], ROUND, 65535.0, ALU.subtract, ALU.min).then_inc(s_sq, 1)
                        dve.wait_ge(s_sq, t.i + 1)
                        nc.vector.scalar_tensor_tensor(out=here, in0=sig[:, v], scalar=1.0 / 65536.0, in1=gate_q[:, v],
                                                       op0=ALU.mult, op1=ALU.mult).then_inc(s_g, 1)
                        dve.wait_ge(s_g, t.i + 1)
                        nc.vector.tensor_reduce(tops[:, bass.ds(t.i, 1)], here, AX.XY, ALU.max,
                                                apply_absolute_value=True).then_inc(s_top, 1)

                turns(dve, turn, -1, 1, GROUPS - 1, GROUPS)

            global_scale(nc, m, block, tops[:], GROUPS, s_top, P, a_scale, a_inv, "a")

        with ExitStack() as ctx:
            m = Names(nc, ctx, "ffo")
            up = m.sb("up", [P, 2, IC, N])
            gr = m.sb("gr", [P, 2, IC, N])
            tops = m.sb("tops", [P, GROUPS])
            round_c = m.sb("round_c", [P, 1])
            s_const, s_ur, s_gr, s_uq, s_gq, s_o, s_top = (m.sem(n) for n in (
                "constants", "up_rounded", "gate_rounded", "up_quantised", "gate_quantised", "multiplied", "maxima"))
            s_up = [m.sem(f"up{v}_loaded") for v in range(2)]
            block = ctx.enter_context(nc.Block())

            @block.sync
            def _(sp):
                def turn(t):
                    if not isinstance(t.i, int) or t.i > 1:
                        sp.wait_ge(s_o, t.i - 1)
                    sp.dma_start(up[:, t.parity], up_rows[bass.ds(t.i, 1)].rearrange("g p c n -> p (g c) n")).then_inc(s_up[t.parity], 16)

                turns(sp, turn, 0, 2, GROUPS, GROUPS)

            @block.scalar
            def _(act):
                act.wait_ge(s_const, 1)

                def turn(t):
                    v = t.parity
                    if not isinstance(t.i, int) or t.i > 1:
                        act.wait_ge(s_o, t.i - 1)
                    nc.scalar.activation(gr[:, v], gate[:, bass.ds(t.i, 1)].rearrange("p a c n -> p (a c) n"),
                                         ACT.Identity, bias=round_c[:], scale=a_inv).then_inc(s_gr, 1)
                    act.wait_ge(s_up[v], 16 * t.half + 16)
                    nc.scalar.activation(up[:, v], up[:, v], ACT.Identity, bias=round_c[:], scale=u_inv).then_inc(s_ur, 1)

                turns(act, turn, 0, 2, GROUPS, GROUPS)

            @block.vector
            def _(dve):
                nc.vector.memset(round_c[:], ROUND).then_inc(s_const, 1)

                def turn(t):
                    v = t.parity
                    here = gate[:, bass.ds(t.i, 1)].rearrange("p a c n -> p (a c) n")
                    dve.wait_ge(s_gr, t.i + 1)
                    nc.vector.tensor_scalar(gr[:, v], gr[:, v], ROUND, a_scale, ALU.subtract, ALU.mult).then_inc(s_gq, 1)
                    dve.wait_ge(s_ur, t.i + 1)
                    nc.vector.tensor_scalar(up[:, v], up[:, v], ROUND, u_scale, ALU.subtract, ALU.mult).then_inc(s_uq, 1)
                    dve.wait_ge(s_gq, t.i + 1)
                    dve.wait_ge(s_uq, t.i + 1)
                    nc.vector.tensor_tensor(here, gr[:, v], up[:, v], ALU.mult).then_inc(s_o, 1)
                    dve.wait_ge(s_o, t.i + 1)
                    nc.vector.tensor_reduce(tops[:, bass.ds(t.i, 1)], here, AX.XY, ALU.max,
                                            apply_absolute_value=True).then_inc(s_top, 1)

                turns(dve, turn, 0, 0, GROUPS, GROUPS)

            global_scale(nc, m, block, tops[:], GROUPS, s_top, P, o_scale, o_inv, "o")

        with ExitStack() as ctx:
            m = Names(nc, ctx, "ffd")
            orr = m.sb("rounded", [P, 2, IC, N])
            oq = m.sb("oq", [P, 2, IC, N])
            round_c = m.sb("round_c", [P, 1])
            ps_y = m.ps("ps_y", [P, 4, 512])
            s_const, s_r, s_q, s_y, s_sum, s_stats = (m.sem(n) for n in (
                "constants", "rounded", "quantised", "summed", "rows_added", "stats_ready"))
            block = ctx.enter_context(nc.Block())

            @block.scalar
            def _(act):
                act.wait_ge(s_const, 1)

                def turn(t):
                    if not isinstance(t.i, int) or t.i > 1:
                        act.wait_ge(s_q, t.i - 1)
                    nc.scalar.activation(orr[:, t.parity], gate[:, bass.ds(t.i, 1)].rearrange("p a c n -> p (a c) n"),
                                         ACT.Identity, bias=round_c[:], scale=o_inv).then_inc(s_r, 1)

                turns(act, turn, 0, 2, GROUPS, GROUPS)

            @block.vector
            def _(dve):
                nc.vector.memset(round_c[:], ROUND).then_inc(s_const, 1)

                def quantise(t):
                    dve.wait_ge(s_r, t.i + 1)
                    if not isinstance(t.i, int) or t.i > 1:
                        dve.wait_ge(s_y, G * (t.i - 1))
                    nc.vector.tensor_scalar(oq[:, t.parity], orr[:, t.parity], ROUND, o_scale,
                                            ALU.subtract, ALU.mult).then_inc(s_q, 1)

                def turn(t):
                    if (t + 1).within(GROUPS):
                        quantise(t + 1)
                    if t.within(GROUPS):
                        for q in range(G):
                            b = t.i * G + q
                            dve.wait_ge(s_y, b + 1)
                            nc.vector.tensor_tensor(at(y_nat, b), ps_y[0:S, q, 0:D], at(y_nat, b), ALU.add).then_inc(s_sum, 1)
                            dve.wait_ge(s_sum, b + 1)
                            nc.vector.bn_stats(at(keep["stats"], b), at(y_nat, b)).then_inc(s_stats, 1)

                turns(dve, turn, -1, 1, GROUPS - 1, GROUPS)

            @block.tensor
            def _(pe):
                def turn(t):
                    pe.wait_ge(s_q, t.i + 1)
                    for q in range(G):
                        if not isinstance(t.i, int) or t.i > 0:
                            pe.wait_ge(s_sum, (t.i - 1) * G + (q + 1))
                        for c in range(IC):
                            last = nc.tensor.matmul(ps_y[0:S, q, 0:D], oq[:, t.parity, c, q * S:(q + 1) * S], w_dT[:, c, :],
                                                    start=(c == 0), stop=(c == IC - 1))
                        last.then_inc(s_y, 1)

                turns(pe, turn, 0, 2, GROUPS, GROUPS)

            finish_norm(nc, m, block, keep, s_stats)


def bass_decoder(nc, io, out):
    B, S, D = io["x"].shape
    with ExitStack() as ctx:
        def kept(name, shape):
            return ctx.enter_context(nc.sbuf_tensor(name, shape, F32))

        keep = {
            "y": kept("y", [S, B, D]),
            "stats": kept("stats", [S, B, 6]),
            "mean": kept("mean", [S, B]),
            "rstd": kept("rstd", [S, B]),
        }
        linear_attention(nc, io, keep)
        mutual_attention(nc, io, keep)
        routed_ffn(nc, io, keep)
        causal_heads(nc, io, keep)
        relative_cross(nc, io, keep)
        quantised_ffn(nc, io, keep)
        store(nc, keep, out)


def store(nc, keep, out):
    S, B, D = keep["y"].shape
    with ExitStack() as ctx:
        m = Names(nc, ctx, "out")
        s_norm, s_out = m.sem("rows_normalised"), m.sem("stored")
        block = ctx.enter_context(nc.Block())
        part = 8

        @block.vector
        def _(dve):
            with dve.Fori(0, B) as b:
                nc.vector.tensor_scalar(at(keep["y"], b), at(keep["y"], b), keep["mean"][:, bass.ds(b, 1)],
                                        keep["rstd"][:, bass.ds(b, 1)], ALU.subtract, ALU.mult).then_inc(s_norm, 1)

        @block.sync
        def _(sp):
            for b in range(0, B, part):
                sp.wait_ge(s_norm, b + part)
                sp.dma_start(out[b:b + part].rearrange("b s d -> s b d"), keep["y"][:, b:b + part, :]).then_inc(s_out, 16)
            sp.wait_ge(s_out, 16 * (B // part))


_TRANSPOSED = {"L0_attn_WvT": "L0_attn_Wv", "L0_xattn_WvT_s": "L0_xattn_Wv_s", "L0_xattn_WvT_c": "L0_xattn_Wv_c",
               "L0_xattn_WgT": "L0_xattn_Wg", "L1_xattn_rel_k_tableT": "L1_xattn_rel_k_table"}
_COLUMNS = ["L0_attn_bq", "L0_attn_bk", "L0_attn_bv"] + [
    "L0_xattn_" + n for n in ("bq_c", "bk_s", "bk_c", "bq_s", "bv_s", "bv_c", "bg")] + [
    "L1_xattn_bq", "L1_xattn_bk"]


def _interpolation(n_in, n_out, chunks):
    import numpy as _np

    pos = (_np.arange(n_out, dtype=_np.float32) + _np.float32(0.5)) * _np.float32(n_in / n_out) - _np.float32(0.5)
    pos = _np.clip(pos, _np.float32(0.0), _np.float32(n_in - 1))
    low = _np.floor(pos).astype(_np.int32)
    high = _np.minimum(low + 1, n_in - 1)
    part = pos - low.astype(_np.float32)
    whole = _np.zeros((n_in, n_out), _np.float32)
    _np.add.at(whole, (low, _np.arange(n_out)), 1 - part)
    _np.add.at(whole, (high, _np.arange(n_out)), part)
    step = n_in // chunks
    rows = n_in - (chunks - 1) * step
    out = _np.zeros((rows, chunks, n_out), _np.float32)
    for c in range(chunks):
        r = rows if c == chunks - 1 else step
        out[:r, c] = whole[c * step:c * step + r]
    return out


def kernel(**inputs):
    import numpy as _np
    import concourse.bacc as _bacc
    from concourse import mybir as _mybir
    from concourse.bass_utils import run_bass_kernel_spmd as _run

    nc = _bacc.Bacc("TRN2", target_bir_lowering=False, num_devices=1)
    a = {n: _np.asarray(v) for n, v in inputs.items()}
    a["xT"] = a["x"].reshape(-1, a["x"].shape[-1]).T
    b1 = a["L0_ffn_b1"]
    a["L0_ffn_b1_cols"] = b1.reshape(b1.shape[0], -1, P).transpose(2, 0, 1)
    a["ctxT"] = a["ctx_1024"].transpose(0, 2, 1)
    a["interp"] = _interpolation(a["ctx_1024"].shape[1], a["x"].shape[1], 3)
    for new, old in _TRANSPOSED.items():
        a[new] = a[old].T
    for name in _COLUMNS:
        a[name + "_cols"] = a[name].reshape(-1, P).T
    arrays, io = {}, {}
    for n, v in a.items():
        v = _np.ascontiguousarray(v)
        arrays[f"in_{n}"] = v
        io[n] = nc.dram_tensor(f"in_{n}", v.shape, _mybir.dt.from_np(v.dtype), kind="ExternalInput").ap()
    out = nc.dram_tensor("out_0", a["x"].shape, _mybir.dt.float32, kind="ExternalOutput").ap()
    bass_decoder(nc, io, out)
    r = _run(nc, [arrays], core_ids=[0])
    return r.results[0]["out_0"]
```

```python
from contextlib import ExitStack

import concourse.bass as bass
from concourse import mybir

F32 = mybir.dt.float32
U32 = mybir.dt.uint32
ALU = mybir.AluOpType
ACT = mybir.ActivationFunctionType
AX = mybir.AxisListType

P = 128
LN_EPS = 1e-5
ROUND = 12582912.0
TINY = 1e-12


class Names:

    def __init__(self, nc, ctx, stage):
        self.nc, self.ctx, self.stage, self.sems = nc, ctx, stage, []
        ctx.callback(self.clear)

    def clear(self):
        if self.sems:
            self.nc.clear_and_free_semaphores(self.sems)
            self.nc.all_engine_barrier()

    def sb(self, name, shape, dt=F32):
        return self.ctx.enter_context(self.nc.sbuf_tensor(f"{self.stage}_{name}", shape, dt))

    def ps(self, name, shape, dt=F32):
        return self.ctx.enter_context(self.nc.psum_tensor(f"{self.stage}_{name}", shape, dt))

    def sem(self, name):
        self.sems.append(self.nc.alloc_semaphore(name=f"{self.stage}_{name}"))
        return self.sems[-1]


class Chain:

    def __init__(self, eng, sem, per):
        self.eng, self.sem, self.per, self.n, self.turn = eng, sem, per, 0, 0

    def start(self, turn):
        self.turn, self.n = turn, 0

    def end(self):
        assert self.n == self.per, (self.n, self.per)

    def __call__(self, instruction):
        self.n += 1
        instruction.then_inc(self.sem, 1)
        self.eng.wait_ge(self.sem, self.turn * self.per + self.n)


def at(x, i):
    v = x[:, bass.ds(i, 1)]
    return v.rearrange("p a b -> p (a b)") if len(v.shape) == 3 else v.rearrange("p a b c -> p (a b) c")


class Turn:

    def __init__(self, i, parity, half):
        self.i, self.parity, self.half = i, parity, half

    def __add__(self, k):
        p = self.parity + k
        return Turn(self.i + k, p % 2, self.half + p // 2)

    def within(self, n):
        return not isinstance(self.i, int) or 0 <= self.i < n


def turns(eng, body, first, loop_from, loop_to, last):
    for i in range(first, loop_from):
        body(Turn(i, i % 2, i // 2))
    with eng.Fori(0, (loop_to - loop_from) // 2) as j:
        for k in range(2):
            i = loop_from + k
            body(Turn(2 * j + i, i % 2, j + i // 2))
    for i in range(loop_to, last):
        body(Turn(i, i % 2, i // 2))


def finish_norm(nc, m, block, keep, s_stats):
    stats, mean, rstd = keep["stats"], keep["mean"], keep["rstd"]
    S, B, _ = stats.shape
    half_sum = m.sb("norm_sum", [S, B])
    diff = m.sb("norm_diff", [S, B])
    spread = m.sb("norm_spread", [S, B])
    var = m.sb("norm_var", [S, B])
    eps = m.sb("norm_eps", [S, 1])
    s_step = m.sem("norm_steps")
    s_log = m.sem("norm_logs")

    @block.vector
    def _(dve):
        step = Chain(dve, s_step, 6)
        step.start(0)
        dve.wait_ge(s_stats, B)
        nc.vector.memset(eps[:], LN_EPS)
        nc.vector.tensor_tensor(half_sum[:], stats[:, :, 1], stats[:, :, 4], ALU.add)
        nc.vector.tensor_tensor(diff[:], stats[:, :, 1], stats[:, :, 4], ALU.subtract)
        step(nc.vector.tensor_tensor(spread[:], stats[:, :, 2], stats[:, :, 5], ALU.add))
        step(nc.vector.tensor_tensor(diff[:], diff[:], diff[:], ALU.mult))
        step(nc.vector.tensor_scalar(mean[:], half_sum[:], 0.5, None, ALU.mult))
        step(nc.vector.tensor_scalar(diff[:], diff[:], 0.25, None, ALU.mult))
        step(nc.vector.scalar_tensor_tensor(out=var[:], in0=spread[:], scalar=1.0 / keep["y"].shape[2],
                                            in1=diff[:], op0=ALU.mult, op1=ALU.add))
        dve.wait_ge(s_log, 1)
        step(nc.vector.tensor_scalar(var[:], rstd[:], -0.5, None, ALU.mult))

    @block.scalar
    def _(act):
        act.wait_ge(s_step, 5)
        nc.scalar.activation(rstd[:], var[:], ACT.Ln, bias=eps[:]).then_inc(s_log, 1)
        act.wait_ge(s_step, 6)
        nc.scalar.activation(rstd[:], var[:], ACT.Exp).then_inc(s_log, 1)


def linear_attention(nc, io, keep):
    B, S, D = io["x"].shape
    E = io["L0_attn_Wq"].shape[1]
    KC, EC = D // P, E // P
    G = 4
    TURNS = B // G
    N = G * S
    y_nat = keep["y"]
    with ExitStack() as ctx:
        m = Names(nc, ctx, "lin")
        w_q = m.sb("w_q", [P, KC, E])
        w_k = m.sb("w_k", [P, KC, E])
        w_vT = m.sb("w_vT", [P, EC, D])
        w_o = m.sb("w_o", [P, EC, D])
        w_vo = m.sb("w_vo", [P, KC, D])
        bias_cols = m.sb("bias_cols", [P, 3, EC])
        bias_up = m.sb("bias_up", [P, 2, EC])
        bv_wide = m.sb("bv_wide", [P, EC, S])
        b_vo = m.sb("b_vo", [S, D])
        b_o = m.sb("b_o", [S, D])
        causal = m.sb("causal", [S, G, S])
        xT = m.sb("xT", [P, 2, KC, N])
        phi = m.sb("phi", [P, 2, 2, EC, N])
        low = m.sb("low", [P, 2, N])
        expd = m.sb("expd", [P, 2, N])
        values = m.sb("values", [S, G, D + 1])
        scores = m.sb("scores", [S, G, S])
        resid = m.sb("resid", [S, 2, G, D])
        den = m.sb("den", [S, G])
        rden = m.sb("rden", [S, G])
        ps_qk = m.ps("ps_qk", [P, 4, 512])
        ps_v = m.ps("ps_v", [P, 1, 512])
        ps_s = m.ps("ps_s", [P, 512])
        ps_o = m.ps("ps_o", [P, 2, 512])

        s_w = m.sem("weights")
        s_x = m.sem("x_whole")
        s_const = m.sem("constants")
        s_wide = m.sem("bv_widened")
        s_wvo = m.sem("wvo_product")
        s_wvo_sb = m.sem("wvo_stored")
        s_xT = [m.sem(f"xT{u}_loaded") for u in range(2)]
        s_proj = m.sem("qk_projected")
        s_low = m.sem("qk_low")
        s_exp = m.sem("qk_exp")
        s_phi = m.sem("qk_phi")
        s_val = m.sem("values_projected")
        s_val_sb = m.sem("values_stored")
        s_sc = m.sem("scores_ready")
        s_sc_sb = m.sem("scores_masked")
        s_out = m.sem("rows_summed")
        s_y = m.sem("rows_divided")
        s_res = m.sem("residual_ready")
        s_res_free = m.sem("residual_free")
        s_chain = m.sem("dve_chain")
        s_stats = m.sem("stats_ready")
        block = ctx.enter_context(nc.Block())

        @block.sync
        def _(sp):
            sp.dma_start(w_q[:], io["L0_attn_Wq"].rearrange("(c p) e -> p c e", p=P)).then_inc(s_w, 16)
            sp.dma_start(w_k[:], io["L0_attn_Wk"].rearrange("(c p) e -> p c e", p=P)).then_inc(s_w, 16)
            sp.dma_start(w_vT[:], io["L0_attn_WvT"].rearrange("(c p) d -> p c d", p=P)).then_inc(s_w, 16)
            sp.dma_start(w_o[:], io["L0_attn_Wo"].rearrange("(c p) d -> p c d", p=P)).then_inc(s_w, 16)
            sp.dma_start(b_o[:], io["L0_attn_bo"].partition_broadcast(S)).then_inc(s_w, 16)
            for n, name in enumerate(("L0_attn_bq", "L0_attn_bk", "L0_attn_bv")):
                sp.dma_start(bias_cols[:, n, :], io[name + "_cols"]).then_inc(s_w, 16)
            sp.dma_start(y_nat[:], io["x"].rearrange("b s d -> s b d")).then_inc(s_x, 16)
            with sp.Fori(0, TURNS // 2) as j:
                for u in range(2):
                    sp.wait_ge(s_val, 2 * (2 * j + u) + 2)
                    sp.dma_start(xT[:, u], io["xT"].rearrange("(c p) n -> p c n", p=P)[
                        :, :, bass.ds((2 * j + u) * N, N)]).then_inc(s_xT[u], 16)

        @block.gpsimd
        def _(pool):
            nc.gpsimd.memset(causal[:], 1.0).then_inc(s_const, 1)
            nc.gpsimd.memset(values[:, :, D:D + 1], 1.0).then_inc(s_const, 1)
            pool.wait_ge(s_const, 2)
            nc.gpsimd.affine_select(out=causal[:], in_=causal[:], pattern=[[0, G], [1, S]], compare_op=ALU.is_ge,
                                    fill=0.0, base=0, channel_multiplier=-1).then_inc(s_const, 1)
            pool.wait_ge(s_w, 8 * 16)
            pool.wait_ge(s_x, 16)
            with pool.Fori(0, TURNS // 2) as j:
                for u in range(2):
                    pool.wait_ge(s_res_free, 2 * j + u + 1)
                    rows = y_nat[:, bass.ds((2 * j + u) * G, G), :]
                    nc.gpsimd.tensor_tensor(resid[:, u], rows, b_o[:].unsqueeze(1).to_broadcast([S, G, D]),
                                            ALU.add).then_inc(s_res, 1)

        @block.scalar
        def _(act):
            act.wait_ge(s_const, 3)
            with act.Fori(0, TURNS // 2) as j:
                for u in range(2):
                    t = 2 * j + u
                    for n in range(2 * EC):
                        act.wait_ge(s_low, t * 2 * EC + (n + 1))
                        nc.scalar.activation(expd[:, n % 2, :], low[:, n % 2, :], ACT.Exp).then_inc(s_exp, 1)

        @block.tensor
        def _(pe):
            pe.wait_ge(s_w, 8 * 16)
            pe.wait_ge(s_wide, 1)
            for c in range(KC):
                for e in range(EC):
                    nc.tensor.matmul(ps_v[:, 0, c * D:(c + 1) * D], w_vT[:, e, c * P:(c + 1) * P], w_o[:, e, :],
                                     start=(e == 0), stop=(e == EC - 1))
            for e in range(EC):
                last = nc.tensor.matmul(ps_o[0:S, 0, 0:D], bv_wide[:, e, :], w_o[:, e, :],
                                        start=(e == 0), stop=(e == EC - 1))
            last.then_inc(s_wvo, 1)
            pe.wait_ge(s_wvo_sb, 1)
            pe.sem_inc(s_val, 4)

            def project(t, chunks):
                u = t.parity
                for n in chunks:
                    if n == 0:
                        pe.wait_ge(s_xT[u], t.half * 16 + 16)
                    w, e = (w_q, w_k)[n // EC], n % EC
                    pe.wait_ge(s_phi, t.i * (2 * EC) + (n + 1))
                    for c in range(KC):
                        last = nc.tensor.matmul(ps_qk[:, n % 4, 0:N],
                                                w[:, c, e * P:(e + 1) * P], xT[:, u, c, :],
                                                start=(c == 0), stop=(c == KC - 1))
                    last.then_inc(s_proj, 1)

            def values_and_scores(t):
                u = t.parity
                for h in range(2):
                    if h:
                        pe.wait_ge(s_val_sb, 2 * t.i + 1)
                    for i in range(2):
                        q = 2 * h + i
                        for c in range(KC):
                            last = nc.tensor.matmul(ps_v[0:S, 0, i * D:(i + 1) * D],
                                                    xT[:, u, c, q * S:(q + 1) * S], w_vo[:, c, :],
                                                    start=(c == 0), stop=(c == KC - 1))
                    last.then_inc(s_val, 1)
                pe.wait_ge(s_phi, t.i * (2 * EC) + (2 * EC + 4))
                for q in range(G):
                    for e in range(EC):
                        last = nc.tensor.matmul(ps_s[0:S, q * S:(q + 1) * S],
                                                phi[:, u, 1, e, q * S:(q + 1) * S],
                                                phi[:, u, 0, e, q * S:(q + 1) * S],
                                                start=(e == 0), stop=(e == EC - 1))
                last.then_inc(s_sc, 1)

            def sums(t, rows):
                for q in rows:
                    if q == 0:
                        pe.wait_ge(s_sc_sb, t.i + 1)
                        pe.wait_ge(s_val_sb, 2 * t.i + 2)
                    pe.wait_ge(s_y, t.i * G + (q + 1))
                    nc.tensor.matmul(ps_o[0:S, q % 2, 0:D + 1], scores[:, q, :], values[:, q, :],
                                     start=True, stop=True).then_inc(s_out, 1)

            def turn(t):
                b, nxt = t, t + 1
                if b.within(TURNS):
                    values_and_scores(b)
                for half in range(2):
                    if nxt.within(TURNS):
                        project(nxt, range(half * EC, (half + 1) * EC))
                    if b.within(TURNS):
                        sums(b, range(half * 2, half * 2 + 2))

            turns(pe, turn, -1, 1, TURNS - 1, TURNS)

        @block.vector
        def _(dve):
            chain = Chain(dve, s_chain, 2 * G)
            dve.wait_ge(s_w, 8 * 16)
            nc.vector.tensor_scalar(bias_up[:], bias_cols[:, 0:2, :], 1.0, None, ALU.add)
            nc.vector.tensor_copy(bv_wide[:], bias_cols[:, 2, :].unsqueeze(2).to_broadcast([P, EC, S])).then_inc(s_wide, 1)
            dve.wait_ge(s_wvo, 1)
            nc.vector.tensor_copy(w_vo[:], ps_v[:, 0, :].rearrange("p (c d) -> p c d", c=KC))
            nc.vector.tensor_copy(b_vo[:], ps_o[0:S, 0, 0:D]).then_inc(s_wvo_sb, 1)
            dve.wait_ge(s_wvo_sb, 1)
            dve.wait_ge(s_const, 3)
            dve.sem_inc(s_phi, 4)
            dve.sem_inc(s_y, 2)
            dve.sem_inc(s_res_free, 2)

            def lower(t, n):
                dve.wait_ge(s_proj, t.i * (2 * EC) + (n + 1))
                nc.vector.tensor_scalar(low[:, n % 2, :], ps_qk[:, n % 4, 0:N],
                                        bias_cols[:, n // EC, n % EC:n % EC + 1], 0.0,
                                        ALU.add, ALU.min).then_inc(s_low, 1)

            def upper(t, n):
                dve.wait_ge(s_exp, t.i * (2 * EC) + (n + 1))
                nc.vector.scalar_tensor_tensor(
                    out=phi[:, t.parity, n // EC, n % EC, :], in0=ps_qk[:, n % 4, 0:N],
                    scalar=bias_up[:, n // EC, n % EC:n % EC + 1], in1=expd[:, n % 2, :],
                    op0=ALU.add, op1=ALU.max).then_inc(s_phi, 1)

            def features(t, chunks):
                for n in chunks:
                    lower(t, n)
                    if n:
                        upper(t, n - 1)
                if n == 2 * EC - 1:
                    upper(t, n)

            def store_values(t):
                for h in range(2):
                    dve.wait_ge(s_val, 2 * t.i + (h + 5))
                    nc.vector.tensor_tensor(
                        values[:, 2 * h:2 * h + 2, 0:D], ps_v[0:S, 0, :].rearrange("p (q d) -> p q d", q=2),
                        b_vo[:].unsqueeze(1).to_broadcast([S, 2, D]), ALU.add).then_inc(s_val_sb, 1)
                dve.wait_ge(s_sc, t.i + 1)
                nc.vector.tensor_tensor(scores[:], ps_s[0:S, 0:N].rearrange("p (q s) -> p q s", q=G),
                                        causal[:], ALU.mult).then_inc(s_sc_sb, 1)
                dve.wait_ge(s_res, t.i + 1)

            def divide(t, rows):
                for q in rows:
                    b = t.i * G + q
                    dve.wait_ge(s_out, b + 1)
                    chain(nc.vector.tensor_scalar(den[:, q:q + 1], ps_o[0:S, q % 2, D:D + 1], 1e-6, None, ALU.add))
                    chain(nc.vector.reciprocal(rden[:, q:q + 1], den[:, q:q + 1]))
                    nc.vector.scalar_tensor_tensor(out=at(y_nat, b), in0=ps_o[0:S, q % 2, 0:D],
                                                   scalar=rden[:, q:q + 1], in1=resid[:, t.parity, q, :],
                                                   op0=ALU.mult, op1=ALU.add).then_inc(s_y, 1)

            def turn(t):
                prev, b, nxt = t + -1, t, t + 1
                if b.within(TURNS):
                    chain.start(b.i)
                    store_values(b)
                if prev.within(TURNS):
                    for q in range(G):
                        n = prev.i * G + q
                        nc.vector.bn_stats(at(keep["stats"], n), at(y_nat, n)).then_inc(s_stats, 1)
                for half in range(2):
                    if nxt.within(TURNS):
                        features(nxt, range(half * EC, (half + 1) * EC))
                    if b.within(TURNS):
                        divide(b, range(half * 2, half * 2 + 2))
                if b.within(TURNS):
                    dve.wait_ge(s_y, b.i * G + (G + 2))
                    dve.sem_inc(s_res_free, 1)
                    chain.end()

            turns(dve, turn, -1, 1, TURNS - 1, TURNS + 1)

        finish_norm(nc, m, block, keep, s_stats)


def mutual_attention(nc, io, keep):
    B, S, D = io["x"].shape
    L = io["ctx_1024"].shape[1]
    KC = D // P
    CH = 3
    STEP = L // CH
    R = L - (CH - 1) * STEP
    SCALE = float(D) ** -0.5
    y_nat, mean, rstd = keep["y"], keep["mean"], keep["rstd"]
    with ExitStack() as ctx:
        m = Names(nc, ctx, "mut")
        w = {n: m.sb(n, [P, KC, D]) for n in ("Wq_c", "Wk_s", "Wk_c", "Wq_s", "WvT_s", "WvT_c")}
        w_gT = m.sb("WgT", [P, 2 * KC, D])
        cols = {n: m.sb(n + "_col", [P, KC]) for n in ("bq_c", "bk_s", "bk_c", "bq_s", "bv_s", "bv_c", "bg")}
        interp = m.sb("interp", [R, CH, S])
        ident = m.sb("ident", [P, P])
        sel_c = m.sb("sel_c", [2, L])
        sel_r = m.sb("sel_r", [2, R])
        a_w = m.sb("a_w", [P, 2, KC, D])
        a_b = m.sb("a_b", [P, 2, KC])
        row_w = m.sb("row_w", [P, KC, 2])
        prod = m.sb("prod", [P, KC, 2])
        ones = m.sb("ones", [P, 2])
        row_b = m.sb("row_b", [2, 1])
        bv = m.sb("bv", [P, 2 * KC])
        neg_bg = m.sb("neg_bg", [P, KC])
        ctx_nat = m.sb("ctx_nat", [R, 2, CH, D])
        ctx_T = m.sb("ctx_T", [P, 2, KC, L])
        xn = m.sb("xn", [S, 2, D])
        xT = m.sb("xT", [P, KC, S])
        u = m.sb("u", [P, 2, KC, S])
        rows = m.sb("rows", [2, S])
        mx1 = m.sb("mx1", [S, 1])
        nmx1 = m.sb("nmx1", [S, 1])
        sum1 = m.sb("sum1", [S, 1])
        rec1 = m.sb("rec1", [S, 1])
        p1 = m.sb("p1", [S, L])
        p1n = m.sb("p1n", [S, L])
        p1T = m.sb("p1T", [R, CH, S])
        mx2 = m.sb("mx2", [R, CH])
        nmx2 = m.sb("nmx2", [R, CH])
        sum2 = m.sb("sum2", [R, CH])
        rec2 = m.sb("rec2", [R, CH])
        p2 = m.sb("p2", [R, CH, S])
        p2n = m.sb("p2n", [R, CH, S])
        tT = m.sb("tT", [S, S])
        yT = m.sb("yT", [P, KC, S])
        zT = m.sb("zT", [P, KC, S])
        cs = m.sb("cs", [P, 2 * KC, S])
        gate_e = m.sb("gate_e", [P, KC, S])
        gate = m.sb("gate", [P, KC, S])
        diff = m.sb("diff", [P, KC, S])
        mix = m.sb("mix", [P, KC, S])
        mixed = m.sb("mixed", [P, KC, S])
        ps_yy = m.ps("ps_yy", [P, 512])
        ps_p = m.ps("ps_p", [P, 512])
        ps_tz = m.ps("ps_tz", [P, 512])
        ps_u = m.ps("ps_u", [P, 512])
        ps_s1 = m.ps("ps_s1", [P, 512])
        ps_s2 = m.ps("ps_s2", [P, 512])
        ps_cs = m.ps("ps_cs", [P, 512])
        ps_g = m.ps("ps_g", [P, 512])
        ps_xT = ps_yy[:, 0:KC * S].rearrange("p (c s) -> p c s", c=KC)
        ps_y = ps_yy[:, 0:KC * S].rearrange("p (c s) -> p c s", c=KC)
        ps_p1T = ps_p[0:R, 0:CH * S].rearrange("p (c s) -> p c s", c=CH)
        ps_rows = ps_s2[0:2, 384:384 + S]
        ps_t = ps_tz[0:S, 0:S]
        ps_z = ps_tz[:, 256:256 + KC * S].rearrange("p (c s) -> p c s", c=KC)
        ps_uv = ps_u[:, 0:2 * KC * S].rearrange("p (n c s) -> p n c s", n=2, c=KC)
        ps_sub = ps_s2[0:R, 0:CH * S].rearrange("p (c s) -> p c s", c=CH)
        ps_csv = ps_cs[:, 0:2 * KC * S].rearrange("p (c s) -> p c s", c=2 * KC)
        ps_gate = ps_g[:, 0:KC * S].rearrange("p (c s) -> p c s", c=KC)
        ps_out = ps_yy[0:S, 0:D]

        s_w = m.sem("weights")
        s_const = m.sem("constants")
        s_mul = m.sem("weights_multiplied")
        s_mul_sb = m.sem("products_stored")
        s_prod = m.sem("bias_products")
        s_ctx = [m.sem(f"context{v}_loaded") for v in range(2)]
        s_xn = m.sem("rows_normalised")
        s_xn_kept = m.sem("rows_normalised_in_place")
        s_xT = m.sem("xT_transposed")
        s_xT_sb = m.sem("xT_stored")
        s_u = m.sem("u_projected")
        s_u_sb = m.sem("u_stored")
        s_rows = m.sem("row_terms")
        s_rows_sb = m.sem("row_terms_stored")
        s_s1 = m.sem("scores1")
        s_mx1 = m.sem("max1")
        s_e1 = m.sem("exp1")
        s_r1 = m.sem("sum1_inverted")
        s_p1n = m.sem("weights1")
        s_p1T = m.sem("weights1_transposed")
        s_p1T_sb = m.sem("weights1T_stored")
        s_s2 = m.sem("scores2")
        s_mx2 = m.sem("max2")
        s_e2 = m.sem("exp2")
        s_r2 = m.sem("sum2_inverted")
        s_p2n = m.sem("weights2")
        s_t = m.sem("t_ready")
        s_t_sb = m.sem("t_stored")
        s_y = m.sem("y_ready")
        s_y_sb = m.sem("y_stored")
        s_z = m.sem("z_ready")
        s_z_sb = m.sem("z_stored")
        s_cs = m.sem("cs_ready")
        s_cs_sb = m.sem("cs_stored")
        s_g = m.sem("gate_logits")
        s_ge = m.sem("gate_exp")
        s_gd = m.sem("gate_denominator")
        s_gate = m.sem("gate_ready")
        s_diff = m.sem("difference")
        s_mix = m.sem("mix_scaled")
        s_mixed = m.sem("mixed")
        s_out = m.sem("out_transposed")
        s_sum = m.sem("rows_added")
        s_stats = m.sem("stats_ready")
        block = ctx.enter_context(nc.Block())
        NW = len(w) + 1 + len(cols) + 1

        @block.sync
        def _(sp):
            for n, tile in w.items():
                sp.dma_start(tile[:], io["L0_xattn_" + n].rearrange("(c p) d -> p c d", p=P)).then_inc(s_w, 16)
            sp.dma_start(w_gT[:], io["L0_xattn_WgT"].rearrange("(c p) d -> p c d", p=P)).then_inc(s_w, 16)
            for n, tile in cols.items():
                sp.dma_start(tile[:], io[f"L0_xattn_{n}_cols"]).then_inc(s_w, 16)
            sp.dma_start(interp[:], io["interp"]).then_inc(s_w, 16)

            def load(t):
                v = t.parity
                nat = io["ctx_1024"]
                sp.wait_ge(s_y, t.i + 1)
                sp.wait_ge(s_s2, t.i + 1)
                sp.dma_start(ctx_nat[:, v], bass.AP(nat.tensor, nat[bass.ds(t.i, 1)].offset,
                                                    [[D, R], [STEP * D, CH], [1, D]])).then_inc(s_ctx[v], 16)
                sp.dma_start(ctx_T[:, v], io["ctxT"].rearrange("b (c p) l -> p b c l", p=P)[
                    :, bass.ds(t.i, 1)].rearrange("p b c l -> p (b c) l")).then_inc(s_ctx[v], 16)

            turns(sp, load, 0, 0, B, B)

        @block.gpsimd
        def _(pool):
            nc.gpsimd.memset(ident[:], 1.0).then_inc(s_const, 1)
            nc.gpsimd.memset(sel_c[:], 1.0).then_inc(s_const, 1)
            nc.gpsimd.memset(sel_r[:], 1.0).then_inc(s_const, 1)
            nc.gpsimd.memset(ones[:], 1.0).then_inc(s_const, 1)
            pool.wait_ge(s_const, 4)
            nc.gpsimd.affine_select(out=ident[:], in_=ident[:], pattern=[[1, P]], compare_op=ALU.is_equal,
                                    fill=0.0, base=0, channel_multiplier=-1).then_inc(s_const, 1)
            nc.gpsimd.affine_select(out=sel_c[:], in_=sel_c[:], pattern=[[0, L]], compare_op=ALU.is_equal,
                                    fill=0.0, base=0, channel_multiplier=1).then_inc(s_const, 1)
            nc.gpsimd.affine_select(out=sel_r[:], in_=sel_r[:], pattern=[[0, R]], compare_op=ALU.is_equal,
                                    fill=0.0, base=-1, channel_multiplier=1).then_inc(s_const, 1)

            pool.sem_inc(s_mixed, 1)

            def turn(b):
                pool.wait_ge(s_cs_sb, b.i + 1)
                nc.gpsimd.tensor_tensor(diff[:], cs[:, 0:KC, :], cs[:, KC:2 * KC, :], ALU.subtract).then_inc(s_diff, 1)
                pool.wait_ge(s_gate, b.i + 1)
                pool.wait_ge(s_diff, b.i + 1)
                nc.gpsimd.tensor_tensor(mix[:], gate[:], diff[:], ALU.mult).then_inc(s_mix, 1)
                pool.wait_ge(s_mix, b.i + 1)
                pool.wait_ge(s_out, b.i + 1)
                nc.gpsimd.tensor_tensor(mixed[:], mix[:], cs[:, KC:2 * KC, :], ALU.add).then_inc(s_mixed, 1)

            turns(pool, turn, 0, 0, B, B)

        @block.scalar
        def _(act):
            def copied(sem, ready, n, out, in_):
                act.wait_ge(ready, n)
                nc.scalar.copy(out, in_).then_inc(sem, 1)

            def turn(t):
                b, nxt = t, t + 1
                if nxt.within(B):
                    copied(s_xT_sb, s_xT, nxt.i + 1, xT[:], ps_xT)
                if b.within(B):
                    copied(s_p1T_sb, s_p1T, b.i + 2, p1T[:], ps_p1T)
                    copied(s_t_sb, s_t, b.i + 2, tT[:], ps_t)
                    copied(s_y_sb, s_y, b.i + 3, yT[:], ps_y)
                    copied(s_z_sb, s_z, b.i + 1, zT[:], ps_z)
                if nxt.within(B):
                    act.wait_ge(s_mx1, 2 * nxt.i + 2)
                    act.wait_ge(s_p1n, nxt.i + 1)
                    nc.scalar.activation(p1[:], ps_s1[0:S, 0:L], ACT.Exp, bias=nmx1[:], scale=SCALE,
                                         accum_out=sum1[:]).then_inc(s_e1, 1)
                    act.wait_ge(s_mx2, 2 * nxt.i + 2)
                    act.wait_ge(s_p2n, nxt.i + 1)
                    for c in range(CH):
                        last = nc.scalar.activation(p2[:, c, :], ps_sub[:, c, :], ACT.Exp, bias=nmx2[:, c:c + 1],
                                                    scale=SCALE, accum_out=sum2[:, c:c + 1])
                    last.then_inc(s_e2, 1)
                if b.within(B):
                    act.wait_ge(s_g, b.i + 1)
                    for c in range(KC):
                        last = nc.scalar.activation(gate_e[:, c, :], ps_gate[:, c, :], ACT.Exp,
                                                    bias=neg_bg[:, c:c + 1], scale=-1.0)
                    last.then_inc(s_ge, 1)

            act.wait_ge(s_mul_sb, 1)
            turns(act, turn, -1, 1, B - 1, B)

        @block.vector
        def _(dve):
            dve.wait_ge(s_w, 16 * NW)
            for c, (x, y) in enumerate((("bq_c", "bk_s"), ("bk_c", "bq_s"))):
                nc.vector.tensor_tensor(prod[:, :, c], cols[x][:], cols[y][:], ALU.mult)
            nc.vector.tensor_copy(bv[:, 0:KC], cols["bv_s"][:])
            nc.vector.tensor_copy(bv[:, KC:2 * KC], cols["bv_c"][:])
            nc.vector.tensor_scalar(neg_bg[:], cols["bg"][:], -1.0, None, ALU.mult).then_inc(s_prod, 1)
            dve.wait_ge(s_mul, 1)
            for n, bank in ((0, ps_s1), (1, ps_s2)):
                nc.vector.tensor_copy(a_w[:, n], bank[:, 0:KC * D].rearrange("p (c d) -> p c d", c=KC))
            nc.vector.tensor_copy(a_b[:], ps_u[:, 0:2 * KC].rearrange("p (n c) -> p n c", n=2))
            nc.vector.tensor_copy(row_w[:], ps_u[:, 64:64 + 2 * KC].rearrange("p (c n) -> p c n", n=2))
            nc.vector.tensor_copy(row_b[:], ps_u[0:2, 128:129]).then_inc(s_mul_sb, 1)
            dve.wait_ge(s_mul_sb, 1)

            dve.sem_inc(s_p1n, 1)
            dve.sem_inc(s_p2n, 1)

            def turn(t):
                prev, b, nxt = t + -1, t, t + 1
                if nxt.within(B):
                    for n, out in enumerate((xn[:, nxt.parity, :], at(y_nat, nxt.i))):
                        last = nc.vector.tensor_scalar(out, at(y_nat, nxt.i), mean[:, bass.ds(nxt.i, 1)],
                                                       rstd[:, bass.ds(nxt.i, 1)], ALU.subtract, ALU.mult)
                        last.then_inc((s_xn, s_xn_kept)[n], 1)
                if prev.within(B):
                    dve.wait_ge(s_ge, prev.i + 1)
                    nc.vector.tensor_scalar(gate_e[:], gate_e[:], 1.0, None, ALU.add).then_inc(s_gd, 1)
                    dve.wait_ge(s_gd, prev.i + 1)
                    nc.vector.reciprocal(gate[:], gate_e[:]).then_inc(s_gate, 1)
                if nxt.within(B):
                    dve.wait_ge(s_u, nxt.i + 1)
                    nc.vector.tensor_tensor(u[:], ps_uv, a_b[:].unsqueeze(3).to_broadcast([P, 2, KC, S]),
                                            ALU.add).then_inc(s_u_sb, 1)
                    dve.wait_ge(s_rows, nxt.i + 1)
                    nc.vector.tensor_scalar(rows[:], ps_rows, row_b[:], None, ALU.add).then_inc(s_rows_sb, 1)
                    dve.wait_ge(s_s1, nxt.i + 1)
                    nc.vector.reduce_max(mx1[:], ps_s1[0:S, 0:L], AX.X).then_inc(s_mx1, 1)
                    dve.wait_ge(s_mx1, 2 * nxt.i + 1)
                    nc.vector.tensor_scalar(nmx1[:], mx1[:], -SCALE, None, ALU.mult).then_inc(s_mx1, 1)
                    dve.wait_ge(s_s2, nxt.i + 3)
                    nc.vector.reduce_max(mx2[:], ps_sub, AX.X).then_inc(s_mx2, 1)
                    dve.wait_ge(s_mx2, 2 * nxt.i + 1)
                    nc.vector.tensor_scalar(nmx2[:], mx2[:], -SCALE, None, ALU.mult).then_inc(s_mx2, 1)
                    dve.wait_ge(s_e1, nxt.i + 1)
                    nc.vector.reciprocal(rec1[:], sum1[:]).then_inc(s_r1, 1)
                    dve.wait_ge(s_r1, nxt.i + 1)
                    dve.wait_ge(s_p1T, nxt.i + 1)
                    nc.vector.tensor_scalar(p1n[:], p1[:], rec1[:], None, ALU.mult).then_inc(s_p1n, 1)
                if b.within(B):
                    dve.wait_ge(s_cs, b.i + 1)
                    dve.wait_ge(s_mixed, b.i + 1)
                    nc.vector.tensor_tensor(cs[:], ps_csv, bv[:].unsqueeze(2).to_broadcast([P, 2 * KC, S]),
                                            ALU.add).then_inc(s_cs_sb, 1)
                if nxt.within(B):
                    dve.wait_ge(s_e2, nxt.i + 1)
                    nc.vector.reciprocal(rec2[:], sum2[:]).then_inc(s_r2, 1)
                    dve.wait_ge(s_r2, nxt.i + 1)
                    dve.wait_ge(s_t, nxt.i + 1)
                    nc.vector.tensor_tensor(p2n[:], p2[:], rec2[:].unsqueeze(2).to_broadcast([R, CH, S]),
                                            ALU.mult).then_inc(s_p2n, 1)
                if prev.within(B):
                    dve.wait_ge(s_out, prev.i + 2)
                    dve.wait_ge(s_xn_kept, prev.i + 1)
                    nc.vector.tensor_tensor(at(y_nat, prev.i), ps_out, at(y_nat, prev.i), ALU.add).then_inc(s_sum, 1)
                    dve.wait_ge(s_sum, prev.i + 1)
                    nc.vector.bn_stats(at(keep["stats"], prev.i), at(y_nat, prev.i)).then_inc(s_stats, 1)

            turns(dve, turn, -1, 1, B - 1, B + 1)

        @block.tensor
        def _(pe):
            def mm(out, lhsT, rhs, k, n, start=None, stop=None):
                return nc.tensor.matmul(out, lhsT, rhs, start=(k == 0) if start is None else start,
                                        stop=(k == n - 1) if stop is None else stop)

            pe.wait_ge(s_w, 16 * NW)
            pe.wait_ge(s_const, 7)
            pe.wait_ge(s_prod, 1)
            for n, (x, y, bank, bx) in enumerate((("Wq_c", "Wk_s", ps_s1, "bq_c"), ("Wk_c", "Wq_s", ps_s2, "bk_c"))):
                for c in range(KC):
                    for o in range(KC):
                        mm(bank[:, c * D:(c + 1) * D], w[x][:, o, c * P:(c + 1) * P], w[y][:, o, :], o, KC)
                for c in range(KC):
                    for o in range(KC):
                        mm(ps_u[:, n * KC + c:n * KC + c + 1], w[y][:, o, c * P:(c + 1) * P], cols[bx][:, o:o + 1], o, KC)
            for n, (x, bx) in enumerate((("Wq_c", "bk_s"), ("Wk_c", "bq_s"))):
                for c in range(KC):
                    for o in range(KC):
                        mm(ps_u[:, 64 + 2 * c + n:65 + 2 * c + n], w[x][:, o, c * P:(c + 1) * P], cols[bx][:, o:o + 1], o, KC)
            for o in range(KC):
                last = mm(ps_u[0:2, 128:129], prod[:, o, :], ones[:, 0:1], o, KC)
            last.then_inc(s_mul, 1)
            pe.wait_ge(s_mul_sb, 1)
            pe.sem_inc(s_y, 2)
            pe.sem_inc(s_s2, 2)
            pe.sem_inc(s_p1T, 1)
            pe.sem_inc(s_t, 1)
            pe.sem_inc(s_out, 1)

            def turn(t):
                prev, b, nxt = t + -1, t, t + 1
                v, vn = b.parity, nxt.parity
                if nxt.within(B):
                    pe.wait_ge(s_xn, nxt.i + 1)
                    if not isinstance(nxt.i, int) or nxt.i > 2:
                        pe.wait_ge(s_sum, nxt.i - 2)
                    for c in range(KC):
                        last = nc.tensor.transpose(ps_xT[:, c, :], xn[:, vn, c * P:(c + 1) * P], ident[0:S, 0:S])
                    last.then_inc(s_xT, 1)
                if b.within(B):
                    pe.wait_ge(s_p1n, b.i + 2)
                    for c in range(CH):
                        last = nc.tensor.transpose(ps_p1T[:, c, :], p1n[:, c * STEP:c * STEP + R], ident[0:S, 0:S])
                    last.then_inc(s_p1T, 1)
                    pe.wait_ge(s_p2n, b.i + 2)
                    for c in range(CH):
                        last = mm(ps_t, p2n[:, c, :], interp[:, c, :], c, CH)
                    last.then_inc(s_t, 1)
                if nxt.within(B):
                    pe.wait_ge(s_xT_sb, nxt.i + 1)
                    for n in range(2):
                        for c in range(KC):
                            for k in range(KC):
                                last = mm(ps_uv[:, n, c, :], a_w[:, n, k, c * P:(c + 1) * P], xT[:, k, :], k, KC)
                    last.then_inc(s_u, 1)
                if b.within(B):
                    if not isinstance(b.i, int) or b.i > 1:
                        pe.wait_ge(s_sum, b.i - 1)
                    pe.wait_ge(s_p1T_sb, b.i + 1)
                    for c in range(KC):
                        for k in range(CH):
                            r = R if k == CH - 1 else STEP
                            last = mm(ps_y[:, c, :], ctx_nat[0:r, v, k, c * P:(c + 1) * P], p1T[0:r, k, :], k, CH)
                    last.then_inc(s_y, 1)
                    pe.wait_ge(s_t_sb, b.i + 1)
                    for c in range(KC):
                        last = mm(ps_z[:, c, :], xn[:, v, c * P:(c + 1) * P], tT[:], 0, 1)
                    last.then_inc(s_z, 1)
                if nxt.within(B):
                    for k in range(KC):
                        last = mm(ps_rows, row_w[:, k, :], xT[:, k, :], k, KC)
                    last.then_inc(s_rows, 1)
                    pe.wait_ge(s_u_sb, nxt.i + 1)
                    pe.wait_ge(s_ctx[vn], 32 * nxt.half + 32)
                    for k in range(KC):
                        mm(ps_s1[0:S, 0:L], u[:, 0, k, :], ctx_T[:, vn, k, :], k, KC, stop=False)
                    pe.wait_ge(s_rows_sb, nxt.i + 1)
                    mm(ps_s1[0:S, 0:L], rows[:], sel_c[:], 1, 2).then_inc(s_s1, 1)
                    for c in range(CH):
                        for k in range(KC):
                            mm(ps_sub[:, c, :], ctx_T[:, vn, k, c * STEP:c * STEP + R], u[:, 1, k, :], k, KC, stop=False)
                        last = mm(ps_sub[:, c, :], sel_r[:], rows[:], 1, 2)
                    last.then_inc(s_s2, 1)
                if b.within(B):
                    pe.wait_ge(s_y_sb, b.i + 1)
                    pe.wait_ge(s_z_sb, b.i + 1)
                    for n, (wn, src) in enumerate((("WvT_s", yT), ("WvT_c", zT))):
                        for c in range(KC):
                            for k in range(KC):
                                last = mm(ps_csv[:, n * KC + c, :], w[wn][:, k, c * P:(c + 1) * P], src[:, k, :], k, KC)
                    last.then_inc(s_cs, 1)
                if prev.within(B):
                    pe.wait_ge(s_mixed, prev.i + 2)
                    for c in range(KC):
                        last = nc.tensor.transpose(ps_out[:, c * P:(c + 1) * P], mixed[:, c, :], ident[:])
                    last.then_inc(s_out, 1)
                if b.within(B):
                    pe.wait_ge(s_cs_sb, b.i + 1)
                    for c in range(KC):
                        for k in range(2 * KC):
                            last = mm(ps_gate[:, c, :], w_gT[:, k, c * P:(c + 1) * P], cs[:, k, :], k, 2 * KC)
                    last.then_inc(s_g, 1)

            turns(pe, turn, -1, 1, B - 1, B + 1)

        finish_norm(nc, m, block, keep, s_stats)


def routed_ffn(nc, io, keep):
    B, S, D = io["x"].shape
    E, _, H = io["L0_ffn_w1"].shape
    KC, HC = D // P, H // P
    TOP, CAP = 3, P
    G = 4
    GROUPS = B // G
    FAR = 1 << 17
    y_nat, mean, rstd = keep["y"], keep["mean"], keep["rstd"]
    x_rows = nc.dram_tensor("moe_x_rows", (B * S + CAP, D), F32, kind="Internal").ap()
    y_rows = nc.dram_tensor("moe_y_rows", (B * S + CAP, D), F32, kind="Internal").ap()
    table = nc.dram_tensor("moe_table", (CAP * E, 2), U32, kind="Internal").ap()
    with ExitStack() as ctx:
        m = Names(nc, ctx, "moe")
        ident = m.sb("ident", [P, P])
        before = m.sb("before", [S, S])
        ones = m.sb("ones", [P, P])
        iota_i = m.sb("iota_i", [S, E], mybir.dt.int32)
        iota_e = m.sb("iota_e", [S, E])
        row_i = m.sb("row_i", [S, G], mybir.dt.int32)
        row_f = m.sb("row_f", [S, G])
        spare = m.sb("spare", [P, E, 2], U32)
        zeros = m.sb("zeros", [CAP, D])
        gate_w = m.sb("gate_w", [P, KC, E])
        gate_b = m.sb("gate_b", [S, E])
        xg = m.sb("xg", [S, 2, G, D])
        xgT = m.sb("xgT", [P, G, KC, S])
        lg = m.sb("lg", [S, G, E])
        top_v = m.sb("top_v", [S, 2, G, 8])
        top_i = m.sb("top_i", [S, G, 8], U32)
        top_f = m.sb("top_f", [S, 2, G, TOP])
        hot = m.sb("hot", [S, 2, G, TOP, E])
        hot01 = m.sb("hot01", [S, G, E])
        mask = m.sb("mask", [S, 2, G, E])
        mask_sum = m.sb("mask_sum", [S, 2, E])
        earlier = m.sb("earlier", [S, E])
        hot_pos = m.sb("hot_pos", [S, G, TOP, E])
        pos = m.sb("pos", [S, G, TOP])
        full = m.sb("full", [S, G, TOP])
        slot = m.sb("slot", [S, G, TOP])
        slot_u = m.sb("slot_u", [S, 2, G, TOP], U32)
        entry = m.sb("entry", [S, 2, G, TOP, 2], U32)
        logit = m.sb("logit", [S, G, TOP])
        expd = m.sb("expd", [S, G, TOP])
        sums = m.sb("sums", [S, G])
        recs = m.sb("recs", [S, G])
        places = m.sb("places", [P, E, 2], U32)
        place = m.sb("place", [P, 2], U32)
        place_out = m.sb("place_out", [P, 2], U32)
        b1 = m.sb("b1", [P, E, HC])
        b2 = m.sb("b2", [1, 2, D])
        w1 = m.sb("w1", [P, 2, KC, H])
        w2 = m.sb("w2", [P, 2, HC, D])
        xe = m.sb("xe", [P, 2, D])
        xeT = m.sb("xeT", [P, 2, KC, CAP])
        hT = m.sb("hT", [P, 2, HC, CAP])
        ye = m.sb("ye", [P, 2, D])
        ps_T = m.ps("ps_T", [P, 2, 512])
        ps_h = m.ps("ps_h", [P, 2, 2, 512])
        ps_y = m.ps("ps_y", [P, 2, 512])
        ps_xT = [ps_T[:, v, 0:2 * KC * S].rearrange("p (g c s) -> p g c s", g=2, c=KC) for v in range(2)]
        ps_logit = ps_h[0:S, 0, 0, 0:G * E].rearrange("p (g e) -> p g e", g=G)
        ps_place = ps_h[0:S, 0, 1, 0:G * E].rearrange("p (g e) -> p g e", g=G)

        sem = m.sem
        s_w, s_const, s_zero, s_zero_out = sem("weights"), sem("constants"), sem("zeros"), sem("table_zeroed")
        s_xg, s_xg_out, s_spare = sem("rows_normalised"), [sem(f"rows{v}_stored") for v in range(2)], sem("spare_rows_stored")
        s_T, s_T_sb, s_lgp, s_lg = sem("rows_transposed"), sem("rowsT_stored"), sem("logits_summed"), sem("logits")
        s_topv, s_top, s_topf, s_hot = sem("top_values"), sem("top_numbers"), sem("top_floats"), sem("one_hot")
        s_hot01, s_mask, s_msum = sem("one_hot_pair"), sem("mask"), sem("mask_summed")
        s_earlier, s_place, s_back = sem("earlier_counts"), sem("places_counted"), sem("back_chain")
        s_logit, s_exp, s_slots = sem("top_logits"), sem("top_exp"), sem("slots")
        s_scat = [sem(f"numbers_scattered{v}") for v in range(2)]
        s_places, s_col = sem("places_loaded"), sem("place_column")
        s_w1 = [sem(f"w1_{v}_loaded") for v in range(2)]
        s_w2 = [sem(f"w2_{v}_loaded") for v in range(2)]
        s_xe = [sem(f"expert_rows{v}") for v in range(2)]
        s_xeT, s_xeT_sb, s_h, s_gelu = sem("expert_rowsT"), sem("expert_rowsT_stored"), sem("hidden"), sem("gelu")
        s_ye, s_ye_sb = sem("expert_out"), sem("expert_out_stored")
        s_col_out, s_added, s_sums = sem("place_out_column"), sem("results_added"), [sem(f"sums{g}_loaded") for g in range(GROUPS)]
        s_hot_pos = sem("places_by_rank")
        s_stats, s_took = sem("stats_ready"), sem("waits_taken")
        block = ctx.enter_context(nc.Block())

        @block.sync
        def _(sp):
            sp.dma_start(gate_w[:], io["L0_ffn_gate_w"].rearrange("(c p) e -> p c e", p=P)).then_inc(s_w, 16)
            sp.dma_start(gate_b[:], io["L0_ffn_gate_b"].partition_broadcast(S)).then_inc(s_w, 16)
            sp.dma_start(b1[:], io["L0_ffn_b1_cols"]).then_inc(s_w, 16)
            sp.wait_ge(s_zero, 3)
            sp.dma_start(table.rearrange("(p c) o -> p (c o)", p=P), spare[:].rearrange("p e o -> p (e o)")
                         ).then_inc(s_zero_out, 16)
            for rows in (x_rows, y_rows):
                sp.dma_start(rows[B * S:B * S + CAP], zeros[:]).then_inc(s_spare, 16)

            def weights(t):
                v = t.parity
                sp.wait_ge(s_h, 2 * t.i + 2)
                sp.dma_start(w1[:, v], io["L0_ffn_w1"][bass.ds(t.i, 1)].rearrange(
                    "o (c p) h -> p (o c) h", p=P)).then_inc(s_w1[v], 16)
                sp.wait_ge(s_ye, t.i + 1)
                sp.dma_start(w2[:, v], io["L0_ffn_w2"][bass.ds(t.i, 1)].rearrange(
                    "o (c p) d -> p (o c) d", p=P)).then_inc(s_w2[v], 16)
                sp.dma_start(b2[:, v], io["L0_ffn_b2"][bass.ds(t.i, 1)]).then_inc(s_w2[v], 16)

            for e in range(2):
                weights(Turn(e, e, 0))
            def keep_rows(g):
                sp.wait_ge(s_xg, g.i + 1)
                sp.sem_inc(s_took, 1)
                for rows in (x_rows, y_rows):
                    sp.dma_start(rows[bass.ds(g.i * (G * S), G * S)].rearrange("(g s) d -> s g d", g=G),
                                 xg[:, g.parity]).then_inc(s_xg_out[g.parity], 16)

            turns(sp, keep_rows, 0, 0, GROUPS, GROUPS)
            for v in range(2):
                sp.wait_ge(s_scat[v], 16 * G * TOP * GROUPS // 2)
            sp.dma_start(places[:].rearrange("p e o -> p (e o)"), table.rearrange("(p e) o -> p (e o)", p=P)).then_inc(s_places, 16)
            turns(sp, weights, 2, 2, E, E)
            sp.wait_ge(s_added, 16 * E)
            for g in range(GROUPS):
                sp.dma_start(y_nat[:, g * G:(g + 1) * G, :], y_rows[g * G * S:(g + 1) * G * S].rearrange(
                    "(g s) d -> s g d", g=G)).then_inc(s_sums[g], 16)

        @block.gpsimd
        def _(pool):
            nc.gpsimd.iota(spare[:, :, 0], pattern=[[0, E]], base=B * S, channel_multiplier=1).then_inc(s_zero, 1)
            nc.gpsimd.memset(spare[:, :, 1], 0).then_inc(s_zero, 1)
            nc.gpsimd.memset(zeros[:], 0.0).then_inc(s_zero, 1)
            nc.gpsimd.memset(ident[:], 1.0).then_inc(s_const, 1)
            nc.gpsimd.memset(before[:], 1.0).then_inc(s_const, 1)
            nc.gpsimd.memset(ones[:], 1.0).then_inc(s_const, 1)
            nc.gpsimd.memset(earlier[:], 0.0).then_inc(s_const, 1)
            nc.gpsimd.iota(iota_i[:], pattern=[[1, E]], base=0, channel_multiplier=0).then_inc(s_const, 1)
            nc.gpsimd.iota(row_i[:], pattern=[[S, G]], base=0, channel_multiplier=1).then_inc(s_const, 1)
            pool.wait_ge(s_const, 6)
            nc.gpsimd.tensor_copy(iota_e[:], iota_i[:]).then_inc(s_const, 1)
            nc.gpsimd.tensor_copy(row_f[:], row_i[:]).then_inc(s_const, 1)
            nc.gpsimd.affine_select(out=ident[:], in_=ident[:], pattern=[[1, P]], compare_op=ALU.is_equal,
                                    fill=0.0, base=0, channel_multiplier=-1).then_inc(s_const, 1)
            nc.gpsimd.affine_select(out=before[:], in_=before[:], pattern=[[1, S]], compare_op=ALU.is_gt,
                                    fill=0.0, base=0, channel_multiplier=-1).then_inc(s_const, 1)
            pool.wait_ge(s_zero_out, 16)

            def route(g):
                v = g.parity
                pool.wait_ge(s_slots, g.i + 1)
                pool.sem_inc(s_took, 1)
                for q in range(G):
                    for k in range(TOP):
                        nc.gpsimd.indirect_dma_start(
                            out=table[:], out_offset=bass.IndirectOffsetOnAxis(ap=slot_u[:, v, q, k:k + 1], axis=0),
                            in_=entry[:, v, q, k, :], in_offset=None, bounds_check=CAP * E - 1,
                            oob_is_err=False).then_inc(s_scat[v], 16)

            turns(pool, route, 0, 0, GROUPS, GROUPS)

            pool.wait_ge(s_places, 16)
            for v in range(2):
                pool.wait_ge(s_xg_out[v], 32 * GROUPS // 2)
            pool.wait_ge(s_spare, 32)

            def gather(t):
                v = t.parity
                pool.wait_ge(s_xeT, t.i + 1)
                pool.sem_inc(s_took, 1)
                nc.gpsimd.tensor_copy(place[:, v:v + 1], at(places, t.i)[:, 0:1]).then_inc(s_col, 1)
                pool.wait_ge(s_col, t.i + 1)
                pool.sem_inc(s_took, 1)
                nc.gpsimd.indirect_dma_start(
                    out=xe[:, v, :], out_offset=None, in_=x_rows[:],
                    in_offset=bass.IndirectOffsetOnAxis(ap=place[:, v:v + 1], axis=0)).then_inc(s_xe[v], 16)

            def add(t):
                v = t.parity
                if not isinstance(t.i, int) or t.i > 0:
                    pool.wait_ge(s_added, 16 * t.i)
                    pool.sem_inc(s_took, 1)
                nc.gpsimd.tensor_copy(place_out[:, v:v + 1], at(places, t.i)[:, 0:1]).then_inc(s_col_out, 1)
                pool.wait_ge(s_ye_sb, t.i + 3)
                pool.sem_inc(s_took, 1)
                pool.wait_ge(s_col_out, t.i + 1)
                pool.sem_inc(s_took, 1)
                nc.gpsimd.indirect_dma_start(
                    out=y_rows[:], out_offset=bass.IndirectOffsetOnAxis(ap=place_out[:, v:v + 1], axis=0),
                    in_=ye[:, v, :], in_offset=None, compute_op=ALU.add).then_inc(s_added, 16)

            def turn(t):
                if (t + 4).within(E):
                    gather(t + 4)
                if t.within(E):
                    add(t)

            turns(pool, turn, -4, 2, E - 4, E)

        @block.scalar
        def _(act):
            def route(t):
                g, far = t, t + 2
                if far.within(GROUPS):
                    for h in range(2):
                        act.wait_ge(s_T, 2 * far.i + (h + 1))
                        nc.scalar.copy(xgT[:, 2 * h:2 * h + 2], ps_xT[h]).then_inc(s_T_sb, 1)
                if g.within(GROUPS):
                    act.wait_ge(s_logit, g.i + 1)
                    nc.scalar.activation(expd[:], logit[:], ACT.Exp).then_inc(s_exp, 1)

            turns(act, route, -2, 2, GROUPS - 2, GROUPS)

            def expert(t):
                v = t.parity
                for h in range(2):
                    act.wait_ge(s_h, 2 * t.i + (h + 5))
                    if h == 0:
                        act.wait_ge(s_ye, t.i + 1)
                    for c in range(HC // 2):
                        k = h * HC // 2 + c
                        last = nc.scalar.activation(hT[:, v, k, :], ps_h[:, v, h, c * CAP:(c + 1) * CAP], ACT.Gelu,
                                                    bias=at(b1, t.i)[:, k:k + 1])
                    last.then_inc(s_gelu, 1)

            turns(act, expert, 0, 0, E, E)

        @block.tensor
        def _(pe):
            def mm(out, lhsT, rhs, k, n):
                return nc.tensor.matmul(out, lhsT, rhs, start=(k == 0), stop=(k == n - 1))

            pe.wait_ge(s_w, 16 * 3)
            pe.wait_ge(s_const, 10)
            pe.sem_inc(s_h, 4)
            pe.sem_inc(s_ye, 2)
            pe.sem_inc(s_xeT, 2)

            def route(t):
                g, far = t, t + 2
                if g.within(GROUPS):
                    v = g.parity
                    pe.wait_ge(s_mask, g.i + 1)
                    pe.wait_ge(s_earlier, g.i + 1)
                    pe.wait_ge(s_hot_pos, g.i + 1)
                    for q in range(G):
                        mm(ps_place[:, q, :], before[:], mask[:, v, q, :], 0, 2)
                        for q2 in range(q):
                            mm(ps_place[:, q, :], ones[0:S, 0:S], mask[:, v, q2, :], 1, 3)
                        last = mm(ps_place[:, q, :], ones[0:S, 0:S], earlier[:], 1, 2)
                    last.then_inc(s_place, 1)
                if far.within(GROUPS):
                    pe.wait_ge(s_xg, far.i + 1)
                    for h in range(2):
                        for q in range(2):
                            for c in range(KC):
                                last = nc.tensor.transpose(ps_xT[h][:, q, c, :], xg[:, far.parity, 2 * h + q, c * P:(c + 1) * P],
                                                           ident[0:S, 0:S])
                        last.then_inc(s_T, 1)
                    pe.wait_ge(s_T_sb, 2 * far.i + 2)
                    if not isinstance(far.i, int) or far.i > 0:
                        pe.wait_ge(s_lg, far.i)
                    for q in range(G):
                        for c in range(KC):
                            last = mm(ps_logit[:, q, :], xgT[:, q, c, :], gate_w[:, c, :], c, KC)
                    last.then_inc(s_lgp, 1)

            turns(pe, route, -2, 2, GROUPS - 2, GROUPS)

            def rowsT(e):
                v = e.parity
                pe.wait_ge(s_xe[v], 16 * e.half + 16)
                for c in range(KC):
                    last = nc.tensor.transpose(ps_T[:, v, c * P:(c + 1) * P], xe[:, v, c * P:(c + 1) * P], ident[:])
                last.then_inc(s_xeT, 1)

            def hidden(e):
                v = e.parity
                pe.wait_ge(s_w1[v], 16 * e.half + 16)
                pe.wait_ge(s_xeT_sb, e.i + 1)
                for h in range(2):
                    for c in range(HC // 2):
                        n = h * HC // 2 + c
                        for k in range(KC):
                            last = mm(ps_h[:, v, h, c * CAP:(c + 1) * CAP], w1[:, v, k, n * P:(n + 1) * P],
                                      xeT[:, v, k, :], k, KC)
                    last.then_inc(s_h, 1)

            def results(e):
                v = e.parity
                pe.wait_ge(s_w2[v], 32 * e.half + 32)
                pe.wait_ge(s_ye_sb, e.i + 1)
                mm(ps_y[:, v, 0:D], ones[0:1, :], b2[:, v, :], 0, 2)
                for h in range(2):
                    pe.wait_ge(s_gelu, 2 * e.i + (h + 1))
                    for c in range(HC // 2):
                        n = h * HC // 2 + c
                        last = mm(ps_y[:, v, 0:D], hT[:, v, n, :], w2[:, v, n, :], 1 if n < HC - 1 else 2, 3)
                last.then_inc(s_ye, 1)

            def expert(t):
                for e, part in ((t + 1, hidden), (t + 2, rowsT), (t, results)):
                    if e.within(E):
                        part(e)

            turns(pe, expert, -2, 0, E - 2, E)

        @block.vector
        def _(dve):
            back = Chain(dve, s_back, 7)
            dve.wait_ge(s_w, 16 * 3)
            dve.wait_ge(s_const, 10)
            dve.sem_inc(s_ye_sb, 2)
            dve.sem_inc(s_hot_pos, 1)
            dve.sem_inc(s_earlier, 1)

            def route(t):
                g, nxt, far = t, t + 1, t + 2
                if far.within(GROUPS):
                    if not isinstance(far.i, int) or far.i > 1:
                        dve.wait_ge(s_xg_out[far.parity], 32 * far.half)
                    for q in range(G):
                        b = far.i * G + q
                        last = nc.vector.tensor_scalar(xg[:, far.parity, q, :], at(y_nat, b), mean[:, bass.ds(b, 1)],
                                                       rstd[:, bass.ds(b, 1)], ALU.subtract, ALU.mult)
                    last.then_inc(s_xg, 1)
                if nxt.within(GROUPS):
                    v = nxt.parity
                    dve.wait_ge(s_lgp, nxt.i + 1)
                    nc.vector.tensor_tensor(lg[:], ps_logit, gate_b[:].unsqueeze(1).to_broadcast([S, G, E]),
                                            ALU.add).then_inc(s_lg, 1)
                    dve.wait_ge(s_lg, nxt.i + 1)
                    dve.sem_inc(s_took, 1)
                    for q in range(G):
                        last = nc.vector.max(top_v[:, v, q, :], lg[:, q, :])
                    last.then_inc(s_topv, 1)
                    dve.wait_ge(s_topv, nxt.i + 1)
                    dve.sem_inc(s_took, 1)
                    for q in range(G):
                        last = nc.vector.max_index(top_i[:, q, :], top_v[:, v, q, :], lg[:, q, :])
                    last.then_inc(s_top, 1)
                    dve.wait_ge(s_top, nxt.i + 1)
                    nc.vector.tensor_copy(top_f[:, v], top_i[:, :, 0:TOP]).then_inc(s_topf, 1)
                    dve.wait_ge(s_topf, nxt.i + 1)
                    for q in range(G):
                        last = nc.vector.tensor_tensor(
                            hot[:, v, q], iota_e[:].unsqueeze(1).to_broadcast([S, TOP, E]),
                            top_f[:, v, q, :].unsqueeze(2).to_broadcast([S, TOP, E]), ALU.is_equal)
                    last.then_inc(s_hot, 1)
                    dve.wait_ge(s_hot, nxt.i + 1)
                    nc.vector.tensor_tensor(hot01[:], hot[:, v, :, 0, :], hot[:, v, :, 1, :], ALU.add).then_inc(s_hot01, 1)
                    dve.wait_ge(s_hot01, nxt.i + 1)
                    nc.vector.tensor_tensor(mask[:, v], hot01[:], hot[:, v, :, 2, :], ALU.add).then_inc(s_mask, 1)
                    dve.wait_ge(s_mask, nxt.i + 1)
                    nc.vector.reduce_sum(mask_sum[:, v, :], mask[:, v].rearrange("p g e -> p e g"), AX.X).then_inc(s_msum, 1)
                if g.within(GROUPS):
                    v = g.parity
                    back.start(g.i)
                    dve.wait_ge(s_place, g.i + 1)
                    nc.vector.tensor_tensor(earlier[:], earlier[:], mask_sum[:, v, :], ALU.add).then_inc(s_earlier, 1)
                    for q in range(G):
                        last = nc.vector.tensor_tensor(hot_pos[:, q], hot[:, v, q],
                                                       ps_place[:, q, :].unsqueeze(1).to_broadcast([S, TOP, E]), ALU.mult)
                    last.then_inc(s_hot_pos, 1)
                    dve.wait_ge(s_hot_pos, g.i + 2)
                    back(nc.vector.reduce_sum(pos[:], hot_pos[:], AX.X))
                    nc.vector.tensor_tensor(logit[:], top_v[:, v, :, 0:TOP],
                                            top_v[:, v, :, 0:1].to_broadcast([S, G, TOP]), ALU.subtract).then_inc(s_logit, 1)
                    back(nc.vector.tensor_scalar(full[:], pos[:], float(CAP), float(FAR), ALU.is_ge, ALU.mult))
                    back(nc.vector.tensor_tensor(full[:], full[:], top_f[:, v], ALU.add))
                    back(nc.vector.scalar_tensor_tensor(out=slot[:], in0=pos[:], scalar=float(E), in1=full[:],
                                                        op0=ALU.mult, op1=ALU.add))
                    dve.wait_ge(s_exp, g.i + 1)
                    back(nc.vector.reduce_sum(sums[:], expd[:], AX.X))
                    back(nc.vector.reciprocal(recs[:], sums[:]))
                    if not isinstance(g.i, int) or g.i > 1:
                        dve.wait_ge(s_scat[v], g.half * (16 * G * TOP))
                    nc.vector.tensor_copy(slot_u[:, v], slot[:])
                    nc.vector.tensor_copy(entry[:, v, :, :, 0], row_f[:].unsqueeze(2).to_broadcast([S, G, TOP]))
                    nc.vector.tensor_tensor(entry[:, v, :, :, 1].bitcast(F32), expd[:],
                                            recs[:].unsqueeze(2).to_broadcast([S, G, TOP]), ALU.mult).then_inc(s_slots, 1)
                    dve.wait_ge(s_slots, g.i + 1)
                    back(nc.vector.tensor_scalar(row_f[:], row_f[:], float(G * S), None, ALU.add))
                    back.end()

            turns(dve, route, -2, 2, GROUPS - 2, GROUPS)

            def rowsT(e):
                dve.wait_ge(s_xeT, e.i + 3)
                nc.vector.tensor_copy(xeT[:, e.parity], ps_T[:, e.parity, 0:KC * CAP].rearrange("p (c n) -> p c n", c=KC)
                                      ).then_inc(s_xeT_sb, 1)

            def expert(t):
                if (t + 2).within(E):
                    rowsT(t + 2)
                if not t.within(E):
                    return
                v = t.parity
                dve.wait_ge(s_ye, t.i + 3)
                if not isinstance(t.i, int) or t.i > 1:
                    dve.wait_ge(s_added, 16 * (t.i - 1))
                nc.vector.tensor_scalar(ye[:, v, :], ps_y[:, v, 0:D], at(places, t.i)[:, 1:2].bitcast(F32), None,
                                        ALU.mult).then_inc(s_ye_sb, 1)

            dve.wait_ge(s_places, 16)
            turns(dve, expert, -2, 2, E - 2, E)
            for g in range(GROUPS):
                dve.wait_ge(s_sums[g], 16)
                for b in range(g * G, (g + 1) * G):
                    nc.vector.bn_stats(keep["stats"][:, b, :], y_nat[:, b, :]).then_inc(s_stats, 1)

        finish_norm(nc, m, block, keep, s_stats)


def head_masks(nc, eng, tile, s_const):
    heads = tile.shape[1]
    d = P // heads
    nc.gpsimd.memset(tile[:], 1.0).then_inc(s_const, 1)
    eng.wait_ge(s_const, 1)
    nc.gpsimd.affine_select(out=tile[:], in_=tile[:], pattern=[[-d, heads]], compare_op=ALU.is_ge, fill=0.0,
                            base=0, channel_multiplier=1).then_inc(s_const, 1)
    eng.wait_ge(s_const, 2)
    nc.gpsimd.affine_select(out=tile[:], in_=tile[:], pattern=[[d, heads]], compare_op=ALU.is_ge, fill=0.0,
                            base=d - 1, channel_multiplier=-1).then_inc(s_const, 1)


def causal_heads(nc, io, keep):
    B, S, D = io["x"].shape
    NH = io["L1_attn_m"].shape[0]
    HD = D // NH
    KC = D // P
    HC = NH // KC
    BH = HC // 2
    SCALE = float(D) ** -0.5
    LOW = -1e30
    y_nat, mean, rstd = keep["y"], keep["mean"], keep["rstd"]
    with ExitStack() as ctx:
        m = Names(nc, ctx, "cau")
        w = m.sb("w", [P, KC, 3 * D])
        slope = m.sb("slope", [S, NH])
        rel_i = m.sb("rel_i", [S, S], mybir.dt.int32)
        rel = m.sb("rel", [S, S])
        bias = m.sb("bias", [S, NH, S])
        in_head = m.sb("in_head", [P, HC])
        ident = m.sb("ident", [P, P])
        xn = m.sb("xn", [S, 2, D])
        xT = m.sb("xT", [P, KC, S])
        qT = m.sb("qT", [P, KC, S])
        k_heads = m.sb("k_heads", [P, KC, HC, S])
        vals = m.sb("vals", [S, 2, NH, HD + 1])
        sc = m.sb("sc", [S, KC, HC, S])
        mx = m.sb("mx", [S, KC, HC])
        low = m.sb("low", [S, KC, HC, S])
        prob = m.sb("prob", [S, KC, HC, S])
        probT = m.sb("probT", [S, KC, HC, S])
        rec = m.sb("rec", [S, NH])
        att = m.sb("att", [S, NH, HD])
        ps_x = m.ps("ps_x", [P, 512])
        ps_kk = m.ps("ps_kk", [P, 512])
        ps_v = m.ps("ps_v", [P, 512])
        ps_s = m.ps("ps_s", [P, 2, 512])
        ps_t = m.ps("ps_t", [P, 2, 512])
        ps_o = m.ps("ps_o", [P, 512])
        ps_xT = ps_x[:, 0:KC * S].rearrange("p (c s) -> p c s", c=KC)
        ps_q = ps_x[:, KC * S:2 * KC * S].rearrange("p (c s) -> p c s", c=KC)
        ps_k = ps_kk[:, 0:KC * S].rearrange("p (c s) -> p c s", c=KC)
        ps_sum = ps_o[0:S, 0:NH * (HD + 1)].rearrange("p (h d) -> p h d", h=NH)
        ps_sc = ps_s[0:S, :, 0:BH * S]
        ps_pT = ps_t[0:S, :, 0:BH * S]

        sem = m.sem
        s_w, s_const, s_head = sem("weights"), sem("constants"), sem("head_masks")
        s_rel, s_bias = sem("distances"), sem("bias_table")
        s_xn, s_xT, s_xT_sb = sem("rows_normalised"), sem("xT_transposed"), sem("xT_stored")
        s_xn_kept = sem("rows_normalised_in_place")
        s_k, s_q, s_q_sb, s_k_sb = sem("k_projected"), sem("q_projected"), sem("q_stored"), sem("k_spread")
        s_v, s_v_sb = sem("values"), sem("values_stored")
        s_s, s_sc, s_mx = sem("scores"), sem("scores_biased"), sem("maxima")
        s_low, s_p = sem("maxima_subtracted"), sem("weights_ready")
        s_t, s_t_sb = sem("weights_transposed"), sem("weightsT_stored")
        s_o, s_rec, s_att = sem("values_summed"), sem("sums_inverted"), sem("attended")
        s_sum, s_stats = sem("rows_added"), sem("stats_ready")
        block = ctx.enter_context(nc.Block())

        @block.sync
        def _(sp):
            sp.dma_start(w[:], io["L1_attn_W_kqv"].rearrange("(c p) n -> p c n", p=P)).then_inc(s_w, 16)
            sp.dma_start(slope[:], io["L1_attn_m"].rearrange("h a b -> (h a b)").partition_broadcast(S)).then_inc(s_w, 16)

        @block.gpsimd
        def _(pool):
            head_masks(nc, pool, in_head, s_head)
            nc.gpsimd.memset(ident[:], 1.0).then_inc(s_const, 1)
            nc.gpsimd.memset(vals[:, :, :, HD:HD + 1], 1.0).then_inc(s_const, 1)
            nc.gpsimd.iota(rel_i[:], pattern=[[1, S]], base=0, channel_multiplier=-1).then_inc(s_const, 1)
            pool.wait_ge(s_const, 3)
            nc.gpsimd.affine_select(out=ident[:], in_=ident[:], pattern=[[1, P]], compare_op=ALU.is_equal,
                                    fill=0.0, base=0, channel_multiplier=-1).then_inc(s_const, 1)
            nc.gpsimd.tensor_copy(rel[:], rel_i[:]).then_inc(s_rel, 1)
            pool.wait_ge(s_rel, 1)
            pool.wait_ge(s_w, 32)
            nc.gpsimd.tensor_tensor(bias[:], rel[:].unsqueeze(1).to_broadcast([S, NH, S]),
                                    slope[:].unsqueeze(2).to_broadcast([S, NH, S]), ALU.mult).then_inc(s_rel, 1)
            pool.wait_ge(s_rel, 2)
            nc.gpsimd.affine_select(out=bias[:], in_=bias[:], pattern=[[0, NH], [-1, S]], compare_op=ALU.is_ge,
                                    fill=LOW, base=0, channel_multiplier=1).then_inc(s_bias, 1)

            def turn(t):
                for h in range(KC):
                    pool.wait_ge(s_mx, 2 * t.i + (h + 1))
                    pool.wait_ge(s_p, 2 * t.i + (h + 1))
                    nc.gpsimd.tensor_tensor(low[:, h], sc[:, h], mx[:, h].unsqueeze(2).to_broadcast([S, HC, S]),
                                            ALU.subtract).then_inc(s_low, 1)

            turns(pool, turn, 0, 0, B, B)

        @block.scalar
        def _(act):
            act.sem_inc(s_p, 2)

            def weightsT(b, h):
                act.wait_ge(s_t, 2 * b.i + (h + 3))
                nc.scalar.copy(probT[:, h].rearrange("p (a h) s -> p a (h s)", a=2), ps_pT).then_inc(s_t_sb, 1)

            def spread(heads):
                for h in heads:
                    last = nc.scalar.activation(k_heads[:, :, h, :], ps_k, ACT.Copy, scale=in_head[:, h:h + 1])
                return last

            def weights(b, h):
                act.wait_ge(s_low, 2 * b.i + (h + 1))
                act.wait_ge(s_t, 2 * b.i + (h + 1))
                nc.scalar.activation(prob[:, h], low[:, h], ACT.Exp).then_inc(s_p, 1)

            def turn(t):
                b, nxt, far = t, t + 1, t + 2
                if b.within(B):
                    weightsT(b, 0)
                if far.within(B):
                    act.wait_ge(s_xT, far.i + 1)
                    nc.scalar.copy(xT[:], ps_xT).then_inc(s_xT_sb, 1)
                if nxt.within(B):
                    act.wait_ge(s_v, nxt.i + 1)
                    nc.scalar.copy(vals[:, nxt.parity, :, 0:HD],
                                   ps_v[0:S, 0:D].rearrange("p (h d) -> p h d", h=NH)).then_inc(s_v_sb, 1)
                if far.within(B):
                    act.wait_ge(s_k, far.i + 1)
                    spread(range(HC // 2))
                if b.within(B):
                    weightsT(b, 1)
                if far.within(B):
                    spread(range(HC // 2, HC)).then_inc(s_k_sb, 1)
                    act.wait_ge(s_q, far.i + 1)
                    nc.scalar.copy(qT[:], ps_q).then_inc(s_q_sb, 1)
                if nxt.within(B):
                    weights(nxt, 0)
                if nxt.within(B):
                    weights(nxt, 1)

            act.wait_ge(s_head, 3)
            act.wait_ge(s_const, 4)
            turns(act, turn, -2, 0, B - 2, B)

        @block.vector
        def _(dve):
            dve.sem_inc(s_att, 1)

            def turn(t):
                b, nxt, far = t, t + 1, t + 3
                if isinstance(nxt.i, int) and nxt.i == 0:
                    dve.wait_ge(s_bias, 1)
                if nxt.within(B):
                    for h in range(KC):
                        dve.wait_ge(s_s, 2 * nxt.i + (h + 1))
                        if not isinstance(nxt.i, int) or nxt.i > 0:
                            dve.wait_ge(s_low, 2 * nxt.i + (h - 1))
                        nc.vector.scalar_tensor_tensor(
                            out=sc[:, h].rearrange("p (a h) s -> p a (h s)", a=2), in0=ps_sc, scalar=SCALE,
                            in1=bias[:, h * HC:(h + 1) * HC].rearrange("p (a h) s -> p a (h s)", a=2),
                            op0=ALU.mult, op1=ALU.add).then_inc(s_sc, 1)
                        dve.wait_ge(s_sc, 2 * nxt.i + (h + 1))
                        nc.vector.reduce_max(mx[:, h], sc[:, h], AX.X).then_inc(s_mx, 1)
                if far.within(B):
                    nc.vector.tensor_scalar(xn[:, far.parity, :], at(y_nat, far.i), mean[:, bass.ds(far.i, 1)],
                                            rstd[:, bass.ds(far.i, 1)], ALU.subtract, ALU.mult).then_inc(s_xn, 1)
                    nc.vector.tensor_scalar(at(y_nat, far.i), at(y_nat, far.i), mean[:, bass.ds(far.i, 1)],
                                            rstd[:, bass.ds(far.i, 1)], ALU.subtract, ALU.mult).then_inc(s_xn_kept, 1)
                if b.within(B):
                    dve.wait_ge(s_o, b.i + 1)
                    nc.vector.reciprocal(rec[:], ps_sum[:, :, HD]).then_inc(s_rec, 1)
                    dve.wait_ge(s_rec, b.i + 1)
                    nc.vector.tensor_tensor(att[:], ps_sum[:, :, 0:HD], rec[:].unsqueeze(2).to_broadcast([S, NH, HD]),
                                            ALU.mult).then_inc(s_att, 1)
                    dve.wait_ge(s_att, b.i + 2)
                    nc.vector.tensor_tensor(at(y_nat, b.i), att[:].rearrange("p h d -> p (h d)"),
                                            at(y_nat, b.i), ALU.add).then_inc(s_sum, 1)
                    dve.wait_ge(s_sum, b.i + 1)
                    nc.vector.bn_stats(at(keep["stats"], b.i), at(y_nat, b.i)).then_inc(s_stats, 1)

            turns(dve, turn, -3, 1, B - 3, B)

        @block.tensor
        def _(pe):
            def mm(out, lhsT, rhs, k, n):
                return nc.tensor.matmul(out, lhsT, rhs, start=(k == 0), stop=(k == n - 1))

            pe.wait_ge(s_w, 32)
            pe.wait_ge(s_const, 4)
            pe.sem_inc(s_t, 2)

            def weightsT(b, h):
                pe.wait_ge(s_p, 2 * b.i + (h + 3))
                if h:
                    pe.wait_ge(s_t_sb, 2 * b.i + h)
                for n in range(HC):
                    last = nc.tensor.transpose(ps_pT[:, n // BH, (n % BH) * S:(n % BH + 1) * S], prob[:, h, n, :],
                                               ident[0:S, 0:S])
                last.then_inc(s_t, 1)

            def sums(b, h):
                pe.wait_ge(s_t_sb, 2 * b.i + (h + 1))
                for n in range(HC):
                    last = mm(ps_sum[:, h * HC + n, :], probT[:, h, n, :], vals[:, b.parity, h * HC + n, :], 0, 1)
                if h == KC - 1:
                    last.then_inc(s_o, 1)

            def scores(b, h):
                if h == 0:
                    pe.wait_ge(s_q_sb, b.i + 1)
                    pe.wait_ge(s_k_sb, b.i + 1)
                if h or not isinstance(b.i, int) or b.i > 0:
                    pe.wait_ge(s_sc, 2 * b.i + h)
                for a in range(2):
                    last = mm(ps_sc[:, a, :], qT[:, h, :],
                              k_heads[:, h, a * BH:(a + 1) * BH, :].rearrange("p h s -> p (h s)"), 0, 1)
                last.then_inc(s_s, 1)

            def project(n, out, sem):
                for c in range(KC):
                    for k in range(KC):
                        last = mm(out[:, c, :], w[:, k, n * D + c * P:n * D + (c + 1) * P], xT[:, k, :], k, KC)
                last.then_inc(sem, 1)

            def turn(t):
                b, nxt, far = t, t + 1, t + 2
                if nxt.within(B):
                    scores(nxt, 0)
                if b.within(B):
                    weightsT(b, 0)
                if nxt.within(B):
                    if not isinstance(nxt.i, int) or nxt.i > 0:
                        pe.wait_ge(s_v_sb, nxt.i)
                    for k in range(KC):
                        last = mm(ps_v[0:S, 0:D], xT[:, k, :], w[:, k, 2 * D:3 * D], k, KC)
                    last.then_inc(s_v, 1)
                if far.within(B):
                    pe.wait_ge(s_xn, far.i + 1)
                    for c in range(KC):
                        last = nc.tensor.transpose(ps_xT[:, c, :], xn[:, far.parity, c * P:(c + 1) * P], ident[0:S, 0:S])
                    last.then_inc(s_xT, 1)
                if nxt.within(B):
                    scores(nxt, 1)
                if far.within(B):
                    pe.wait_ge(s_xT_sb, far.i + 1)
                    project(0, ps_k, s_k)
                if b.within(B):
                    weightsT(b, 1)
                if far.within(B):
                    project(1, ps_q, s_q)
                if b.within(B):
                    pe.wait_ge(s_v_sb, b.i + 1)
                    pe.wait_ge(s_att, b.i + 1)
                    sums(b, 0)
                    sums(b, 1)

            turns(pe, turn, -2, 0, B - 2, B)

        finish_norm(nc, m, block, keep, s_stats)


def relative_cross(nc, io, keep):
    B, S, D = io["x"].shape
    L = io["ctx_1024"].shape[1]
    N_REL, HD = io["L1_xattn_rel_k_table"].shape
    REACH = N_REL // 2
    ND = 2 * REACH
    NH = D // HD
    KC = D // P
    HC = NH // KC
    CH = 3
    STEP = L // CH
    R = L - (CH - 1) * STEP
    NEAR = S + REACH - 1
    LEFT = S - 1 - REACH
    RW = NEAR + S - 1
    PW = REACH + NEAR
    FAR = LEFT + 1
    PAIRS = NH // 2
    SCALE = float(HD) ** -0.5
    y_nat, mean, rstd = keep["y"], keep["mean"], keep["rstd"]
    r_rows = nc.dram_tensor("rel_scores", (2, S, NH, RW), F32, kind="Internal").ap()
    p_rows = nc.dram_tensor("rel_weights", (2, S, NH, PW), F32, kind="Internal").ap()
    with ExitStack() as ctx:
        m = Names(nc, ctx, "rel")
        w = {n: m.sb(n, [P, KC, D]) for n in ("Wq", "Wk", "Wv", "Wo")}
        cols = {n: m.sb(n + "_col", [P, KC]) for n in ("bq", "bk")}
        bv = m.sb("bv", [R, D])
        bo = m.sb("bo", [S, D])
        last_v = m.sb("last_v", [R, 1, HD])
        tabT = m.sb("tabT", [P, N_REL])
        tab_diff = m.sb("tab_diff", [P, ND])
        tabT_heads = m.sb("tabT_heads", [P, HC, ND])
        tab_v = m.sb("tab_v", [P, HD])
        tab_v_last = m.sb("tab_v_last", [P, HD])
        tab_v_pair = m.sb("tab_v_pair", [P, 2, HD])
        k_bias = m.sb("k_bias", [P, KC])
        v_bias = m.sb("v_bias", [R, NH, HD])
        in_head = m.sb("in_head", [P, HC])
        beyond = m.sb("beyond", [S, FAR])
        ident = m.sb("ident", [P, P])
        zeros = m.sb("zeros", [S, NH, RW - NEAR])
        ctx_T = m.sb("ctx_T", [P, 2, KC, L])
        xn = m.sb("xn", [S, D])
        xT = m.sb("xT", [P, KC, S])
        qT = m.sb("qT", [P, KC, S])
        q_heads = m.sb("q_heads", [P, 2, KC, HC, S])
        kT = m.sb("kT", [P, 2, KC, L])
        vals = m.sb("vals", [R, 2, CH, NH, HD + 1])
        r_ext = m.sb("r_ext", [S, NH, NEAR])
        r_key = m.sb("r_key", [S, NH, NEAR])
        mx = m.sb("mx", [S, NH])
        nmx = m.sb("nmx", [S, NH])
        prob = m.sb("prob", [S, 2, NH, L])
        probT = m.sb("probT", [R, 2, CH, S])
        far = m.sb("far", [S, NH, FAR])
        by_dist = m.sb("by_dist", [S, NH, ND])
        distT = m.sb("distT", [P, PAIRS, S])
        att = m.sb("att", [S, NH, HD + 1])
        summed = m.sb("summed", [S, NH, HD])
        rec = m.sb("rec", [S, NH])
        att_n = m.sb("att_n", [S, D])
        attT = m.sb("attT", [P, KC, S])
        ps_m = m.ps("ps_m", [P, 2, 512])
        ps_s = m.ps("ps_s", [P, 2, 2, 512])
        ps_t = m.ps("ps_t", [P, 512])
        ps_o = m.ps("ps_o", [P, 512])
        ps_two, ps_k, ps_v, ps_r, ps_dT, ps_w2 = [], [], [], [], [], []
        for v in range(2):
            ps_two.append(ps_m[:, v, 0:KC * S].rearrange("p (c s) -> p c s", c=KC))
            ps_k.append(ps_m[:, v, 0:L])
            ps_v.append(ps_m[0:R, v, 0:D])
            ps_r.append(ps_m[0:S, v, 0:HC * ND])
            ps_dT.append(ps_m[:, v, 0:PAIRS // 2 * S].rearrange("p (n s) -> p n s", n=PAIRS // 2))
            ps_w2.append(ps_m[0:S, v, 0:D])
        ps_out = ps_w2
        ps_pT = ps_t[0:R, 0:CH * S].rearrange("p (c s) -> p c s", c=CH)
        ps_sum = ps_o[0:S, 0:NH * (HD + 1)].rearrange("p (h d) -> p h d", h=NH)

        sem = m.sem
        s_w, s_const, s_head, s_zero = sem("weights"), sem("constants"), sem("head_masks"), sem("zeros_in_dram")
        s_tab, s_ready = sem("table_steps"), sem("tables_ready")
        s_ctx = [sem(f"context{v}_loaded") for v in range(2)]
        s_xn = sem("rows_normalised")
        s_job = [sem(f"bank{v}_filled") for v in range(2)]
        s_job_sb = [sem(f"bank{v}_emptied") for v in range(2)]
        s_xb = sem("residual_ready")
        s_qh = sem("queries_spread")
        s_rpad = sem("distances_padded")
        s_rout, s_rkey = sem("distances_in_dram"), sem("distances_by_key")
        s_s, s_add, s_max, s_neg, s_p = (sem("scores"), sem("scores_added"), sem("maxima"), sem("maxima_scaled"),
                                         sem("weights_ready"))
        s_t, s_t_sb, s_pv, s_att = sem("weights_transposed"), sem("weightsT_stored"), sem("values_summed"), sem("sums_stored")
        s_pout, s_pdist, s_far, s_far_sum = (sem("weights_in_dram"), sem("weights_by_distance"), sem("far_masked"),
                                             sem("far_summed"))
        s_tail = sem("tail_chain")
        s_stats, s_took = sem("stats_ready"), sem("waits_taken")
        block = ctx.enter_context(nc.Block())

        JOBS = [("next", "xT"), ("next", "q"), ("next", "r0"), ("next", "r1"), ("next", "k0"), ("next", "k1"),
                ("last", "d0"), ("next", "v0"), ("last", "d1"), ("next", "v1"), ("last", "w2"), ("next", "v2"),
                ("last", "aT"), ("last", "out")]
        SLOTS = [(0,), (1,), (2, 3), (4, 5), (6, 7), (8, 9), (10, 11), (12, 13)]
        NUMBER = {what: n for n, (_, what) in enumerate(JOBS)}

        def share(v, n, *kinds):
            return sum(k % 2 == v and who in kinds for k, (who, _) in enumerate(JOBS[:n]))

        def before(t, n):
            v, nj = n % 2, len(JOBS)
            nexts = share(v, nj, "next")
            if isinstance(t.i, int) and t.i <= 0:
                return (t.i + 1) * nexts + share(v, n, "next")
            if isinstance(t.i, int) and t.i >= B - 1:
                return (2 * nexts + (B - 2) * share(v, nj, "next", "last")
                        + (t.i - (B - 1)) * share(v, nj, "last") + share(v, n, "last"))
            return 2 * nexts + (t.i - 1) * share(v, nj, "next", "last") + share(v, n, "next", "last")

        def wait_filled(eng, t, what):
            n = NUMBER[what]
            eng.wait_ge(s_job[n % 2], before(t, n) + 1)

        def wait_emptied(eng, t, what):
            n = NUMBER[what]
            eng.wait_ge(s_job_sb[n % 2], before(t, n) + 1)

        def jobs(t, slot):
            for n in SLOTS[slot]:
                who, what = JOBS[n]
                b = t + 1 if who == "next" else t + -1
                if b.within(B):
                    yield n, what, b

        @block.sync
        def _(sp):
            for n, tile in w.items():
                sp.dma_start(tile[:], io["L1_xattn_" + n].rearrange("(c p) d -> p c d", p=P)).then_inc(s_w, 16)
            for n, tile in cols.items():
                sp.dma_start(tile[:], io[f"L1_xattn_{n}_cols"]).then_inc(s_w, 16)
            sp.dma_start(bv[:], io["L1_xattn_bv"].partition_broadcast(R)).then_inc(s_w, 16)
            sp.dma_start(bo[:], io["L1_xattn_bo"].partition_broadcast(S)).then_inc(s_w, 16)
            sp.dma_start(last_v[:, 0, :], io["L1_xattn_rel_v_table"][N_REL - 1].partition_broadcast(R)).then_inc(s_w, 16)
            sp.dma_start(tab_v_last[:], io["L1_xattn_rel_v_table"][N_REL - 1].partition_broadcast(P)).then_inc(s_w, 16)
            for h in range(HC):
                sp.dma_start(tabT[h * HD:(h + 1) * HD, :], io["L1_xattn_rel_k_tableT"]).then_inc(s_w, 16)
            for h in range(2):
                sp.dma_start(tab_v[h * ND:(h + 1) * ND, :], io["L1_xattn_rel_v_table"][0:ND]).then_inc(s_w, 16)
            sp.wait_ge(s_const, 4)
            for v in range(2):
                sp.dma_start(r_rows[v, :, :, NEAR:RW], zeros[:]).then_inc(s_zero, 16)
                sp.dma_start(p_rows[v, :, :, 0:REACH], zeros[:, :, 0:REACH]).then_inc(s_zero, 16)
            sp.wait_ge(s_zero, 64)

            def turn(t):
                b, nxt, prev = t, t + 1, t + -1
                if nxt.within(B):
                    if not isinstance(nxt.i, int) or nxt.i > 1:
                        wait_filled(sp, t + -2, "v2")
                    sp.sem_inc(s_took, 1)
                    sp.dma_start(ctx_T[:, nxt.parity], io["ctxT"].rearrange("b (c p) l -> p b c l", p=P)[
                        :, bass.ds(nxt.i, 1)].rearrange("p b c l -> p (b c) l")).then_inc(s_ctx[nxt.parity], 16)
                if prev.within(B):
                    v = prev.parity
                    sp.wait_ge(s_p, PAIRS * prev.i + (PAIRS + 2))
                    sp.dma_start(p_rows[v, :, :, REACH:PW], prob[:, v, :, 0:NEAR]).then_inc(s_pout, 16)
                    sp.wait_ge(s_pout, 16 * prev.i + 16)
                    sp.sem_inc(s_took, 1)
                    if not isinstance(prev.i, int) or prev.i > 0:
                        wait_filled(sp, t + -1, "d1")
                    sp.dma_start(by_dist[:], bass.AP(p_rows.tensor, p_rows[v].offset,
                                                     [[NH * PW + 1, S], [PW, NH], [1, ND]])).then_inc(s_pdist, 16)
                if nxt.within(B):
                    v = nxt.parity
                    sp.wait_ge(s_rpad, nxt.i + 1)
                    sp.dma_start(r_rows[v, :, :, 0:NEAR], r_ext[:]).then_inc(s_rout, 16)
                    sp.wait_ge(s_rout, 16 * nxt.i + 16)
                    sp.sem_inc(s_took, 1)
                    if not isinstance(nxt.i, int) or nxt.i > 0:
                        sp.wait_ge(s_add, PAIRS * nxt.i)
                    sp.dma_start(r_key[:], bass.AP(r_rows.tensor, r_rows[v].offset + (S - 1),
                                                   [[NH * RW - 1, S], [RW, NH], [1, NEAR]])).then_inc(s_rkey, 16)

            turns(sp, turn, -1, 3, B - 1, B + 1)

        @block.gpsimd
        def _(pool):
            head_masks(nc, pool, in_head, s_head)
            nc.gpsimd.memset(ident[:], 1.0).then_inc(s_const, 1)
            nc.gpsimd.memset(beyond[:], 1.0).then_inc(s_const, 1)
            nc.gpsimd.memset(zeros[:], 0.0).then_inc(s_const, 1)
            nc.gpsimd.memset(vals[:, :, :, :, HD:HD + 1], 1.0).then_inc(s_const, 1)
            nc.gpsimd.memset(tab_v_pair[:], 0.0).then_inc(s_const, 1)
            pool.wait_ge(s_const, 5)
            nc.gpsimd.affine_select(out=ident[:], in_=ident[:], pattern=[[1, P]], compare_op=ALU.is_equal,
                                    fill=0.0, base=0, channel_multiplier=-1).then_inc(s_const, 1)
            nc.gpsimd.affine_select(out=beyond[:], in_=beyond[:], pattern=[[-1, FAR]], compare_op=ALU.is_ge,
                                    fill=0.0, base=-REACH, channel_multiplier=1).then_inc(s_const, 1)
            pool.wait_ge(s_ready, 1)

            def turn(t):
                nxt, prev = t + 1, t + -1
                if prev.within(B):
                    pool.wait_ge(s_p, PAIRS * prev.i + (PAIRS + 2))
                    if not isinstance(prev.i, int) or prev.i > 0:
                        pool.wait_ge(s_far_sum, prev.i)
                    nc.gpsimd.tensor_tensor(far[:], prob[:, prev.parity, :, 0:FAR],
                                            beyond[:].unsqueeze(1).to_broadcast([S, NH, FAR]), ALU.mult).then_inc(s_far, 1)
                if nxt.within(B):
                    wait_emptied(pool, t, "r1")
                    nc.gpsimd.tensor_tensor(q_heads[:, nxt.parity], qT[:].unsqueeze(2).to_broadcast([P, KC, HC, S]),
                                            in_head[:].unsqueeze(1).unsqueeze(3).to_broadcast([P, KC, HC, S]),
                                            ALU.mult).then_inc(s_qh, 1)
                    nc.gpsimd.tensor_copy(r_ext[:, :, 0:LEFT], r_ext[:, :, LEFT:LEFT + 1].to_broadcast([S, NH, LEFT])
                                          ).then_inc(s_rpad, 1)
                    pool.wait_ge(s_xn, nxt.i + 1)
                    pool.sem_inc(s_took, 1)
                    nc.gpsimd.tensor_tensor(at(y_nat, nxt.i), xn[:], bo[:], ALU.add).then_inc(s_xb, 1)

            turns(pool, turn, -1, 3, B - 1, B + 1)

        ON_ACT = ("xT", "r0", "r1", "k0", "k1", "aT")

        @block.scalar
        def _(act):
            act.wait_ge(s_ready, 1)
            act.sem_inc(s_p, 2)

            def empty(t, n, what, b):
                bank = n % 2
                wait_filled(act, t, what)
                if what == "xT":
                    nc.scalar.copy(xT[:], ps_two[bank]).then_inc(s_job_sb[bank], 1)
                elif what in ("r0", "r1"):
                    h = int(what[1])
                    if h == 0 and (not isinstance(b.i, int) or b.i > 0):
                        act.wait_ge(s_rout, 16 * b.i)
                    nc.scalar.copy(r_ext[:, h * HC:(h + 1) * HC, LEFT:NEAR],
                                   ps_r[bank].rearrange("p (h r) -> p h r", h=HC)).then_inc(s_job_sb[bank], 1)
                elif what in ("k0", "k1"):
                    c = int(what[1])
                    nc.scalar.activation(kT[:, b.parity, c, :], ps_k[bank], ACT.Identity,
                                         bias=k_bias[:, c:c + 1]).then_inc(s_job_sb[bank], 1)
                else:
                    nc.scalar.copy(attT[:], ps_two[bank]).then_inc(s_job_sb[bank], 1)

            def turn(t):
                for n in range(PAIRS):
                    et, en = (t, n - 1) if n >= 1 else (t + -1, PAIRS - 1)
                    pt, pn = (t, n - 2) if n >= 2 else (t + -1, n + PAIRS - 2)
                    g = PAIRS * pt.i + pn

                    def transposed(h):
                        act.wait_ge(s_t, 2 * g + (h + 1))
                        if h == 0 and (not isinstance(g, int) or g > 0):
                            act.wait_ge(s_pv, g)
                        nc.scalar.copy(probT[:, h], ps_pT).then_inc(s_t_sb, 1)

                    if pt.within(B):
                        transposed(0)
                    if et.within(B):
                        act.wait_ge(s_neg, PAIRS * et.i + (en + 1))
                        if en == 0 and (not isinstance(et.i, int) or et.i > 1):
                            act.wait_ge(s_pout, 16 * (et.i - 1))
                            act.wait_ge(s_far, et.i - 1)
                        for h in range(2):
                            last = nc.scalar.activation(prob[:, et.parity, 2 * en + h, :], ps_s[0:S, en % 2, h, 0:L], ACT.Exp,
                                                        bias=nmx[:, 2 * en + h:2 * en + h + 1], scale=SCALE)
                        last.then_inc(s_p, 1)
                    if pt.within(B):
                        transposed(1)
                    for k, what, b in jobs(t, n):
                        if what in ON_ACT:
                            empty(t, k, what, b)

            turns(act, turn, -1, 3, B - 1, B + 1)

        @block.vector
        def _(dve):
            tab = Chain(dve, s_tab, 6)
            tab.start(0)
            dve.wait_ge(s_w, 16 * (4 + 2 + 4 + HC + 2))
            dve.wait_ge(s_head, 3)
            dve.wait_ge(s_const, 7)
            nc.vector.tensor_scalar(k_bias[:], cols["bk"][:], tabT[:, ND:ND + 1], None, ALU.add)
            tab(nc.vector.tensor_scalar(tab_diff[:], tabT[:, 0:ND], tabT[:, ND:ND + 1], None, ALU.subtract))
            tab(nc.vector.tensor_tensor(tabT_heads[:], tab_diff[:].unsqueeze(1).to_broadcast([P, HC, ND]),
                                        in_head[:].unsqueeze(2).to_broadcast([P, HC, ND]), ALU.mult))
            tab(nc.vector.tensor_tensor(v_bias[:], bv[:].rearrange("p (h d) -> p h d", h=NH),
                                        last_v[:, 0:1, :].to_broadcast([R, NH, HD]), ALU.add))
            tab(nc.vector.tensor_tensor(tab_v[:], tab_v[:], tab_v_last[:], ALU.subtract))
            tab(nc.vector.tensor_copy(tab_v_pair[0:ND, 0, :], tab_v[0:ND, :]))
            tab(nc.vector.tensor_copy(tab_v_pair[ND:2 * ND, 1, :], tab_v[ND:2 * ND, :]))
            dve.sem_inc(s_ready, 1)
            tail = Chain(dve, s_tail, 2)

            def empty(t, n, what, b):
                bank = n % 2
                wait_filled(dve, t, what)
                if what == "q":
                    nc.vector.tensor_tensor(qT[:], ps_two[bank], cols["bq"][:].unsqueeze(2).to_broadcast([P, KC, S]),
                                            ALU.add).then_inc(s_job_sb[bank], 1)
                elif what in ("v0", "v1", "v2"):
                    c = int(what[1])
                    nc.vector.tensor_tensor(vals[:, b.parity, c, :, 0:HD], ps_v[bank].rearrange("p (h d) -> p h d", h=NH),
                                            v_bias[:], ALU.add).then_inc(s_job_sb[bank], 1)
                elif what in ("d0", "d1"):
                    h = int(what[1])
                    nc.vector.tensor_copy(distT[:, h * PAIRS // 2:(h + 1) * PAIRS // 2, :], ps_dT[bank]).then_inc(s_job_sb[bank], 1)
                elif what == "w2":
                    tail.start(b.i)
                    tail(nc.vector.reciprocal(rec[:], att[:, :, HD]))
                    nc.vector.tensor_tensor(summed[:], ps_w2[bank].rearrange("p (h d) -> p h d", h=NH), att[:, :, 0:HD],
                                            ALU.add).then_inc(s_job_sb[bank], 1)
                    wait_emptied(dve, t, what)
                    tail(nc.vector.tensor_tensor(att_n[:].rearrange("p (h d) -> p h d", h=NH), summed[:],
                                                 rec[:].unsqueeze(2).to_broadcast([S, NH, HD]), ALU.mult))
                elif what == "out":
                    dve.wait_ge(s_xb, b.i + 1)
                    nc.vector.tensor_tensor(at(y_nat, b.i), ps_out[bank], at(y_nat, b.i), ALU.add).then_inc(s_job_sb[bank], 1)
                    wait_emptied(dve, t, what)
                    nc.vector.bn_stats(at(keep["stats"], b.i), at(y_nat, b.i)).then_inc(s_stats, 1)
                    tail.end()

            def turn(t):
                nxt, prev = t + 1, t + -1
                for n in range(PAIRS):
                    if n == 0 and nxt.within(B):
                        if not isinstance(nxt.i, int) or nxt.i > 0:
                            dve.wait_ge(s_xb, nxt.i)
                        nc.vector.tensor_scalar(xn[:], at(y_nat, nxt.i), mean[:, bass.ds(nxt.i, 1)],
                                                rstd[:, bass.ds(nxt.i, 1)], ALU.subtract, ALU.mult).then_inc(s_xn, 1)
                    if t.within(B):
                        g = PAIRS * t.i + n
                        bank = ps_s[0:S, n % 2]
                        two = slice(2 * n, 2 * n + 2)
                        if n == 0:
                            dve.wait_ge(s_rkey, 16 * t.i + 16)
                        dve.wait_ge(s_s, g + 1)
                        nc.vector.tensor_tensor(bank[:, :, 0:NEAR], bank[:, :, 0:NEAR], r_key[:, two, :],
                                                ALU.add).then_inc(s_add, 1)
                        dve.wait_ge(s_add, g + 1)
                        nc.vector.reduce_max(mx[:, two], bank[:, :, 0:L], AX.X).then_inc(s_max, 1)
                        dve.wait_ge(s_max, g + 1)
                        nc.vector.tensor_scalar(nmx[:, two], mx[:, two], -SCALE, None, ALU.mult).then_inc(s_neg, 1)
                    if n == 1 and prev.within(B):
                        dve.wait_ge(s_pv, PAIRS * prev.i + PAIRS)
                        nc.vector.tensor_copy(att[:], ps_sum).then_inc(s_att, 1)
                    if n == 3 and prev.within(B):
                        dve.wait_ge(s_far, prev.i + 1)
                        dve.wait_ge(s_pdist, 16 * prev.i + 16)
                        nc.vector.reduce_sum(by_dist[:, :, 0], far[:], AX.X).then_inc(s_far_sum, 1)
                    for k, what, b in jobs(t, n):
                        if what not in ON_ACT:
                            empty(t, k, what, b)

            turns(dve, turn, -1, 3, B - 1, B + 1)

        @block.tensor
        def _(pe):
            def mm(out, lhsT, rhs, k, n):
                return nc.tensor.matmul(out, lhsT, rhs, start=(k == 0), stop=(k == n - 1))

            pe.wait_ge(s_ready, 1)

            def fill(t, n, what, b):
                bank = n % 2
                o = before(t, n)
                if not isinstance(o, int) or o > 0:
                    pe.wait_ge(s_job_sb[bank], o)
                if what == "xT":
                    pe.wait_ge(s_xn, b.i + 1)
                    for c in range(KC):
                        last = nc.tensor.transpose(ps_two[bank][:, c, :], xn[:, c * P:(c + 1) * P], ident[0:S, 0:S])
                elif what == "q":
                    wait_emptied(pe, t, "xT")
                    for c in range(KC):
                        for k in range(KC):
                            last = mm(ps_two[bank][:, c, :], w["Wq"][:, k, c * P:(c + 1) * P], xT[:, k, :], k, KC)
                elif what in ("r0", "r1"):
                    if what == "r0":
                        wait_emptied(pe, t, "q")
                    last = mm(ps_r[bank], qT[:, int(what[1]), :], tabT_heads[:].rearrange("p h r -> p (h r)"), 0, 1)
                elif what in ("k0", "k1"):
                    c = int(what[1])
                    if c == 0:
                        pe.wait_ge(s_ctx[b.parity], 16 * b.half + 16)
                    for k in range(KC):
                        last = mm(ps_k[bank], w["Wk"][:, k, c * P:(c + 1) * P], ctx_T[:, b.parity, k, :], k, KC)
                elif what in ("v0", "v1", "v2"):
                    c = int(what[1])
                    for k in range(KC):
                        last = mm(ps_v[bank], ctx_T[:, b.parity, k, c * STEP:c * STEP + R], w["Wv"][:, k, :], k, KC)
                elif what in ("d0", "d1"):
                    h = int(what[1])
                    pe.wait_ge(s_far_sum, b.i + 1)
                    for k in range(PAIRS // 2):
                        p = h * (PAIRS // 2) + k
                        last = nc.tensor.transpose(ps_dT[bank][:, k, :], by_dist[:, 2 * p:2 * p + 2, :].rearrange("p h r -> p (h r)"),
                                                   ident[0:S, 0:S])
                elif what == "w2":
                    for p in range(PAIRS):
                        last = mm(ps_w2[bank][:, p * 2 * HD:(p + 1) * 2 * HD], distT[:, p, :],
                                  tab_v_pair[:].rearrange("p h d -> p (h d)"), 0, 1)
                elif what == "aT":
                    pe.wait_ge(s_tail, 2 * b.i + 2)
                    for c in range(KC):
                        last = nc.tensor.transpose(ps_two[bank][:, c, :], att_n[:, c * P:(c + 1) * P], ident[0:S, 0:S])
                else:
                    wait_emptied(pe, t, "aT")
                    for k in range(KC):
                        last = mm(ps_out[bank], attT[:, k, :], w["Wo"][:, k, :], k, KC)
                last.then_inc(s_job[bank], 1)

            def turn(t):
                if t.within(B):
                    for what in ("k0", "v2"):
                        wait_emptied(pe, t + -1, what)
                for n in range(PAIRS):
                    todo = list(jobs(t, n))
                    pt, pn = (t, n - 2) if n >= 2 else (t + -1, n + PAIRS - 2)
                    g = PAIRS * pt.i + pn
                    for h in range(2):
                        if pt.within(B):
                            if h == 0:
                                pe.wait_ge(s_p, g + 3)
                            if not isinstance(g, int) or g + h > 0:
                                pe.wait_ge(s_t_sb, 2 * g + h)
                            for c in range(CH):
                                last = nc.tensor.transpose(ps_pT[:, c, :], prob[:, pt.parity, 2 * pn + h, c * STEP:c * STEP + R],
                                                           ident[0:S, 0:S])
                            last.then_inc(s_t, 1)
                        if t.within(B):
                            if h == 0:
                                pe.wait_ge(s_p, PAIRS * t.i + (n + 1))
                                if n == 0:
                                    pe.wait_ge(s_qh, t.i + 1)
                            head = 2 * n + h
                            last = mm(ps_s[0:S, n % 2, h, 0:L], q_heads[:, t.parity, head // HC, head % HC, :],
                                      kT[:, t.parity, head // HC, :], 0, 1)
                            if h == 1:
                                last.then_inc(s_s, 1)
                    for k, what, b in todo[:1]:
                        fill(t, k, what, b)
                    if pt.within(B):
                        pe.wait_ge(s_t_sb, 2 * g + 2)
                        if pn == 0 and (not isinstance(pt.i, int) or pt.i > 0):
                            pe.wait_ge(s_att, pt.i)
                        for h in range(2):
                            for c in range(CH):
                                r = R if c == CH - 1 else STEP
                                last = mm(ps_sum[:, 2 * pn + h, :], probT[0:r, h, c, :],
                                          vals[0:r, pt.parity, c, 2 * pn + h, :], c, CH)
                        last.then_inc(s_pv, 1)
                    for k, what, b in todo[1:]:
                        fill(t, k, what, b)

            turns(pe, turn, -1, 3, B - 1, B + 1)

        finish_norm(nc, m, block, keep, s_stats)


QMAX = 2.0 ** 15 - 1.0


def global_scale(nc, m, block, maxima, n_sem, sem_done, parts, scale, inverse, tag):
    top = m.sb(f"{tag}_top", [parts, 1])
    all_top = m.sb(f"{tag}_all_top", [parts, 1])
    s_top, s_all, s_scale, s_inv = (m.sem(f"{tag}_{n}") for n in ("top", "all_top", "scaled", "inverted"))

    @block.vector
    def _(dve):
        dve.wait_ge(sem_done, n_sem)
        nc.vector.reduce_max(top[:], maxima, AX.X).then_inc(s_top, 1)
        dve.wait_ge(s_all, 1)
        nc.vector.tensor_scalar(scale, all_top[:], 1.0 / QMAX, TINY, ALU.mult, ALU.max).then_inc(s_scale, 1)
        dve.wait_ge(s_scale, 1)
        nc.vector.reciprocal(inverse, scale).then_inc(s_inv, 1)
        dve.wait_ge(s_inv, 1)

    @block.gpsimd
    def _(pool):
        pool.wait_ge(s_top, 1)
        nc.gpsimd.partition_all_reduce(all_top[:], top[:], parts, bass.bass_isa.ReduceOp.max).then_inc(s_all, 1)


def quantised_ffn(nc, io, keep):
    B, S, D = io["x"].shape
    I = io["L1_ffn_w_up"].shape[0]
    BLOCK = 32
    KC, IC = D // P, I // P
    G = 4
    GROUPS = B // G
    N = G * S
    y_nat, mean, rstd = keep["y"], keep["mean"], keep["rstd"]
    up_rows = nc.dram_tensor("ffn_up", (GROUPS, P, IC, N), F32, kind="Internal").ap()
    with ExitStack() as outer:
        o = Names(nc, outer, "ffn")
        ident = o.sb("ident", [P, P])
        w_inT = o.sb("w_inT", [P, 2, KC, I])
        w_dT = o.sb("w_dT", [P, IC, D])
        scales = o.sb("scales", [P, 10])
        gate = o.sb("gate", [P, GROUPS, IC, N])
        x_scale, x_inv = scales[0:S, 0:1], scales[0:S, 1:2]
        (u_scale, u_inv), (g_scale, g_inv), (a_scale, a_inv), (o_scale, o_inv) = (
            (scales[:, 2 * n:2 * n + 1], scales[:, 2 * n + 1:2 * n + 2]) for n in range(1, 5))

        with ExitStack() as ctx:
            m = Names(nc, ctx, "ffw")
            w_in = m.sb("w_in", [P, 2, IC, D])
            w_d = m.sb("w_d", [P, KC, I])
            flat = [w_in[:, 0].rearrange("p c d -> p (c d)"), w_in[:, 1].rearrange("p c d -> p (c d)"),
                    w_d[:].rearrange("p c d -> p (c d)")]
            NB = I * D // P // BLOCK
            top = m.sb("top", [P, 3, NB])
            step_ = m.sb("step", [P, 3, NB])
            inv = m.sb("inv", [P, 3, NB])
            row_top = m.sb("row_top", [S, GROUPS])
            shift = m.sb("shift", [S, B])
            ps = m.ps("ps", [P, 4, 512])
            s_w = [m.sem(f"weights{n}_loaded") for n in range(3)]
            s_const, s_q, s_t, s_t_sb = m.sem("constants"), m.sem("quantised"), m.sem("transposed"), m.sem("stored")
            s_wq = m.sem("weights_ready")
            s_shift, s_x, s_top = m.sem("shift"), m.sem("rows_normalised"), m.sem("row_maxima")
            block = ctx.enter_context(nc.Block())

            @block.sync
            def _(sp):
                sp.dma_start(w_in[:, 0], io["L1_ffn_w_up"].rearrange("(c p) d -> p c d", p=P)).then_inc(s_w[0], 16)
                sp.dma_start(w_in[:, 1], io["L1_ffn_w_gate"].rearrange("(c p) d -> p c d", p=P)).then_inc(s_w[1], 16)
                sp.dma_start(w_d[:], io["L1_ffn_w_down"].rearrange("(c p) d -> p c d", p=P)).then_inc(s_w[2], 16)

            @block.gpsimd
            def _(pool):
                nc.gpsimd.memset(ident[:], 1.0).then_inc(s_const, 1)
                pool.wait_ge(s_const, 1)
                nc.gpsimd.affine_select(out=ident[:], in_=ident[:], pattern=[[1, P]], compare_op=ALU.is_equal,
                                        fill=0.0, base=0, channel_multiplier=-1).then_inc(s_const, 1)

            @block.vector
            def _(dve):
                nc.vector.scalar_tensor_tensor(out=shift[:], in0=mean[:], scalar=-1.0, in1=rstd[:],
                                               op0=ALU.mult, op1=ALU.mult).then_inc(s_shift, 1)
                q = Chain(dve, s_q, 15)
                q.start(0)
                for n in range(3):
                    dve.wait_ge(s_w[n], 16)
                    blocks = flat[n].rearrange("p (b k) -> p b k", k=BLOCK)
                    wide = lambda x: x[:, n].unsqueeze(2).to_broadcast([P, NB, BLOCK])
                    q(nc.vector.tensor_reduce(top[:, n], blocks, AX.X, ALU.max, apply_absolute_value=True))
                    q(nc.vector.tensor_scalar(step_[:, n], top[:, n], 1.0 / 7.0, TINY, ALU.mult, ALU.max))
                    q(nc.vector.reciprocal(inv[:, n], step_[:, n]))
                    q(nc.vector.tensor_tensor(blocks, blocks, wide(inv), ALU.mult))
                    q(nc.vector.tensor_scalar(blocks, blocks, ROUND, ROUND, ALU.add, ALU.subtract))
                    nc.vector.tensor_tensor(blocks, blocks, wide(step_), ALU.mult).then_inc(s_wq, 1)

                def largest(t):
                    dve.wait_ge(s_x, t.i * G + G)
                    nc.vector.tensor_reduce(row_top[:, bass.ds(t.i, 1)], y_nat[:, bass.ds(t.i * G, G), :], AX.XY, ALU.max,
                                            apply_absolute_value=True).then_inc(s_top, 1)

                turns(dve, largest, 0, 0, GROUPS, GROUPS)

            def transposes():
                for n in range(2):
                    for k in range(KC):
                        for c0 in range(0, IC, 4):
                            cs = range(c0, min(c0 + 4, IC))
                            yield n, [w_in[:, n, c, k * P:(k + 1) * P] for c in cs], w_inT[:, n, k, c0 * P:(cs[-1] + 1) * P]
                for c in range(0, IC, 2):
                    yield 2, [w_d[:, k, (c + e) * P:(c + e + 1) * P] for e in range(2) for k in range(KC)], \
                        w_dT[:, c:c + 2, :].rearrange("p e d -> p (e d)")

            @block.tensor
            def _(pe):
                pe.wait_ge(s_const, 2)
                for i, (n, tiles, _) in enumerate(transposes()):
                    pe.wait_ge(s_wq, n + 1)
                    if i >= 4:
                        pe.wait_ge(s_t_sb, i - 3)
                    for e, tile in enumerate(tiles):
                        last = nc.tensor.transpose(ps[:, i % 4, e * P:(e + 1) * P], tile, ident[:])
                    last.then_inc(s_t, 1)

            @block.scalar
            def _(act):
                act.wait_ge(s_shift, 1)
                with act.Fori(0, GROUPS) as g:
                    for q in range(G):
                        b = g * G + q
                        nc.scalar.activation(at(y_nat, b), at(y_nat, b), ACT.Identity, bias=shift[:, bass.ds(b, 1)],
                                             scale=rstd[:, bass.ds(b, 1)]).then_inc(s_x, 1)
                for i, (n, tiles, out) in enumerate(transposes()):
                    act.wait_ge(s_t, i + 1)
                    nc.scalar.copy(out, ps[:, i % 4, 0:len(tiles) * P]).then_inc(s_t_sb, 1)

            global_scale(nc, m, block, row_top[:], GROUPS, s_top, S, x_scale, x_inv, "x")

        with ExitStack() as ctx:
            m = Names(nc, ctx, "ffp")
            xr = m.sb("xr", [S, G, D])
            xq = m.sb("xq", [S, 2, G, D])
            xqT = m.sb("xqT", [P, 2, KC, N])
            up = m.sb("up", [P, 2, IC, N])
            tops = m.sb("tops", [P, 2, GROUPS, IC])
            ps_x = m.ps("ps_x", [P, 2, 512])
            ps_h = m.ps("ps_h", [P, 4, 512])
            s_r, s_q, s_t, s_t_sb = m.sem("rounded"), m.sem("quantised"), m.sem("transposed"), m.sem("xT_stored")
            s_h, s_top, s_h_sb = m.sem("hidden"), m.sem("maxima"), m.sem("hidden_stored")
            s_up = [m.sem(f"up{v}_in_dram") for v in range(2)]
            block = ctx.enter_context(nc.Block())
            NH = 2 * IC
            MIDDLE = IC // 2

            @block.vector
            def _(dve):
                def quantise(t):
                    rows = y_nat[:, bass.ds(t.i * G, G), :]
                    if not isinstance(t.i, int) or t.i > 0:
                        dve.wait_ge(s_q, t.i)
                    nc.vector.tensor_scalar(xr[:], rows, x_inv, ROUND, ALU.mult, ALU.add).then_inc(s_r, 1)
                    dve.wait_ge(s_r, t.i + 1)
                    if not isinstance(t.i, int) or t.i > 1:
                        dve.wait_ge(s_t, KC * (t.i - 1))
                    nc.vector.tensor_scalar(xq[:, t.parity], xr[:], ROUND, x_scale, ALU.subtract, ALU.mult).then_inc(s_q, 1)

                def turn(t):
                    if not t.within(GROUPS):
                        quantise(t + 1)
                    if t.within(GROUPS):
                        for n in range(NH):
                            if n == MIDDLE and (t + 1).within(GROUPS):
                                quantise(t + 1)
                            k, c = n // IC, n % IC
                            dve.wait_ge(s_h_sb, NH * t.i + (n + 1))
                            nc.vector.tensor_reduce(at(tops[:, k], t.i)[:, c:c + 1], ps_h[:, n % 4, 0:N], AX.X, ALU.max,
                                                    apply_absolute_value=True).then_inc(s_top, 1)

                turns(dve, turn, -1, 1, GROUPS - 1, GROUPS)

            @block.scalar
            def _(act):
                def storeT(t):
                    for c in range(KC):
                        act.wait_ge(s_t, KC * t.i + (c + 1))
                        nc.scalar.copy(xqT[:, t.parity, c, :], ps_x[:, c, 0:N]).then_inc(s_t_sb, 1)

                def turn(t):
                    if not t.within(GROUPS):
                        storeT(t + 1)
                    if t.within(GROUPS):
                        for n in range(NH):
                            if n == MIDDLE + 4 and (t + 1).within(GROUPS):
                                storeT(t + 1)
                            k, c = n // IC, n % IC
                            act.wait_ge(s_h, NH * t.i + (n + 1))
                            if n == 0 and (not isinstance(t.i, int) or t.i > 1):
                                act.wait_ge(s_up[t.parity], 16 * t.half)
                            out = up[:, t.parity, c, :] if k == 0 else gate[:, bass.ds(t.i, 1), c, :].rearrange("p a n -> p (a n)")
                            nc.scalar.copy(out, ps_h[:, n % 4, 0:N]).then_inc(s_h_sb, 1)

                turns(act, turn, -1, 1, GROUPS - 1, GROUPS)

            @block.sync
            def _(sp):
                def turn(t):
                    sp.wait_ge(s_h_sb, NH * t.i + IC)
                    sp.dma_start(up_rows[bass.ds(t.i, 1)].rearrange("g p c n -> p (g c) n"), up[:, t.parity]).then_inc(s_up[t.parity], 16)

                turns(sp, turn, 0, 0, GROUPS, GROUPS)
                for v in range(2):
                    sp.wait_ge(s_up[v], 16 * GROUPS // 2)

            @block.tensor
            def _(pe):
                def rowsT(t):
                    pe.wait_ge(s_q, t.i + 1)
                    if not isinstance(t.i, int) or t.i > 0:
                        pe.wait_ge(s_t_sb, KC * t.i)
                    for c in range(KC):
                        for q in range(G):
                            last = nc.tensor.transpose(ps_x[:, c, q * S:(q + 1) * S], xq[:, t.parity, q, c * P:(c + 1) * P],
                                                       ident[0:S, 0:S])
                        last.then_inc(s_t, 1)

                def turn(t):
                    if not t.within(GROUPS):
                        rowsT(t + 1)
                    if t.within(GROUPS):
                        pe.wait_ge(s_t_sb, KC * t.i + KC)
                        for n in range(NH):
                            if n == MIDDLE + 4 and (t + 1).within(GROUPS):
                                rowsT(t + 1)
                            k, c = n // IC, n % IC
                            if not isinstance(t.i, int) or NH * t.i + n >= 4:
                                pe.wait_ge(s_top, (t.i - 1) * NH + (n + NH - 3))
                            for j in range(KC):
                                last = nc.tensor.matmul(ps_h[:, n % 4, 0:N], w_inT[:, k, j, c * P:(c + 1) * P],
                                                        xqT[:, t.parity, j, :], start=(j == 0), stop=(j == KC - 1))
                            last.then_inc(s_h, 1)

                turns(pe, turn, -1, 1, GROUPS - 1, GROUPS)

            global_scale(nc, m, block, tops[:, 0].rearrange("p g c -> p (g c)"), NH * GROUPS, s_top, P, u_scale, u_inv, "u")
            global_scale(nc, m, block, tops[:, 1].rearrange("p g c -> p (g c)"), NH * GROUPS, s_top, P, g_scale, g_inv, "g")

        with ExitStack() as ctx:
            m = Names(nc, ctx, "ffs")
            rounded = m.sb("rounded", [P, 2, IC, N])
            gate_q = m.sb("gate_q", [P, 2, IC, N])
            sig = m.sb("sig", [P, 2, IC, N])
            tops = m.sb("tops", [P, GROUPS])
            consts = m.sb("consts", [P, 3])
            s_const = m.sem("constants")
            s_r, s_q, s_s, s_sr, s_sq = (m.sem(n) for n in (
                "rounded", "quantised", "sigmoids", "sigmoids_rounded", "sigmoids_clipped"))
            s_g, s_top = m.sem("gated"), m.sem("maxima")
            block = ctx.enter_context(nc.Block())
            ROUND_16 = ROUND / 65536.0
            MOST = 65535.0 / 65536.0

            @block.scalar
            def _(act):
                act.wait_ge(s_const, 3)

                def turn(t):
                    nxt, v = t + 1, t.parity
                    if t.within(GROUPS):
                        act.wait_ge(s_q, t.i + 1)
                        if not isinstance(t.i, int) or t.i > 1:
                            act.wait_ge(s_g, t.i - 1)
                        nc.scalar.activation(sig[:, v], gate_q[:, v], ACT.Sigmoid).then_inc(s_s, 1)
                    if nxt.within(GROUPS):
                        nc.scalar.activation(rounded[:, nxt.parity], gate[:, bass.ds(nxt.i, 1)].rearrange("p a c n -> p (a c) n"),
                                             ACT.Identity, bias=consts[:, 0:1], scale=g_inv).then_inc(s_r, 1)
                    if t.within(GROUPS):
                        act.wait_ge(s_s, t.i + 1)
                        nc.scalar.activation(sig[:, v], sig[:, v], ACT.Identity, bias=consts[:, 1:2]).then_inc(s_sr, 1)
                        act.wait_ge(s_sr, t.i + 1)
                        nc.scalar.activation(sig[:, v], sig[:, v], ACT.Relu, bias=consts[:, 2:3], scale=-1.0).then_inc(s_sq, 1)

                turns(act, turn, -1, 1, GROUPS - 1, GROUPS)

            @block.vector
            def _(dve):
                for n, value in enumerate((ROUND, ROUND_16, ROUND_16 + MOST)):
                    nc.vector.memset(consts[:, n:n + 1], value).then_inc(s_const, 1)

                def quantise(t):
                    dve.wait_ge(s_r, t.i + 1)
                    nc.vector.tensor_scalar(gate_q[:, t.parity], rounded[:, t.parity], ROUND, g_scale,
                                            ALU.subtract, ALU.mult).then_inc(s_q, 1)

                def turn(t):
                    v = t.parity
                    if (t + 1).within(GROUPS):
                        quantise(t + 1)
                    if t.within(GROUPS):
                        here = gate[:, bass.ds(t.i, 1)].rearrange("p a c n -> p (a c) n")
                        dve.wait_ge(s_sq, t.i + 1)
                        nc.vector.scalar_tensor_tensor(out=here, in0=sig[:, v], scalar=MOST, in1=gate_q[:, v],
                                                       op0=ALU.subtract, op1=ALU.mult).then_inc(s_g, 1)
                        dve.wait_ge(s_g, t.i + 1)
                        nc.vector.tensor_reduce(tops[:, bass.ds(t.i, 1)], here, AX.XY, ALU.max,
                                                apply_absolute_value=True).then_inc(s_top, 1)

                turns(dve, turn, -1, 1, GROUPS - 1, GROUPS)

            global_scale(nc, m, block, tops[:], GROUPS, s_top, P, a_scale, a_inv, "a")

        with ExitStack() as ctx:
            m = Names(nc, ctx, "ffo")
            up = m.sb("up", [P, 2, IC, N])
            gr = m.sb("gr", [P, 2, IC, N])
            tops = m.sb("tops", [P, GROUPS])
            consts = m.sb("consts", [P, 2])
            s_const, s_ur, s_gr, s_uq, s_gq, s_o, s_top = (m.sem(n) for n in (
                "constants", "up_rounded", "gate_rounded", "up_quantised", "gate_quantised", "multiplied", "maxima"))
            s_up = [m.sem(f"up{v}_loaded") for v in range(2)]
            block = ctx.enter_context(nc.Block())

            @block.sync
            def _(sp):
                def turn(t):
                    if not isinstance(t.i, int) or t.i > 1:
                        sp.wait_ge(s_o, t.i - 1)
                    sp.dma_start(up[:, t.parity], up_rows[bass.ds(t.i, 1)].rearrange("g p c n -> p (g c) n")).then_inc(s_up[t.parity], 16)

                turns(sp, turn, 0, 2, GROUPS, GROUPS)

            @block.scalar
            def _(act):
                act.wait_ge(s_const, 2)

                def turn(t):
                    v = t.parity
                    act.wait_ge(s_up[v], 16 * t.half + 16)
                    nc.scalar.activation(up[:, v], up[:, v], ACT.Identity, bias=consts[:, 0:1], scale=u_inv).then_inc(s_ur, 1)
                    if not isinstance(t.i, int) or t.i > 1:
                        act.wait_ge(s_o, t.i - 1)
                    nc.scalar.activation(gr[:, v], gate[:, bass.ds(t.i, 1)].rearrange("p a c n -> p (a c) n"),
                                         ACT.Identity, bias=consts[:, 0:1], scale=a_inv).then_inc(s_gr, 1)
                    act.wait_ge(s_gr, t.i + 1)
                    nc.scalar.activation(gr[:, v], gr[:, v], ACT.Identity, bias=consts[:, 1:2]).then_inc(s_gq, 1)

                turns(act, turn, 0, 2, GROUPS, GROUPS)

            @block.vector
            def _(dve):
                nc.vector.memset(consts[:, 0:1], ROUND).then_inc(s_const, 1)
                nc.vector.memset(consts[:, 1:2], -ROUND).then_inc(s_const, 1)

                def turn(t):
                    v = t.parity
                    here = gate[:, bass.ds(t.i, 1)].rearrange("p a c n -> p (a c) n")
                    dve.wait_ge(s_ur, t.i + 1)
                    nc.vector.tensor_scalar(up[:, v], up[:, v], ROUND, u_scale, ALU.subtract, ALU.mult).then_inc(s_uq, 1)
                    dve.wait_ge(s_gq, t.i + 1)
                    dve.wait_ge(s_uq, t.i + 1)
                    nc.vector.scalar_tensor_tensor(out=here, in0=gr[:, v], scalar=a_scale, in1=up[:, v],
                                                   op0=ALU.mult, op1=ALU.mult).then_inc(s_o, 1)
                    dve.wait_ge(s_o, t.i + 1)
                    nc.vector.tensor_reduce(tops[:, bass.ds(t.i, 1)], here, AX.XY, ALU.max,
                                            apply_absolute_value=True).then_inc(s_top, 1)

                turns(dve, turn, 0, 0, GROUPS, GROUPS)

            global_scale(nc, m, block, tops[:], GROUPS, s_top, P, o_scale, o_inv, "o")

        with ExitStack() as ctx:
            m = Names(nc, ctx, "ffd")
            orr = m.sb("rounded", [P, 2, IC, N])
            oq = m.sb("oq", [P, 2, IC, N])
            round_c = m.sb("round_c", [P, 1])
            ps_y = m.ps("ps_y", [P, 4, 512])
            s_const, s_r, s_q, s_y, s_sum, s_stats = (m.sem(n) for n in (
                "constants", "rounded", "quantised", "summed", "rows_added", "stats_ready"))
            block = ctx.enter_context(nc.Block())

            @block.scalar
            def _(act):
                act.wait_ge(s_const, 1)

                def turn(t):
                    if not isinstance(t.i, int) or t.i > 1:
                        act.wait_ge(s_q, t.i - 1)
                    nc.scalar.activation(orr[:, t.parity], gate[:, bass.ds(t.i, 1)].rearrange("p a c n -> p (a c) n"),
                                         ACT.Identity, bias=round_c[:], scale=o_inv).then_inc(s_r, 1)

                turns(act, turn, 0, 2, GROUPS, GROUPS)

            @block.vector
            def _(dve):
                nc.vector.memset(round_c[:], ROUND).then_inc(s_const, 1)

                def quantise(t):
                    dve.wait_ge(s_r, t.i + 1)
                    if not isinstance(t.i, int) or t.i > 1:
                        dve.wait_ge(s_y, G * (t.i - 1))
                    nc.vector.tensor_scalar(oq[:, t.parity], orr[:, t.parity], ROUND, o_scale,
                                            ALU.subtract, ALU.mult).then_inc(s_q, 1)

                def turn(t):
                    if (t + 1).within(GROUPS):
                        quantise(t + 1)
                    if t.within(GROUPS):
                        for q in range(G):
                            b = t.i * G + q
                            dve.wait_ge(s_y, b + 1)
                            nc.vector.tensor_tensor(at(y_nat, b), at(y_nat, b), ps_y[0:S, q, 0:D], ALU.subtract).then_inc(s_sum, 1)
                            dve.wait_ge(s_sum, b + 1)
                            nc.vector.bn_stats(at(keep["stats"], b), at(y_nat, b)).then_inc(s_stats, 1)

                turns(dve, turn, -1, 1, GROUPS - 1, GROUPS)

            @block.tensor
            def _(pe):
                def turn(t):
                    pe.wait_ge(s_q, t.i + 1)
                    for q in range(G):
                        if not isinstance(t.i, int) or t.i > 0:
                            pe.wait_ge(s_sum, (t.i - 1) * G + (q + 1))
                        for c in range(IC):
                            last = nc.tensor.matmul(ps_y[0:S, q, 0:D], oq[:, t.parity, c, q * S:(q + 1) * S], w_dT[:, c, :],
                                                    start=(c == 0), stop=(c == IC - 1))
                        last.then_inc(s_y, 1)

                turns(pe, turn, 0, 2, GROUPS, GROUPS)

            finish_norm(nc, m, block, keep, s_stats)


def bass_decoder(nc, io, out):
    B, S, D = io["x"].shape
    with ExitStack() as ctx:
        def kept(name, shape):
            return ctx.enter_context(nc.sbuf_tensor(name, shape, F32))

        keep = {
            "y": kept("y", [S, B, D]),
            "stats": kept("stats", [S, B, 6]),
            "mean": kept("mean", [S, B]),
            "rstd": kept("rstd", [S, B]),
        }
        linear_attention(nc, io, keep)
        mutual_attention(nc, io, keep)
        routed_ffn(nc, io, keep)
        causal_heads(nc, io, keep)
        relative_cross(nc, io, keep)
        quantised_ffn(nc, io, keep)
        store(nc, keep, out)


def store(nc, keep, out):
    S, B, D = keep["y"].shape
    with ExitStack() as ctx:
        m = Names(nc, ctx, "out")
        s_norm, s_out = m.sem("rows_normalised"), m.sem("stored")
        block = ctx.enter_context(nc.Block())
        part = 8

        @block.vector
        def _(dve):
            with dve.Fori(0, B) as b:
                nc.vector.tensor_scalar(at(keep["y"], b), at(keep["y"], b), keep["mean"][:, bass.ds(b, 1)],
                                        keep["rstd"][:, bass.ds(b, 1)], ALU.subtract, ALU.mult).then_inc(s_norm, 1)

        @block.sync
        def _(sp):
            for b in range(0, B, part):
                sp.wait_ge(s_norm, b + part)
                sp.dma_start(out[b:b + part].rearrange("b s d -> s b d"), keep["y"][:, b:b + part, :]).then_inc(s_out, 16)
            sp.wait_ge(s_out, 16 * (B // part))


_TRANSPOSED = {"L0_attn_WvT": "L0_attn_Wv", "L0_xattn_WvT_s": "L0_xattn_Wv_s", "L0_xattn_WvT_c": "L0_xattn_Wv_c",
               "L0_xattn_WgT": "L0_xattn_Wg", "L1_xattn_rel_k_tableT": "L1_xattn_rel_k_table"}
_COLUMNS = ["L0_attn_bq", "L0_attn_bk", "L0_attn_bv"] + [
    "L0_xattn_" + n for n in ("bq_c", "bk_s", "bk_c", "bq_s", "bv_s", "bv_c", "bg")] + [
    "L1_xattn_bq", "L1_xattn_bk"]


def _interpolation(n_in, n_out, chunks):
    import numpy as _np

    pos = (_np.arange(n_out, dtype=_np.float32) + _np.float32(0.5)) * _np.float32(n_in / n_out) - _np.float32(0.5)
    pos = _np.clip(pos, _np.float32(0.0), _np.float32(n_in - 1))
    low = _np.floor(pos).astype(_np.int32)
    high = _np.minimum(low + 1, n_in - 1)
    part = pos - low.astype(_np.float32)
    whole = _np.zeros((n_in, n_out), _np.float32)
    _np.add.at(whole, (low, _np.arange(n_out)), 1 - part)
    _np.add.at(whole, (high, _np.arange(n_out)), part)
    step = n_in // chunks
    rows = n_in - (chunks - 1) * step
    out = _np.zeros((rows, chunks, n_out), _np.float32)
    for c in range(chunks):
        r = rows if c == chunks - 1 else step
        out[:r, c] = whole[c * step:c * step + r]
    return out


def kernel(**inputs):
    import numpy as _np
    import concourse.bacc as _bacc
    from concourse import mybir as _mybir
    from concourse.bass_utils import run_bass_kernel_spmd as _run

    nc = _bacc.Bacc("TRN2", target_bir_lowering=False, num_devices=1)
    a = {n: _np.asarray(v) for n, v in inputs.items()}
    a["xT"] = a["x"].reshape(-1, a["x"].shape[-1]).T
    b1 = a["L0_ffn_b1"]
    a["L0_ffn_b1_cols"] = b1.reshape(b1.shape[0], -1, P).transpose(2, 0, 1)
    a["ctxT"] = a["ctx_1024"].transpose(0, 2, 1)
    a["interp"] = _interpolation(a["ctx_1024"].shape[1], a["x"].shape[1], 3)
    for new, old in _TRANSPOSED.items():
        a[new] = a[old].T
    for name in _COLUMNS:
        a[name + "_cols"] = a[name].reshape(-1, P).T
    arrays, io = {}, {}
    for n, v in a.items():
        v = _np.ascontiguousarray(v)
        arrays[f"in_{n}"] = v
        io[n] = nc.dram_tensor(f"in_{n}", v.shape, _mybir.dt.from_np(v.dtype), kind="ExternalInput").ap()
    out = nc.dram_tensor("out_0", a["x"].shape, _mybir.dt.float32, kind="ExternalOutput").ap()
    bass_decoder(nc, io, out)
    r = _run(nc, [arrays], core_ids=[0])
    return r.results[0]["out_0"]
```
